# Optimizing a Trainium2 kernel written in Bass

```python
import numpy as np
import jax
import jax.numpy as jnp

def _softmax(x, axis=-1):
    return jax.nn.softmax(x, axis=axis)

def _gelu(x):
    return jax.nn.gelu(x, approximate=True)

def _silu(x):
    return jax.nn.silu(x)

def _sigmoid(x):
    return jax.nn.sigmoid(x)

def _layernorm(x, axis=-1, eps=1e-05):
    m = jnp.mean(x, axis=axis, keepdims=True)
    v = jnp.var(x, axis=axis, keepdims=True)
    return (x - m) / jnp.sqrt(v + eps)

def _scatter_add(tgt, idx, src, axis=0):
    return tgt.at[idx].add(src)

def _segment_sum(src, seg, n):
    return jax.ops.segment_sum(src, seg, n)
kernel_name = 'mk_gnn_resnorm_d4_gnn_r16_fadf27'

def setup_inputs(seed: int=0):
    np.random.seed(seed)
    _w = jnp.asarray

    def _rec_inputs():
        import jax
        import jax.numpy as jnp
        _gk = jax.random.key(seed)
        x = -8.776e-05 + 1 * jax.random.normal(jax.random.fold_in(_gk, 1), (6250, 128), jnp.float32)
        _s = jax.random.randint(jax.random.fold_in(_gk, 2), (50000,), 0, 6250, jnp.int32)
        _d = jax.random.randint(jax.random.fold_in(_gk, 3), (50000,), 0, 6250, jnp.int32)
        _loop = jnp.arange(6250, dtype=jnp.int32)
        src = jnp.concatenate([_s, _d, _loop])
        dst = jnp.concatenate([_d, _s, _loop])
        _o = jnp.argsort(dst, stable=True)
        src = src[_o]
        dst = dst[_o]
        edge_attr_16 = 0.000254156 + 0.999948 * jax.random.normal(jax.random.fold_in(_gk, 12), (106250, 16), jnp.float32)
        edge_attr_3 = 0.000844983 + 0.999762 * jax.random.normal(jax.random.fold_in(_gk, 13), (106250, 3), jnp.float32)
        edge_weight = jax.random.uniform(jax.random.fold_in(_gk, 15), (106250,), jnp.float32, 0.0, 0.999999)
        edge_weight1 = jax.random.uniform(jax.random.fold_in(_gk, 16), (106250, 1), jnp.float32, 0.0, 5.99999)
        return (x, src, dst, edge_attr_16, edge_attr_3, edge_weight, edge_weight1)
    x, src, dst, edge_attr_16, edge_attr_3, edge_weight, edge_weight1 = _rec_inputs()

    def _L0_gnn_setup():
        import jax, jax.numpy as jnp
        import numpy as np
        import math
        N = 2500
        E = 40000
        HID = 128
        H = 8
        HD = HID // H
        CUTOFF = 5.0
        LN_EPS = 1e-05

        def _linear_params(key, out_d, in_d):
            k1, k2 = jax.random.split(key)
            s = 1.0 / np.sqrt(in_d)
            W = jax.random.uniform(k1, (out_d, in_d), minval=-s, maxval=s, dtype=jnp.float32)
            b = jax.random.uniform(k2, (out_d,), minval=-s, maxval=s, dtype=jnp.float32)
            return (W, b)
        key = jax.random.key(seed)
        ks = jax.random.split(key, 12)
        x = jax.random.normal(ks[0], (N, HID), dtype=jnp.float32)
        edge_index = jax.random.randint(ks[1], (2, E), 0, N, dtype=jnp.int64)
        edge_vec = jax.random.normal(ks[2], (E, 3), dtype=jnp.float32)
        edge_length = jax.random.uniform(ks[3], (E, 1), dtype=jnp.float32) * 6.0
        Wq, bq = _linear_params(ks[4], HID, HID)
        Wk, bk = _linear_params(ks[5], HID, HID)
        Wv, bv = _linear_params(ks[6], HID, HID)
        We1, be1 = _linear_params(ks[7], HID, 1)
        We2, be2 = _linear_params(ks[8], H, HID)
        Wo, bo = _linear_params(ks[9], HID, HID)
        ln_g = jnp.ones((HID,), jnp.float32)
        ln_b = jnp.zeros((HID,), jnp.float32)
        return {'x': x, 'edge_vec': edge_vec, 'edge_length': edge_length, 'Wq': Wq, 'bq': bq, 'Wk': Wk, 'bk': bk, 'Wv': Wv, 'bv': bv, 'We1': We1, 'be1': be1, 'We2': We2, 'be2': be2, 'Wo': Wo, 'bo': bo, 'ln_g': ln_g, 'ln_b': ln_b, 'edge_index': edge_index}
    _L0_gnn_all = _L0_gnn_setup()
    _L0_gnn_in = {k: v for k, v in _L0_gnn_all.items() if k in ('Wq', 'bq', 'Wk', 'bk', 'Wv', 'bv', 'We1', 'be1', 'We2', 'be2', 'Wo', 'bo', 'ln_g', 'ln_b')}
    del _L0_gnn_all

    def _L1_gnn_setup():
        import jax, jax.numpy as jnp
        import numpy as np
        N_NODES = 6250
        N_EDGES = 100000
        IN_DIM = 128
        HEADS = 4
        OUT_C = 32
        NEG_SLOPE = 0.2
        key = jax.random.key(seed)
        ks = jax.random.split(key, 8)
        x = jax.random.normal(ks[0], (N_NODES, IN_DIM), dtype=jnp.float32)
        s = float(np.sqrt(2.0 / (IN_DIM + HEADS * OUT_C)))
        W_l = jax.random.normal(ks[1], (IN_DIM, HEADS * OUT_C), dtype=jnp.float32) * s
        b_l = jnp.zeros((HEADS * OUT_C,), dtype=jnp.float32)
        W_r = jax.random.normal(ks[2], (IN_DIM, HEADS * OUT_C), dtype=jnp.float32) * s
        b_r = jnp.zeros((HEADS * OUT_C,), dtype=jnp.float32)
        att = jax.random.normal(ks[3], (HEADS, OUT_C), dtype=jnp.float32) * float(np.sqrt(2.0 / (HEADS + OUT_C)))
        bias = jnp.zeros((HEADS * OUT_C,), dtype=jnp.float32)
        src = jax.random.randint(ks[4], (N_EDGES,), 0, N_NODES, dtype=jnp.int64)
        dst = jax.random.randint(ks[5], (N_EDGES,), 0, N_NODES, dtype=jnp.int64)
        dst = jnp.where(dst == src, (dst + 1) % N_NODES, dst)
        return {'x': x, 'W_l': W_l, 'b_l': b_l, 'W_r': W_r, 'b_r': b_r, 'att': att, 'bias': bias, 'src': src, 'dst': dst}
    _L1_gnn_all = _L1_gnn_setup()
    _L1_gnn_in = {k: v for k, v in _L1_gnn_all.items() if k in ('W_l', 'b_l', 'W_r', 'b_r', 'att', 'bias')}
    del _L1_gnn_all

    def _L2_gnn_setup():
        import jax, jax.numpy as jnp
        import numpy as np
        N_NODES = 3125
        N_EDGES = 50000
        IN_C = 128
        OUT_C = 128
        EDGE_F = 16
        NEG_SLOPE = 0.2
        BN_EPS = 1e-05
        key = jax.random.key(seed)
        ks = jax.random.split(key, 8)
        x = jax.random.normal(ks[0], (N_NODES, IN_C), dtype=jnp.float32)
        edge_index = jax.random.randint(ks[1], (2, N_EDGES), 0, N_NODES, dtype=jnp.int64)
        edge_attr = jax.random.normal(ks[2], (N_EDGES, EDGE_F), dtype=jnp.float32)
        W = jax.random.normal(ks[3], (IN_C, OUT_C), dtype=jnp.float32) / np.sqrt(IN_C)
        att_src = jax.random.normal(ks[4], (OUT_C,), dtype=jnp.float32) / np.sqrt(OUT_C)
        att_dst = jax.random.normal(ks[5], (OUT_C,), dtype=jnp.float32) / np.sqrt(OUT_C)
        bias = jnp.zeros((OUT_C,), dtype=jnp.float32)
        gamma = jnp.ones((OUT_C,), dtype=jnp.float32)
        beta = jnp.zeros((OUT_C,), dtype=jnp.float32)
        return {'x': x, 'edge_index': edge_index, 'edge_attr': edge_attr, 'W': W, 'att_src': att_src, 'att_dst': att_dst, 'bias': bias, 'gamma': gamma, 'beta': beta}
    _L2_gnn_all = _L2_gnn_setup()
    _L2_gnn_in = {k: v for k, v in _L2_gnn_all.items() if k in ('W', 'att_src', 'att_dst', 'bias', 'gamma', 'beta')}
    del _L2_gnn_all

    def _L3_gnn_setup():
        import jax, jax.numpy as jnp
        import numpy as np
        N, E, D = (6250, 100000, 128)

        def _graph_conv(h, src, dst, Wr, br, Ws, ew=None):
            m = h[src]
            if ew is not None:
                m = m * ew[:, None]
            agg = jax.ops.segment_sum(m, dst, num_segments=h.shape[0])
            return agg @ Wr + br + h @ Ws
        key = jax.random.key(seed)
        ks = jax.random.split(key, 10)
        x = jax.random.normal(ks[0], (N, D), dtype=jnp.float32)
        edge_index = jax.random.randint(ks[1], (2, E), 0, N, dtype=jnp.int64)
        edge_weight = jax.random.uniform(ks[2], (E,), dtype=jnp.float32)
        s = 1.0 / np.sqrt(D)
        Wr0 = jax.random.uniform(ks[3], (D, D), jnp.float32, -s, s)
        br0 = jax.random.uniform(ks[4], (D,), jnp.float32, -s, s)
        Ws0 = jax.random.uniform(ks[5], (D, D), jnp.float32, -s, s)
        Wr1 = jax.random.uniform(ks[6], (D, D), jnp.float32, -s, s)
        br1 = jax.random.uniform(ks[7], (D,), jnp.float32, -s, s)
        Ws1 = jax.random.uniform(ks[8], (D, D), jnp.float32, -s, s)
        return {'x': x, 'edge_index': edge_index, 'edge_weight': edge_weight, 'Wr0': Wr0, 'br0': br0, 'Ws0': Ws0, 'Wr1': Wr1, 'br1': br1, 'Ws1': Ws1}
    _L3_gnn_all = _L3_gnn_setup()
    _L3_gnn_in = {k: v for k, v in _L3_gnn_all.items() if k in ('Wr0', 'br0', 'Ws0', 'Wr1', 'br1', 'Ws1')}
    del _L3_gnn_all
    return {'x': x, 'src': src, 'dst': dst, 'edge_attr_16': edge_attr_16, 'edge_attr_3': edge_attr_3, 'edge_weight': edge_weight, 'edge_weight1': edge_weight1, 'L0_gnn_Wq': _L0_gnn_in['Wq'], 'L0_gnn_bq': _L0_gnn_in['bq'], 'L0_gnn_Wk': _L0_gnn_in['Wk'], 'L0_gnn_bk': _L0_gnn_in['bk'], 'L0_gnn_Wv': _L0_gnn_in['Wv'], 'L0_gnn_bv': _L0_gnn_in['bv'], 'L0_gnn_We1': _L0_gnn_in['We1'], 'L0_gnn_be1': _L0_gnn_in['be1'], 'L0_gnn_We2': _L0_gnn_in['We2'], 'L0_gnn_be2': _L0_gnn_in['be2'], 'L0_gnn_Wo': _L0_gnn_in['Wo'], 'L0_gnn_bo': _L0_gnn_in['bo'], 'L0_gnn_ln_g': _L0_gnn_in['ln_g'], 'L0_gnn_ln_b': _L0_gnn_in['ln_b'], 'L1_gnn_W_l': _L1_gnn_in['W_l'], 'L1_gnn_b_l': _L1_gnn_in['b_l'], 'L1_gnn_W_r': _L1_gnn_in['W_r'], 'L1_gnn_b_r': _L1_gnn_in['b_r'], 'L1_gnn_att': _L1_gnn_in['att'], 'L1_gnn_bias': _L1_gnn_in['bias'], 'L2_gnn_W': _L2_gnn_in['W'], 'L2_gnn_att_src': _L2_gnn_in['att_src'], 'L2_gnn_att_dst': _L2_gnn_in['att_dst'], 'L2_gnn_bias': _L2_gnn_in['bias'], 'L2_gnn_gamma': _L2_gnn_in['gamma'], 'L2_gnn_beta': _L2_gnn_in['beta'], 'L3_gnn_Wr0': _L3_gnn_in['Wr0'], 'L3_gnn_br0': _L3_gnn_in['br0'], 'L3_gnn_Ws0': _L3_gnn_in['Ws0'], 'L3_gnn_Wr1': _L3_gnn_in['Wr1'], 'L3_gnn_br1': _L3_gnn_in['br1'], 'L3_gnn_Ws1': _L3_gnn_in['Ws1']}

def reference(x, src, dst, edge_attr_16, edge_attr_3, edge_weight, edge_weight1, L0_gnn_Wq, L0_gnn_bq, L0_gnn_Wk, L0_gnn_bk, L0_gnn_Wv, L0_gnn_bv, L0_gnn_We1, L0_gnn_be1, L0_gnn_We2, L0_gnn_be2, L0_gnn_Wo, L0_gnn_bo, L0_gnn_ln_g, L0_gnn_ln_b, L1_gnn_W_l, L1_gnn_b_l, L1_gnn_W_r, L1_gnn_b_r, L1_gnn_att, L1_gnn_bias, L2_gnn_W, L2_gnn_att_src, L2_gnn_att_dst, L2_gnn_bias, L2_gnn_gamma, L2_gnn_beta, L3_gnn_Wr0, L3_gnn_br0, L3_gnn_Ws0, L3_gnn_Wr1, L3_gnn_br1, L3_gnn_Ws1):
    import jax
    import jax.numpy as jnp

    def _L0_gnn_ref(x, edge_vec, edge_length, Wq, bq, Wk, bk, Wv, bv, We1, be1, We2, be2, Wo, bo, ln_g, ln_b, edge_index):
        import jax, jax.numpy as jnp
        import numpy as np
        import math
        N = 2500
        E = 40000
        HID = 128
        H = 8
        HD = HID // H
        CUTOFF = 5.0
        LN_EPS = 1e-05

        def _linear_params(key, out_d, in_d):
            k1, k2 = jax.random.split(key)
            s = 1.0 / np.sqrt(in_d)
            W = jax.random.uniform(k1, (out_d, in_d), minval=-s, maxval=s, dtype=jnp.float32)
            b = jax.random.uniform(k2, (out_d,), minval=-s, maxval=s, dtype=jnp.float32)
            return (W, b)
        row, col = (edge_index[0], edge_index[1])
        n = x.shape[0]
        q = (x @ Wq.T + bq).reshape(n, H, HD)
        k = (x @ Wk.T + bk).reshape(n, H, HD)
        v = (x @ Wv.T + bv).reshape(n, H, HD)
        attn = jnp.einsum('ehd,ehd->eh', q[row], k[col]) / math.sqrt(HD)
        edge_bias = jax.nn.silu(edge_length @ We1.T + be1) @ We2.T + be2
        attn = attn + edge_bias
        cut = 0.5 * (jnp.cos(edge_length * math.pi / CUTOFF) + 1.0)
        cut = cut * (edge_length < CUTOFF).astype(jnp.float32)
        attn = attn * cut
        attn_exp = jnp.exp(attn - jnp.max(attn, axis=0, keepdims=True))
        attn_sum = jax.ops.segment_sum(attn_exp, row, num_segments=n)
        attn = attn_exp / (attn_sum[row] + 1e-08)
        out = jax.ops.segment_sum(attn[:, :, None] * v[col], row, num_segments=n)
        out = out.reshape(n, HID) @ Wo.T + bo
        h = x + out
        mu = jnp.mean(h, axis=-1, keepdims=True)
        var = jnp.mean(jnp.square(h - mu), axis=-1, keepdims=True)
        return (h - mu) / jnp.sqrt(var + LN_EPS) * ln_g + ln_b

    def _L1_gnn_ref(x, W_l, b_l, W_r, b_r, att, bias, src, dst):
        import jax, jax.numpy as jnp
        import numpy as np
        N_NODES = 6250
        N_EDGES = 100000
        IN_DIM = 128
        HEADS = 4
        OUT_C = 32
        NEG_SLOPE = 0.2
        N = x.shape[0]
        H, C = att.shape
        x_l = (x @ W_l + b_l).reshape(N, H, C)
        x_r = (x @ W_r + b_r).reshape(N, H, C)
        loop = jnp.arange(N, dtype=src.dtype)
        s = jnp.concatenate([src, loop])
        d = jnp.concatenate([dst, loop])
        m = x_l[s] + x_r[d]
        m = jnp.where(m >= 0, m, NEG_SLOPE * m)
        e = jnp.einsum('ehc,hc->eh', m, att)
        seg_max = jax.ops.segment_max(e, d, num_segments=N)
        e = jnp.exp(e - seg_max[d])
        denom = jax.ops.segment_sum(e, d, num_segments=N)
        alpha = e / denom[d]
        out = jax.ops.segment_sum(alpha[:, :, None] * x_l[s], d, num_segments=N)
        return out.reshape(N, H * C) + bias

    def _L2_gnn_ref(x, edge_index, edge_attr, W, att_src, att_dst, bias, gamma, beta):
        import jax, jax.numpy as jnp
        import numpy as np
        N_NODES = 3125
        N_EDGES = 50000
        IN_C = 128
        OUT_C = 128
        EDGE_F = 16
        NEG_SLOPE = 0.2
        BN_EPS = 1e-05
        N = x.shape[0]
        h = x @ W
        loops = jnp.broadcast_to(jnp.arange(N, dtype=edge_index.dtype)[None, :], (2, N))
        ei = jnp.concatenate([edge_index, loops], axis=1)
        src, dst = (ei[0], ei[1])
        a_src = h @ att_src
        a_dst = h @ att_dst
        e = jax.nn.leaky_relu(a_src[src] + a_dst[dst], NEG_SLOPE)
        m = jax.ops.segment_max(e, dst, num_segments=N)
        ex = jnp.exp(e - m[dst])
        denom = jax.ops.segment_sum(ex, dst, num_segments=N)
        alpha = ex / denom[dst]
        out = jax.ops.segment_sum(alpha[:, None] * h[src], dst, num_segments=N) + bias
        mean = jnp.mean(out, axis=0)
        var = jnp.mean((out - mean) ** 2, axis=0)
        y = (out - mean) * jax.lax.rsqrt(var + BN_EPS) * gamma + beta
        return jax.nn.relu(y)

    def _L3_gnn_ref(x, edge_index, edge_weight, Wr0, br0, Ws0, Wr1, br1, Ws1):
        import jax, jax.numpy as jnp
        import numpy as np
        N, E, D = (6250, 100000, 128)

        def _graph_conv(h, src, dst, Wr, br, Ws, ew=None):
            m = h[src]
            if ew is not None:
                m = m * ew[:, None]
            agg = jax.ops.segment_sum(m, dst, num_segments=h.shape[0])
            return agg @ Wr + br + h @ Ws
        src, dst = (edge_index[0], edge_index[1])
        h = jax.nn.relu(_graph_conv(x, src, dst, Wr0, br0, Ws0, edge_weight))
        h = jax.nn.relu(_graph_conv(h, src, dst, Wr1, br1, Ws1))
        return h
    edge_index = jnp.stack([src, dst])
    x = _layernorm(x + _L0_gnn_ref(x, edge_attr_3, edge_weight1, L0_gnn_Wq, L0_gnn_bq, L0_gnn_Wk, L0_gnn_bk, L0_gnn_Wv, L0_gnn_bv, L0_gnn_We1, L0_gnn_be1, L0_gnn_We2, L0_gnn_be2, L0_gnn_Wo, L0_gnn_bo, L0_gnn_ln_g, L0_gnn_ln_b, edge_index), axis=-1)
    x = _layernorm(x + _L1_gnn_ref(x, L1_gnn_W_l, L1_gnn_b_l, L1_gnn_W_r, L1_gnn_b_r, L1_gnn_att, L1_gnn_bias, src, dst), axis=-1)
    x = _layernorm(x + _L2_gnn_ref(x, edge_index, edge_attr_16, L2_gnn_W, L2_gnn_att_src, L2_gnn_att_dst, L2_gnn_bias, L2_gnn_gamma, L2_gnn_beta), axis=-1)
    x = _layernorm(x + _L3_gnn_ref(x, edge_index, edge_weight, L3_gnn_Wr0, L3_gnn_br0, L3_gnn_Ws0, L3_gnn_Wr1, L3_gnn_br1, L3_gnn_Ws1), axis=-1)
    return x

_drawn_inputs = setup_inputs


def setup_inputs(seed=0):
    import zlib

    import numpy as np

    out = dict(_drawn_inputs(seed))
    spreads = {'L0_gnn_ln_g': (1.0, 0.2),
     'L0_gnn_ln_b': (0.0, 0.1),
     'L1_gnn_b_l': (0.0, 0.1),
     'L1_gnn_b_r': (0.0, 0.391),
     'L1_gnn_bias': (0.0, 0.1),
     'L2_gnn_bias': (0.0, 2.0),
     'L2_gnn_gamma': (1.0, 0.2),
     'L2_gnn_beta': (0.0, 0.1)}
    factors = {'edge_weight1': 200.0,
     'L0_gnn_Wq': 193.854,
     'L0_gnn_bq': 200.0,
     'L0_gnn_Wk': 200.0,
     'L0_gnn_bk': 200.0,
     'L0_gnn_We1': 200.0,
     'L0_gnn_be1': 200.0,
     'L0_gnn_We2': 200.0,
     'L0_gnn_be2': 64.0,
     'L3_gnn_br1': 7.166,
     'L0_gnn_Wv': 32.927,
     'L0_gnn_bv': 64.0,
     'L0_gnn_Wo': 26.051}
    for name, (base, spread) in spreads.items():
        noise = np.random.default_rng([zlib.crc32(name.encode()), seed]).standard_normal(out[name].shape)
        drawn = base * np.exp(spread * noise) if base else spread * noise
        out[name] = jnp.asarray(drawn.astype(out[name].dtype))
    for name, factor in factors.items():
        out[name] = (out[name] * factor).astype(out[name].dtype)
    return out
```

```python
from contextlib import ExitStack, contextmanager

import concourse.bass as bass
from concourse import mybir

P = 128
N = 6250
E = 106250
D = 128
NB = 50
NP = NB * P
G = 7
R = 126
W = G * P
T = R * G
EP = T * P
SLOTS = 3
assert EP >= E + N and NP >= N + P and R % SLOTS == 0 and R % 2 == 0
H0, H1 = 8, 4
HB = 50
BIG = 1e30
LN_EPS = 1e-5
CUTOFF = 5.0

ALU = mybir.AluOpType
ACT = mybir.ActivationFunctionType
AX = mybir.AxisListType
F32 = mybir.dt.float32
BF16 = mybir.dt.bfloat16
I32 = mybir.dt.int32
U32 = mybir.dt.uint32


class Stage:

    def __init__(self, nc, name, stack):
        self.nc, self.name, self.stack, self.sems = nc, name, stack, []

    def sem(self, name):
        s = self.nc.alloc_semaphore(f"{self.name}_{name}")
        self.sems.append(s)
        return s

    def sb(self, name, shape, dt=F32):
        return self.stack.enter_context(self.nc.sbuf_tensor(f"{self.name}_{name}", shape, dt))

    def ps(self, name, shape, dt=F32):
        return self.stack.enter_context(self.nc.psum_tensor(f"{self.name}_ps_{name}", shape, dt))


@contextmanager
def stage(nc, name):
    with ExitStack() as stack:
        st = Stage(nc, name, stack)
        yield st
    nc.clear_and_free_semaphores(st.sems)
    nc.all_engine_barrier()


class Chain:

    def __init__(self, eng, sem):
        self.eng, self.sem, self.n = eng, sem, 0

    def __call__(self, ins):
        self.n += 1
        ins.then_inc(self.sem, 1)
        self.eng.wait_ge(self.sem, self.n)


def over_tiles(ap, inner):
    g = ap.shape[1]
    return ap.rearrange("p (g o) -> p g o", o=1).to_broadcast([ap.shape[0], g, inner])


def per_tile(ap, g=G):
    return ap.rearrange("p (o n) -> p o n", o=1).to_broadcast([ap.shape[0], g, ap.shape[1]])


def group(col, gi, width=1):
    return col[:, bass.ds(gi * (G * width), G * width)]


class Order:

    def __init__(self, nc, name, keep):
        self.name = name
        self.payload = nc.dram_tensor(f"payload_{name}", [EP, 4], F32).ap()
        self.base_dram = nc.dram_tensor(f"base_{name}", [1, R * 8], I32).ap()
        sb = lambda n, s, dt=F32: keep.enter_context(nc.sbuf_tensor(f"{name}_{n}", s, dt))
        self.other = sb("other", [P, T], I32)
        self.rel = sb("rel", [P, T])
        self.rel_bf = sb("rel_bf", [P, T], BF16)
        self.base = sb("base", [1, R * 8], I32)
        self.weight = sb("weight", [P, T])
        self.start = sb("start", [R, W])
        self.end = sb("end", [R, W])
        self.has_start = sb("has_start", [1, R])
        self.has_end = sb("has_end", [1, R])


def constants(nc, keep):
    class C:
        pass
    c = C()
    sb = lambda n, s, dt=F32: keep.enter_context(nc.sbuf_tensor(f"const_{n}", s, dt))
    c.ident, c.ident_bf = sb("ident", [P, P]), sb("ident_bf", [P, P], BF16)
    c.lane, c.column = sb("lane", [P, 1]), sb("column", [P, P])
    c.before, c.after = sb("before", [P, P]), sb("after", [P, P])
    c.ones = sb("ones", [P, P])
    with stage(nc, "constants") as st:
        made, ones_ready, ident_ready, bf_ready = (st.sem(n) for n in ("made", "ones", "ident", "bf"))
        with nc.Block() as block:
            @block.gpsimd
            def _(pool):
                pool.memset(c.ident[:], 0.0).then_inc(ident_ready, 1)
                pool.wait_ge(ident_ready, 1)
                pool.affine_select(out=c.ident[:], in_=c.ident[:], compare_op=ALU.not_equal, fill=1.0, base=0,
                                   pattern=[[-1, P]], channel_multiplier=1).then_inc(ident_ready, 1)
                pool.iota(c.lane[:], [[0, 1]], base=0, channel_multiplier=1,
                          allow_small_or_imprecise_dtypes=True).then_inc(made, 1)
                pool.iota(c.column[:], [[1, P]], base=0, channel_multiplier=0,
                          allow_small_or_imprecise_dtypes=True).then_inc(made, 1)
                pool.memset(c.ones[:], 1.0).then_inc(ones_ready, 1)
                pool.wait_ge(ones_ready, 1)
                pool.affine_select(out=c.before[:], in_=c.ones[:], compare_op=ALU.is_ge, fill=0.0, base=-1,
                                   pattern=[[-1, P]], channel_multiplier=1).then_inc(made, 1)
                pool.affine_select(out=c.after[:], in_=c.ones[:], compare_op=ALU.is_ge, fill=0.0, base=-1,
                                   pattern=[[1, P]], channel_multiplier=-1).then_inc(made, 1)
                pool.wait_ge(made, 4)

            @block.vector
            def _(dve):
                dve.wait_ge(ident_ready, 2)
                dve.tensor_copy(c.ident_bf[:], c.ident[:]).then_inc(bf_ready, 1)
                dve.wait_ge(bf_ready, 1)
    return c


def sort_edges(nc, c, o, key_d, other_d, weight_d, real_d):
    with stage(nc, f"load_{o.name}") as st:
        key, other = st.sb("key", [P, T], I32), st.sb("other", [P, T], I32)
        weight, real = st.sb("weight", [P, T]), st.sb("real", [P, T])
        bits = st.sb("bits", [P, T], I32)
        key_f, lo, hi = st.sb("key_f", [P, T]), st.sb("lo", [P, T]), st.sb("hi", [P, T])
        lo_bf, hi_bf = st.sb("lo_bf", [P, T], BF16), st.sb("hi_bf", [P, T], BF16)
        pay = st.sb("pay", [P, T, 4])
        counts, totals = st.sb("counts", [P, HB]), st.sb("totals", [P, HB])
        upto, first = st.sb("upto", [P, HB]), st.sb("first", [P, HB])
        one_lo, one_hi = st.sb("one_lo", [P, 2, G, P], BF16), st.sb("one_hi", [P, 2, G, HB], BF16)
        zero = st.sb("zero", [P, P], BF16)
        ps_counts, ps_sums = st.ps("counts", [P, 512]), st.ps("sums", [P, 512])
        loaded, steps, paid, split = (st.sem(n) for n in ("loaded", "steps", "paid", "split"))
        cleared, hot_ready, hot_used, counted, copied, summed = (
            st.sem(n) for n in ("cleared", "hot_ready", "hot_used", "counted", "copied", "summed"))

        with nc.Block() as block:
            @block.sync
            def _(sp):
                for buf, src in ((key, key_d), (other, other_d), (weight, weight_d), (real, real_d)):
                    sp.dma_start(buf[:], src).then_inc(loaded, 16)
                sp.wait_ge(loaded, 64)

            @block.scalar
            def _(act):
                act.wait_ge(loaded, 64)
                for f, buf in enumerate((key, other, weight, real)):
                    act.copy(pay[:, :, f], buf[:]).then_inc(paid, 1)
                act.wait_ge(paid, 4)
                act.wait_ge(counted, 1)
                act.copy(counts[:], ps_counts[:, 0:HB]).then_inc(copied, 1)
                act.wait_ge(copied, 1)

            @block.vector
            def _(dve):
                link = Chain(dve, steps)
                dve.memset(zero[:], 0.0).then_inc(cleared, 1)
                dve.wait_ge(loaded, 64)
                link(dve.tensor_copy(key_f[:], key[:]))
                link(dve.tensor_single_scalar(bits[:], key[:], P - 1, ALU.bitwise_and))
                link(dve.tensor_copy(lo[:], bits[:]))
                link(dve.tensor_copy(lo_bf[:], bits[:]))
                link(dve.tensor_single_scalar(bits[:], key[:], 7, ALU.arith_shift_right))
                link(dve.tensor_copy(hi[:], bits[:]))
                link(dve.tensor_scalar(hi_bf[:], hi[:], float(P), None, ALU.mult))
                dve.sem_inc(hot_used, 2)
                with dve.Fori(0, R // 2) as i:
                    for s in range(2):
                        gi = 2 * i + s
                        dve.wait_ge(hot_used, gi + 1)
                        dve.tensor_tensor(one_lo[:, s], per_tile(c.column[:]), over_tiles(group(lo, gi), P),
                                          ALU.is_equal).then_inc(hot_ready, 1)
                        dve.tensor_tensor(one_hi[:, s], per_tile(c.column[:, 0:HB]), over_tiles(group(hi, gi), HB),
                                          ALU.is_equal).then_inc(hot_ready, 1)
                dve.wait_ge(hot_ready, 2 * R)
                dve.wait_ge(summed, 1)
                link(dve.tensor_copy(totals[:], ps_sums[:, 64:64 + HB]))
                link(dve.tensor_tensor_scan(upto[:], c.ones[:, 0:HB], totals[:], 0.0, ALU.mult, ALU.add))
                link(dve.tensor_tensor(upto[:], upto[:], totals[:], ALU.subtract))
                link(dve.tensor_tensor(first[:], upto[:], ps_sums[:, 0:HB], ALU.add))

            @block.tensor
            def _(pe):
                pe.wait_ge(cleared, 1)
                pe.matmul(ps_counts[:, 0:HB], zero[:], zero[:, 0:HB], start=True, stop=True, skip_group_check=True)
                with pe.Fori(0, R // 2) as i:
                    for s in range(2):
                        gi = 2 * i + s
                        pe.wait_ge(hot_ready, 2 * gi + 2)
                        for j in range(G):
                            mm = pe.matmul(ps_counts[:, 0:HB], one_lo[:, s, j, :], one_hi[:, s, j, :],
                                           start=False, stop=True, skip_group_check=True)
                        mm.then_inc(hot_used, 1)
                pe.matmul(ps_sums[:, 448:450], zero[:], zero[:, 0:2], start=True, stop=True).then_inc(counted, 1)
                pe.wait_ge(copied, 1)
                pe.matmul(ps_sums[:, 0:HB], c.after[:], counts[:], start=True, stop=True)
                pe.matmul(ps_sums[:, 64:64 + HB], c.ones[:], counts[:], start=True, stop=True).then_inc(summed, 1)

        one_lo_t = st.sb("one_lo_t", [P, G, P])
        same, rank, at = st.sb("same", [P, G, P]), st.sb("rank", [P, 2, G]), st.sb("at", [P, 2, G])
        picked = st.sb("picked", [P, G, HB])
        at_i = st.sb("at_i", [P, 2, G], I32)
        pay_slot = st.sb("pay_slot", [P, 2, G, 4])
        running = st.sb("running", [P, 2, HB])
        ps_lo, ps_key = st.ps("lo", [P, 8, P]), st.ps("key", [P, 8, P])
        ps_run, ps_look = st.ps("run", [P, 512]), st.ps("look", [P, G, 64])
        (spread, keys_read, lo_t_ready, ran, snapped, looked, picked_s, look_read, ranked, placed, staged, slot_free,
         pool_go, at_ready) = (
            st.sem(n) for n in ("spread", "keys_read", "lo_t", "ran", "snapped", "looked", "picked", "look_read",
                                "ranked", "placed", "staged", "slot_free", "pool_go", "at_ready"))
        hot2_ready = st.sem("hot2_ready")
        scattered = [st.sem(f"scattered{s}") for s in range(2)]

        with nc.Block() as block:
            @block.tensor
            def _(pe):
                pe.matmul(ps_run[:, 0:HB], c.ident[:], first[:], start=True, stop=True,
                          skip_group_check=True).then_inc(ran, 1)
                with pe.Fori(0, R // 2) as i:
                    for s in range(2):
                        gi = 2 * i + s
                        pe.wait_ge(keys_read, gi + 1)
                        for j in range(G):
                            col = bass.ds(gi * G + j, 1)
                            a = lo_bf[:, col].to_broadcast([P, P])
                            b = hi_bf[:, col].to_broadcast([P, P])
                            pe.matmul(ps_lo[:, j, :], a, c.ident_bf[:], start=True, stop=True)
                            pe.matmul(ps_key[:, j, :], a, c.ident_bf[:], start=True, stop=False)
                            mm = pe.matmul(ps_key[:, j, :], b, c.ident_bf[:], start=False, stop=True)
                        mm.then_inc(spread, 1)
                        pe.wait_ge(lo_t_ready, gi + 1)
                        pe.wait_ge(hot2_ready, 2 * gi + 2)
                        pe.wait_ge(look_read, gi + 1)
                        for j in range(G):
                            k = (s * G + j) % 2
                            pe.wait_ge(snapped, gi * G + (j + 1))
                            pe.matmul(ps_look[:, j, 0:HB], one_lo_t[:, j, :], running[:, k, :],
                                      start=True, stop=True).then_inc(looked, 1)
                            pe.matmul(ps_run[:, 0:HB], one_lo[:, s, j, :], one_hi[:, s, j, :], start=False, stop=True,
                                      skip_group_check=True).then_inc(ran, 1)

            @block.scalar
            def _(act):
                with act.Fori(0, R // 2) as i:
                    for s in range(2):
                        gi = 2 * i + s
                        act.wait_ge(slot_free, gi + 1)
                        act.copy(pay_slot[:, s].rearrange("p g f -> p (g f)"),
                                 group(pay[:].rearrange("p t f -> p (t f)"), gi, 4)).then_inc(staged, 1)
                        for j in range(G):
                            k = (s * G + j) % 2
                            act.wait_ge(ran, gi * G + (j + 1))
                            act.copy(running[:, k, :], ps_run[:, 0:HB]).then_inc(snapped, 1)

            @block.vector
            def _(dve):
                dve.sem_inc(keys_read, 1)
                dve.sem_inc(look_read, 1)
                with dve.Fori(0, R // 2) as i:
                    for s in range(2):
                        gi = 2 * i + s
                        dve.tensor_tensor(one_lo[:, s], per_tile(c.column[:]), over_tiles(group(lo, gi), P),
                                          ALU.is_equal).then_inc(hot2_ready, 1)
                        dve.tensor_tensor(one_hi[:, s], per_tile(c.column[:, 0:HB]), over_tiles(group(hi, gi), HB),
                                          ALU.is_equal).then_inc(hot2_ready, 1)
                        dve.wait_ge(spread, gi + 1)
                        dve.tensor_scalar(one_lo_t[:], ps_lo[:, 0:G, :], c.lane[:, 0:1], None,
                                          ALU.is_equal).then_inc(lo_t_ready, 1)
                        for j in range(G):
                            dve.scalar_tensor_tensor(same[:, j, :], ps_key[:, j, :], key_f[:, bass.ds(gi * G + j, 1)],
                                                     c.before[:], ALU.is_equal, ALU.mult,
                                                     accum_out=rank[:, s, j:j + 1]).then_inc(ranked, 1)
                        dve.wait_ge(ranked, gi * G + G)
                        dve.sem_inc(keys_read, 1)
                        dve.wait_ge(looked, gi * G + G)
                        dve.tensor_tensor(picked[:], one_hi[:, s], ps_look[:, :, 0:HB], ALU.mult).then_inc(look_read, 1)
                        dve.wait_ge(look_read, gi + 2)
                        dve.tensor_reduce(at[:, s], picked[:], AX.X, ALU.add).then_inc(picked_s, 1)
                        dve.wait_ge(picked_s, gi + 1)
                        dve.wait_ge(slot_free, gi + 1)
                        dve.tensor_tensor(at_i[:, s], at[:, s], rank[:, s], ALU.add).then_inc(at_ready, 1)
                dve.wait_ge(at_ready, R)

            @block.gpsimd
            def _(pool):
                with pool.Fori(0, R // 2) as i:
                    for s in range(2):
                        gi = 2 * i + s
                        pool.wait_ge(staged, gi + 1)
                        pool.wait_ge(at_ready, gi + 1)
                        pool.sem_inc(pool_go, 1)
                        for j in range(G):
                            pool.indirect_dma_start(
                                o.payload, bass.IndirectOffsetOnAxis(ap=at_i[:, s, j:j + 1].bitcast(U32), axis=0),
                                pay_slot[:, s, j, :], None).then_inc(scattered[s], 16)

            @block.sync
            def _(sp):
                sp.sem_inc(slot_free, 2)
                with sp.Fori(0, R // 2) as i:
                    for s in range(2):
                        sp.wait_ge(scattered[s], 16 * G * (i + 1))
                        sp.sem_inc(slot_free, 1)

    with stage(nc, f"rows_{o.name}") as st:
        rows = st.sb("rows", [R, W, 4])
        key, rel = st.sb("key", [R, W]), st.sb("rel", [R, W])
        last_key, next_key = st.sb("last_key", [P, 1]), st.sb("next_key", [P, 1])
        base_i = st.sb("base_i", [R, 8], I32)
        flag = st.sb("flag", [R, 2])
        loaded, steps, based, based2, turned = (st.sem(n) for n in ("loaded", "steps", "based", "based2", "turned"))
        edge_keys = o.payload.rearrange("(r w) f -> r w f", w=W)
        ps_flag = st.ps("flag", [P, 2, P])
        with nc.Block() as block:
            @block.sync
            def _(sp):
                sp.dma_start(rows[:].rearrange("r w f -> r (w f)"),
                             o.payload.rearrange("(r w) f -> r (w f)", w=W)).then_inc(loaded, 16)
                sp.wait_ge(steps, 2)
                with nc.allow_non_contiguous_dma(reason="one key per row"):
                    sp.dma_start(last_key[1:R, :], edge_keys[0:R - 1, W - 1, 0:1]).then_inc(loaded, 16)
                    sp.dma_start(next_key[0:R - 1, :], edge_keys[1:R, 0, 0:1]).then_inc(loaded, 16)
                sp.wait_ge(based, 1)
                sp.dma_start(o.base_dram.rearrange("o (r g) -> (o r) g", g=8), base_i[:]).then_inc(based2, 16)
                sp.wait_ge(based2, 16)
                sp.dma_start(o.base[:], o.base_dram).then_inc(based2, 16)
                sp.wait_ge(based2, 32)

            @block.vector
            def _(dve):
                link = Chain(dve, steps)
                link(dve.memset(last_key[:], -1.0))
                link(dve.memset(next_key[:], -1.0))
                link(dve.memset(base_i[:], 0))
                dve.wait_ge(loaded, 48)
                link(dve.tensor_copy(key[:], rows[:, :, 0]))
                firsts = key[:].rearrange("r (g e) -> r g e", e=P)[:, :, 0]
                link(dve.tensor_copy(base_i[:, 0:G], firsts))
                dve.sem_inc(based, 1)
                link(dve.tensor_tensor(rel[:].rearrange("r (g e) -> r g e", e=P),
                                       key[:].rearrange("r (g e) -> r g e", e=P), over_tiles(firsts, P), ALU.subtract))
                link(dve.tensor_tensor(o.start[:, 1:W], key[:, 1:W], key[:, 0:W - 1], ALU.not_equal))
                link(dve.tensor_tensor(o.start[:, 0:1], key[:, 0:1], last_key[0:R, :], ALU.not_equal))
                link(dve.tensor_tensor(o.end[:, 0:W - 1], key[:, 1:W], key[:, 0:W - 1], ALU.not_equal))
                link(dve.tensor_tensor(o.end[:, W - 1:W], key[:, W - 1:W], next_key[0:R, :], ALU.not_equal))
                link(dve.tensor_reduce(flag[:, 0:1], o.start[:], AX.X, ALU.max))
                link(dve.tensor_reduce(flag[:, 1:2], o.end[:], AX.X, ALU.max))
                dve.wait_ge(turned, 1)
                link(dve.tensor_copy(o.has_start[:], ps_flag[0:1, 0, 0:R]))
                link(dve.tensor_copy(o.has_end[:], ps_flag[0:1, 1, 0:R]))

            @block.tensor
            def _(pe):
                pe.wait_ge(steps, 12)
                pe.transpose(ps_flag[0:1, 0, 0:R], flag[:, 0:1], c.ident[0:R, 0:R])
                pe.transpose(ps_flag[0:1, 1, 0:R], flag[:, 1:2], c.ident[0:R, 0:R]).then_inc(turned, 1)

        rows_to_columns(nc, c, f"turn_{o.name}", [
            (rows[:, :, 1], [o.other]), (rel[:], [o.rel, o.rel_bf]), (rows[:, :, 2], [o.weight])])
        if o.real is not None:
            with stage(nc, f"real_{o.name}") as st2:
                done = st2.sem("done")
                with nc.Block() as block:
                    @block.vector
                    def _(dve):
                        dve.tensor_copy(o.real[:], rows[:, :, 3]).then_inc(done, 1)
                        dve.tensor_copy(o.length[:], rows[:, :, 2]).then_inc(done, 1)
                        dve.wait_ge(done, 2)


def rows_to_columns(nc, c, name, pairs):
    with stage(nc, name) as st:
        ps = st.ps("turn", [P, 2, 8, P])
        turned, copied = st.sem("turned"), st.sem("copied")
        with nc.Block() as block:
            @block.tensor
            def _(pe):
                done = 0
                for n, (row, cols) in enumerate(pairs):
                    if n >= 2:
                        pe.wait_ge(copied, sum(len(x) for _, x in pairs[:n - 1]))
                    for g in range(G):
                        mm = pe.transpose(ps[:, n % 2, g, 0:R], row[:, g * P:(g + 1) * P], c.ident[0:R, 0:R])
                    mm.then_inc(turned, 1)

            @block.scalar
            def _(act):
                for n, (row, cols) in enumerate(pairs):
                    act.wait_ge(turned, n + 1)
                    for col in cols:
                        act.copy(col[:].rearrange("p (r g) -> p g r", g=G),
                                 ps[:, n % 2, 0:G, 0:R]).then_inc(copied, 1)
                act.wait_ge(copied, sum(len(x) for _, x in pairs))


def load_weights(nc, name, loads):
    with stage(nc, name) as st:
        loaded = st.sem("loaded")
        with nc.Block() as block:
            @block.sync
            def _(sp):
                with nc.allow_non_contiguous_dma(reason="vectors across partitions, once"):
                    for dst, src in loads:
                        sp.dma_start(dst, src).then_inc(loaded, 16)
                sp.wait_ge(loaded, 16 * len(loads))


def spread_row(vec, n):
    return vec.rearrange("(o n) -> o n", o=1).to_broadcast([P, n])


def transpose_weights(nc, c, name, pairs):
    with stage(nc, name) as st:
        ps = st.ps("turn", [P, len(pairs), 512])
        turned, copied = st.sem("turned"), st.sem("copied")
        with nc.Block() as block:
            @block.tensor
            def _(pe):
                for n, (dst, src) in enumerate(pairs):
                    k, m = src.shape
                    pe.transpose(ps[0:m, n, 0:k], src, c.ident[0:k, 0:k]).then_inc(turned, 1)

            @block.vector
            def _(dve):
                for n, (dst, src) in enumerate(pairs):
                    k, m = src.shape
                    dve.wait_ge(turned, n + 1)
                    dve.tensor_copy(dst, ps[0:m, n, 0:k]).then_inc(copied, 1)
                dve.wait_ge(copied, len(pairs))


def node_tables(nc, c, name, x, weight, bias, out_w, tables, dots=None):
    with stage(nc, name) as st:
        xs, xt, y = st.sb("xs", [P, 2, D]), st.sb("xt", [P, 2, D]), st.sb("y", [P, 2, out_w])
        prod, dot = st.sb("prod", [P, 2, D]), st.sb("dot", [P, 2, 1])
        ps_t, ps_y = st.ps("t", [P, 2, 512]), st.ps("y", [P, 2, 512])
        xs_ready, turned, xt_ready, multiplied, y_ready, dot_ready, slot_free = (
            st.sem(n) for n in ("xs_ready", "turned", "xt_ready", "multiplied", "y_ready", "dot_ready", "slot_free"))
        stored = [st.sem(f"stored{s}") for s in range(2)]
        n_st = len(tables) + (dots is not None)
        with nc.Block() as block:
            @block.scalar
            def _(act):
                act.sem_inc(slot_free, 2)
                with act.Fori(0, NB // 2) as i:
                    for s in range(2):
                        b = 2 * i + s
                        act.wait_ge(slot_free, b + 1)
                        act.copy(xs[:, s], x[:, b, :]).then_inc(xs_ready, 1)
                        act.wait_ge(turned, b + 1)
                        act.copy(xt[:, s], ps_t[:, s, 0:P]).then_inc(xt_ready, 1)

            @block.tensor
            def _(pe):
                with pe.Fori(0, NB // 2) as i:
                    for s in range(2):
                        b = 2 * i + s
                        pe.wait_ge(xs_ready, b + 1)
                        pe.transpose(ps_t[:, s, 0:P], xs[:, s], c.ident[:]).then_inc(turned, 1)
                        pe.wait_ge(xt_ready, b + 1)
                        pe.matmul(ps_y[:, s, 0:out_w], xt[:, s], weight, start=True, stop=True).then_inc(multiplied, 1)

            @block.vector
            def _(dve):
                with dve.Fori(0, NB // 2) as i:
                    for s in range(2):
                        b = 2 * i + s
                        dve.wait_ge(multiplied, b + 1)
                        if bias is None:
                            dve.tensor_copy(y[:, s], ps_y[:, s, 0:out_w]).then_inc(y_ready, 1)
                        else:
                            dve.tensor_tensor(y[:, s], ps_y[:, s, 0:out_w], bias, ALU.add).then_inc(y_ready, 1)
                        if dots is not None:
                            dve.wait_ge(y_ready, b + 1)
                            dve.tensor_tensor(prod[:, s], y[:, s, 0:D], dots[0], ALU.mult).then_inc(dot_ready, 1)
                            dve.wait_ge(dot_ready, 2 * b + 1)
                            dve.tensor_reduce(dot[:, s], prod[:, s], AX.X, ALU.add).then_inc(dot_ready, 1)

            @block.sync
            def _(sp):
                with sp.Fori(0, NB // 2) as i:
                    for s in range(2):
                        b = 2 * i + s
                        sp.wait_ge(y_ready, b + 1)
                        if dots is not None:
                            sp.wait_ge(dot_ready, 2 * b + 2)
                        for table, c0, w in tables:
                            sp.dma_start(table[bass.ds(b * P, P), :], y[:, s, c0:c0 + w]).then_inc(stored[s], 16)
                        if dots is not None:
                            with nc.allow_non_contiguous_dma(reason="one value per node"):
                                sp.dma_start(dots[1][bass.ds(b * P, P), :], dot[:, s]).then_inc(stored[s], 16)
                    for s in range(2):
                        sp.wait_ge(stored[s], (16 * n_st) * (i + 1))
                        sp.sem_inc(slot_free, 1)


def edge_scores(nc, c, o, name, table, table_w, window, window_w, spill, spill_at, scores, heads, mode, k):
    with stage(nc, name) as st:
        idx = st.sb("idx", [P, SLOTS, G], I32)
        rel = st.sb("rel", [P, SLOTS, G], BF16)
        rows = st.sb("rows", [P, SLOTS, G, table_w])
        win = st.sb("win", [P, SLOTS, G, window_w])
        hot_t = st.sb("hot_t", [P, G, P])
        prod, act_m = st.sb("prod", [P, G, D]), st.sb("act_m", [P, G, D])
        red = st.sb("red", [P, G * heads])
        ps_rel, ps_x = st.ps("rel", [P, 8, P]), st.ps("x", [P, 8, P])
        (idx_staged, rel_staged, spread, hot_ready, expanded, consumed, reduced, scored, spill_done, pool_go, multiplied,
         leaked) = (
            st.sem(n) for n in ("idx_staged", "rel_staged", "spread", "hot_ready", "expanded", "consumed", "reduced",
                                "scored", "spill_done", "pool_go", "multiplied", "leaked"))
        gathered, win_loaded, spilled = ([st.sem(f"{n}{s}") for s in range(SLOTS)]
                                         for n in ("gathered", "win_loaded", "spilled"))
        bias_mode = mode == "dot"
        if bias_mode:
            length = st.sb("length", [P, SLOTS, G])
            hidden = st.sb("hidden", [P, G, P])
            ps_len, ps_bias = st.ps("len", [P, 8, P]), st.ps("bias", [P, G, H0])
            len_staged, len_spread, hid_ready, biased = (
                st.sem(n) for n in ("len_staged", "len_spread", "hid_ready", "biased"))
        with nc.Block() as block:
            @block.scalar
            def _(act):
                with act.Fori(0, R // SLOTS) as i:
                    for s in range(SLOTS):
                        gi = SLOTS * i + s
                        act.wait_ge(consumed, gi + 1)
                        act.copy(idx[:, s], group(o.other, gi)).then_inc(idx_staged, 1)
                        act.copy(rel[:, s], group(o.rel_bf, gi)).then_inc(rel_staged, 1)
                        if bias_mode:
                            act.copy(length[:, s], group(o.weight, gi)).then_inc(len_staged, 1)
                        _, base = nc.values_load_multi_w_load_instructions(
                            o.base[0:1, bass.ds(gi * 8, 8)], engines=[act.engine], min_val=0, max_val=N,
                            skip_runtime_bounds_check_because="keys are node numbers")
                        with nc.allow_non_contiguous_dma(reason="a row of one value per node"):
                            for j in range(G):
                                act.dma_start(win[:, s, j, :], window[bass.ds(base[j], P), :]).then_inc(win_loaded[s], 16)
                        if bias_mode:
                            act.wait_ge(len_spread, gi + 1)
                            act.wait_ge(biased, gi + 1)
                            act.activation(hidden[:], ps_len[:, 0:G, :], ACT.Silu, bias=k["be1"],
                                           scale=k["we1"]).then_inc(hid_ready, 1)

            @block.gpsimd
            def _(pool):
                with pool.Fori(0, R // SLOTS) as i:
                    for s in range(SLOTS):
                        gi = SLOTS * i + s
                        pool.wait_ge(idx_staged, gi + 1)
                        pool.wait_ge(spill_done, gi + 1)
                        pool.sem_inc(pool_go, 1)
                        for j in range(G):
                            pool.indirect_dma_start(
                                rows[:, s, j, :], None, table,
                                bass.IndirectOffsetOnAxis(ap=idx[:, s, j:j + 1].bitcast(U32), axis=0)
                            ).then_inc(gathered[s], 16)

            @block.sync
            def _(sp):
                sp.sem_inc(spill_done, SLOTS)
                with sp.Fori(0, R // SLOTS) as i:
                    for s in range(SLOTS):
                        gi = SLOTS * i + s
                        sp.wait_ge(gathered[s], (16 * G) * (i + 1))
                        sp.dma_start(spill[bass.ds(gi * P, P), :].rearrange("p (g d) -> p g d", g=G),
                                     rows[:, s, :, spill_at:spill_at + D]).then_inc(spilled[s], 16)
                        if s > 0:
                            sp.wait_ge(spilled[s - 1], 16 * (i + 1))
                            sp.sem_inc(spill_done, 1)
                    sp.wait_ge(spilled[SLOTS - 1], 16 * (i + 1))
                    sp.sem_inc(spill_done, 1)

            @block.tensor
            def _(pe):
                if bias_mode:
                    pe.sem_inc(biased, 1)
                with pe.Fori(0, R // SLOTS) as i:
                    for s in range(SLOTS):
                        gi = SLOTS * i + s
                        pe.wait_ge(rel_staged, gi + 1)
                        pe.wait_ge(hot_ready, gi + 1)
                        for j in range(G):
                            mm = pe.matmul(ps_rel[:, j, :], rel[:, s, j:j + 1].to_broadcast([P, P]), c.ident_bf[:],
                                           start=True, stop=True)
                        mm.then_inc(spread, 1)
                        if bias_mode:
                            pe.wait_ge(len_staged, gi + 1)
                            for j in range(G):
                                mm = pe.matmul(ps_len[:, j, :], length[:, s, j:j + 1].to_broadcast([P, P]), c.ident[:],
                                               start=True, stop=True)
                            mm.then_inc(len_spread, 1)
                        pe.wait_ge(hot_ready, gi + 2)
                        pe.wait_ge(win_loaded[s], (16 * G) * (i + 1))
                        pe.wait_ge(consumed, gi + SLOTS)
                        for j in range(G):
                            mm = pe.matmul(ps_x[:, j, 0:window_w], hot_t[:, j, :], win[:, s, j, :], start=True, stop=True)
                        mm.then_inc(expanded, 1)
                        if bias_mode:
                            pe.wait_ge(hid_ready, gi + 1)
                            pe.wait_ge(scored, gi + 1)
                            for j in range(G):
                                mm = pe.matmul(ps_bias[:, j, :], hidden[:, j, :], k["we2t"], start=True, stop=True)
                            mm.then_inc(biased, 1)

            @block.vector
            def _(dve):
                dve.sem_inc(consumed, SLOTS)
                dve.sem_inc(hot_ready, 1)
                dve.sem_inc(scored, 1)
                with dve.Fori(0, R // SLOTS) as i:
                    for s in range(SLOTS):
                        gi = SLOTS * i + s
                        dve.wait_ge(spread, gi + 1)
                        dve.tensor_scalar(hot_t[:], ps_rel[:, 0:G, :], c.lane[:, 0:1], None,
                                          ALU.is_equal).then_inc(hot_ready, 1)
                        dve.wait_ge(expanded, gi + 1)
                        dve.wait_ge(gathered[s], (16 * G) * (i + 1))
                        out = scores[:, bass.ds(gi * (G * heads), G * heads)]
                        if mode == "dot":
                            dve.tensor_tensor(prod[:], ps_x[:, 0:G, :], rows[:, s, :, 0:D], ALU.mult).then_inc(consumed, 1)
                            dve.wait_ge(consumed, gi + (SLOTS + 1))
                            dve.tensor_reduce(red[:], prod[:].rearrange("p g (h d) -> p (g h) d", h=heads),
                                              AX.X, ALU.add).then_inc(reduced, 1)
                            dve.wait_ge(reduced, gi + 1)
                            dve.wait_ge(biased, gi + 2)
                            dve.scalar_tensor_tensor(out, red[:], 1.0 / (D // heads) ** 0.5,
                                                     ps_bias[:].rearrange("p g h -> p (g h)"),
                                                     ALU.mult, ALU.add).then_inc(scored, 1)
                        elif mode == "gat2":
                            dve.tensor_tensor(prod[:], ps_x[:, 0:G, :], rows[:, s], ALU.add).then_inc(consumed, 1)
                            dve.wait_ge(consumed, gi + (SLOTS + 1))
                            dve.scalar_tensor_tensor(act_m[:], prod[:], 0.2, prod[:], ALU.mult, ALU.max).then_inc(leaked, 1)
                            dve.wait_ge(leaked, gi + 1)
                            dve.tensor_tensor(prod[:], act_m[:], per_tile(k["att"]), ALU.mult).then_inc(multiplied, 1)
                            dve.wait_ge(multiplied, gi + 1)
                            dve.tensor_reduce(out, prod[:].rearrange("p g (h d) -> p (g h) d", h=heads),
                                              AX.X, ALU.add).then_inc(scored, 1)
                        else:
                            dve.tensor_tensor(prod[:], rows[:, s], per_tile(k["att"]), ALU.mult).then_inc(multiplied, 1)
                            dve.wait_ge(multiplied, gi + 1)
                            dve.tensor_reduce(red[:], prod[:], AX.X, ALU.add).then_inc(reduced, 1)
                            dve.wait_ge(reduced, gi + 1)
                            dve.tensor_tensor(act_m[:, 0, 0:G], ps_x[:, 0:G, 0], red[:], ALU.add).then_inc(consumed, 1)
                            dve.wait_ge(consumed, gi + (SLOTS + 1))
                            dve.scalar_tensor_tensor(out, act_m[:, 0, 0:G], 0.2, act_m[:, 0, 0:G],
                                                     ALU.mult, ALU.max).then_inc(scored, 1)
                dve.wait_ge(scored, R + 1)


def weighted_sum(nc, c, o, name, acc, alpha, heads, spill=None, table=None):
    with stage(nc, name) as st:
        rows = st.sb("rows", [P, SLOTS, G, D])
        hot, msg = st.sb("hot", [P, SLOTS, G, P]), st.sb("msg", [P, SLOTS, G, D])
        idx = st.sb("idx", [P, SLOTS, G], I32)
        ps_sum = st.ps("sum", [P, SLOTS, 8, P])
        ready, hot_ready, summed, added, idx_staged, pool_go, used = (
            st.sem(n) for n in ("ready", "hot_ready", "summed", "added", "idx_staged", "pool_go", "used"))
        loaded = [st.sem(f"loaded{s}") for s in range(SLOTS)]
        per_slot = 16 * (G if spill is None else 1)
        with nc.Block() as block:
            if spill is not None:
                @block.sync
                def _(sp):
                    with sp.Fori(0, R // SLOTS) as i:
                        for s in range(SLOTS):
                            gi = SLOTS * i + s
                            sp.wait_ge(ready, gi + 1)
                            sp.dma_start(rows[:, s].rearrange("p g d -> p (g d)"),
                                         spill[bass.ds(gi * P, P), :]).then_inc(loaded[s], 16)
            else:
                @block.scalar
                def _(act):
                    with act.Fori(0, R // SLOTS) as i:
                        for s in range(SLOTS):
                            gi = SLOTS * i + s
                            act.wait_ge(ready, gi + 1)
                            act.copy(idx[:, s], group(o.other, gi)).then_inc(idx_staged, 1)

                @block.gpsimd
                def _(pool):
                    with pool.Fori(0, R // SLOTS) as i:
                        for s in range(SLOTS):
                            gi = SLOTS * i + s
                            pool.wait_ge(idx_staged, gi + 1)
                            pool.sem_inc(pool_go, 1)
                            for j in range(G):
                                pool.indirect_dma_start(
                                    rows[:, s, j, :], None, table,
                                    bass.IndirectOffsetOnAxis(ap=idx[:, s, j:j + 1].bitcast(U32), axis=0)
                                ).then_inc(loaded[s], 16)

            @block.vector
            def _(dve):
                dve.memset(acc[:], 0.0).then_inc(added, 1)
                dve.sem_inc(ready, SLOTS)

                def messages(i, s):
                    gi = SLOTS * i + s
                    dve.tensor_tensor(hot[:, s], per_tile(c.column[:]), over_tiles(group(o.rel, gi), P),
                                      ALU.is_equal).then_inc(hot_ready, 1)
                    dve.wait_ge(loaded[s], per_slot * (i + 1))
                    w = alpha[:, bass.ds(gi * (G * heads), G * heads)]
                    dve.tensor_tensor(msg[:, s].rearrange("p g (h d) -> p (g h) d", h=heads),
                                      rows[:, s].rearrange("p g (h d) -> p (g h) d", h=heads),
                                      over_tiles(w, D // heads), ALU.mult).then_inc(ready, 1)

                def add(i, s):
                    gi = SLOTS * i + s
                    _, base = nc.values_load_multi_w_load_instructions(
                        o.base[0:1, bass.ds(gi * 8, 8)], engines=[dve.engine], min_val=0, max_val=N,
                        skip_runtime_bounds_check_because="keys are node numbers")
                    dve.wait_ge(summed, gi + 1)
                    for j in range(G):
                        at = acc[:, bass.ds(base[j], P)]
                        dve.wait_ge(added, gi * G + (j + 1))
                        dve.tensor_tensor(at, at, ps_sum[:, s, j, :], ALU.add).then_inc(added, 1)

                with dve.Fori(0, R // SLOTS) as i:
                    messages(i, 0)
                    for s in range(1, SLOTS):
                        messages(i, s)
                        add(i, s - 1)
                    add(i, SLOTS - 1)
                dve.wait_ge(added, T + 1)

            @block.tensor
            def _(pe):
                with pe.Fori(0, R // SLOTS) as i:
                    for s in range(SLOTS):
                        gi = SLOTS * i + s
                        pe.wait_ge(hot_ready, gi + 1)
                        pe.wait_ge(ready, gi + (SLOTS + 1))
                        for j in range(G):
                            mm = pe.matmul(ps_sum[:, s, j, :], msg[:, s, j, :], hot[:, s, j, :], start=True, stop=True)
                        mm.then_inc(summed, 1)


def segment_softmax(nc, c, o, name, scores, heads, first):
    with stage(nc, name) as st:
        e, f, g = st.sb("e", [R, heads, W]), st.sb("f", [R, W]), st.sb("g", [R, W])
        keep, keep_end, neg = st.sb("keep", [R, W]), st.sb("keep_end", [R, W]), st.sb("neg", [R, W])
        r_keep, r_keep_end, r_neg = st.sb("r_keep", [1, R]), st.sb("r_keep_end", [1, R]), st.sb("r_neg", [1, R])
        last, carry = st.sb("last", [R, 1]), st.sb("carry", [R, 1])
        chain_row = st.sb("chain_row", [1, R + 1])
        col_max, max_row, neg_max = st.sb("col_max", [R, H0]), st.sb("max_row", [1, H0]), st.sb("neg_max", [R, H0])
        ps_row, ps_col, ps_turn = st.ps("row", [P, 512]), st.ps("col", [P, 512]), st.ps("turn", [P, 2, 8, P])
        (steps, turned, copied, last_ready, row_turned, row_ready, col_turned, exp_in, exp_out, max_in, max_t, max_row_s,
         max_all, done) = (
            st.sem(n) for n in ("steps", "turned", "copied", "last_ready", "row_turned", "row_ready", "col_turned",
                                "exp_in", "exp_out", "max_in", "max_t", "max_row", "max_all", "done"))
        n_carry = heads * (2 if first else 4)
        cols = scores[:].rearrange("p (r g h) -> p g h r", g=G, h=heads)
        with nc.Block() as block:
            @block.tensor
            def _(pe):
                for h in range(heads):
                    if h >= 2:
                        pe.wait_ge(copied, h - 1)
                    for t in range(G):
                        mm = pe.transpose(ps_turn[0:R, h % 2, t, :], cols[:, t, h, :], c.ident[:])
                    mm.then_inc(turned, 1)
                if first:
                    for h in range(heads):
                        pe.wait_ge(max_in, 1)
                        mm = pe.transpose(ps_col[0:1, 0:R] if h % 2 else ps_row[0:1, 0:R], col_max[:, h:h + 1],
                                          c.ident[0:R, 0:R])
                        mm.then_inc(max_t, 1)
                        pe.wait_ge(max_row_s, h + 1)
                    pe.matmul(ps_row[0:R, 0:heads], c.ones[0:1, 0:R], max_row[0:1, 0:heads],
                              start=True, stop=True).then_inc(max_all, 1)
                    pe.wait_ge(done, 1)
                for n in range(n_carry):
                    pe.wait_ge(last_ready, n + 1)
                    pe.transpose(ps_row[0:1, 0:R], last[:], c.ident[0:R, 0:R]).then_inc(row_turned, 1)
                    pe.wait_ge(row_ready, n + 1)
                    row = chain_row[0:1, 0:R] if n % 2 == 0 else chain_row[0:1, 1:R + 1]
                    pe.transpose(ps_col[0:R, 0:1], row, c.ident[0:1, 0:1]).then_inc(col_turned, 1)

            @block.scalar
            def _(act):
                for h in range(heads):
                    act.wait_ge(turned, h + 1)
                    act.copy(e[:, h].rearrange("r (g j) -> r g j", g=G), ps_turn[0:R, h % 2, 0:G, :]).then_inc(copied, 1)
                for h in range(heads):
                    act.wait_ge(exp_in, h + 1)
                    if first:
                        act.activation(e[:, h], e[:, h], ACT.Exp, bias=neg_max[:, h:h + 1]).then_inc(exp_out, 1)
                    else:
                        act.activation(e[:, h], e[:, h], ACT.Exp).then_inc(exp_out, 1)
                act.wait_ge(exp_out, heads)

            @block.vector
            def _(dve):
                link = Chain(dve, steps)
                n = [0]

                def scanned(out, a, b, start, op0, op1, row_flags, backward):
                    way = slice(None, None, -1) if backward else slice(None)
                    link(dve.tensor_tensor_scan(out[:, way], a[:, way], b[:, way], start, op0, op1))
                    dve.tensor_copy(last[:], out[:, 0:1] if backward else out[:, W - 1:W]).then_inc(last_ready, 1)
                    dve.wait_ge(row_turned, n[0] + 1)
                    if backward:
                        link(dve.memset(chain_row[0:1, R:R + 1], start))
                        dve.tensor_tensor_scan(chain_row[0:1, 0:R][:, ::-1], row_flags[0:1, ::-1], ps_row[0:1, 0:R][:, ::-1],
                                               start, op0, op1).then_inc(row_ready, 1)
                    else:
                        link(dve.memset(chain_row[0:1, 0:1], start))
                        dve.tensor_tensor_scan(chain_row[0:1, 1:R + 1], row_flags, ps_row[0:1, 0:R],
                                               start, op0, op1).then_inc(row_ready, 1)
                    n[0] += 1
                    dve.wait_ge(col_turned, n[0])
                    link(dve.tensor_copy(carry[:], ps_col[0:R, 0:1]))
                    link(dve.tensor_tensor_scan(out[:, way], a[:, way], b[:, way], carry[:, 0:1], op0, op1))

                def whole(out, tmp):
                    link(dve.tensor_tensor(tmp, tmp, o.end[:], ALU.mult))
                    scanned(out, keep_end, tmp, 0.0, ALU.mult, ALU.add, r_keep_end[:], True)

                link(dve.tensor_scalar(keep[:], o.start[:], -1.0, 1.0, ALU.mult, ALU.add))
                link(dve.tensor_scalar(keep_end[:], o.end[:], -1.0, 1.0, ALU.mult, ALU.add))
                link(dve.tensor_scalar(neg[:], o.start[:], -BIG, None, ALU.mult))
                link(dve.tensor_scalar(r_keep[:], o.has_start[:], -1.0, 1.0, ALU.mult, ALU.add))
                link(dve.tensor_scalar(r_keep_end[:], o.has_end[:], -1.0, 1.0, ALU.mult, ALU.add))
                link(dve.tensor_scalar(r_neg[:], o.has_start[:], -BIG, None, ALU.mult))
                dve.wait_ge(copied, heads)
                if first:
                    link(dve.tensor_scalar(neg[:], first["real"], BIG, -BIG, ALU.mult, ALU.add))
                    for h in range(heads):
                        link(dve.scalar_tensor_tensor(e[:, h], e[:, h], first["be2"][0:R, h:h + 1], first["cut"],
                                                      ALU.add, ALU.mult))
                        link(dve.tensor_tensor(e[:, h], e[:, h], neg[:], ALU.add))
                        link(dve.tensor_reduce(col_max[:, h:h + 1], e[:, h], AX.X, ALU.max))
                    dve.sem_inc(max_in, 1)
                    for h in range(heads):
                        dve.wait_ge(max_t, h + 1)
                        dve.tensor_reduce(max_row[0:1, h:h + 1], (ps_col if h % 2 else ps_row)[0:1, 0:R], AX.X,
                                          ALU.max).then_inc(max_row_s, 1)
                    dve.wait_ge(max_all, 1)
                    dve.tensor_scalar(neg_max[:], ps_row[0:R, 0:heads], -1.0, None, ALU.mult).then_inc(done, 1)
                    dve.wait_ge(done, 1)
                    dve.sem_inc(exp_in, heads)
                else:
                    for h in range(heads):
                        scanned(f, neg, e[:, h], -BIG, ALU.add, ALU.max, r_neg[:], False)
                        whole(g, f[:])
                        dve.tensor_tensor(e[:, h], e[:, h], g[:], ALU.subtract).then_inc(exp_in, 1)
                        dve.wait_ge(exp_in, h + 1)
                for h in range(heads):
                    dve.wait_ge(exp_out, h + 1)
                    scanned(f, keep, e[:, h], 0.0, ALU.mult, ALU.add, r_keep[:], False)
                    whole(g, f[:])
                    if first:
                        link(dve.tensor_scalar(g[:], g[:], 1e-8, None, ALU.add))
                    link(dve.reciprocal(f[:], g[:]))
                    link(dve.tensor_tensor(e[:, h], e[:, h], f[:], ALU.mult))
        with stage(nc, name + "_turn") as st2:
            back, out = st2.sem("back"), st2.sem("out")
            with nc.Block() as block:
                @block.tensor
                def _(pe):
                    for h in range(heads):
                        if h >= 2:
                            pe.wait_ge(out, h - 1)
                        for t in range(G):
                            mm = pe.transpose(ps_turn[:, h % 2, t, 0:R], e[:, h, t * P:(t + 1) * P], c.ident[0:R, 0:R])
                        mm.then_inc(back, 1)

                @block.scalar
                def _(act):
                    for h in range(heads):
                        act.wait_ge(back, h + 1)
                        act.copy(cols[:, :, h, :], ps_turn[:, h % 2, 0:G, 0:R]).then_inc(out, 1)
                    act.wait_ge(out, heads)


def cutoff(nc, o, cut):
    with stage(nc, "cutoff") as st:
        u, ui = st.sb("u", [R, W]), st.sb("ui", [R, W], I32)
        v, inside = st.sb("v", [R, W]), st.sb("inside", [R, W])
        half_pi = st.sb("half_pi", [R, 1])
        steps, turn_ready, sined = st.sem("steps"), st.sem("turn_ready"), st.sem("sined")
        two_pi = 6.283185307179586
        with nc.Block() as block:
            @block.vector
            def _(dve):
                link = Chain(dve, steps)
                link(dve.memset(half_pi[:], two_pi / 4))
                link(dve.tensor_scalar(u[:], o.length[:], 0.5 / CUTOFF, None, ALU.mult))
                link(dve.tensor_copy(ui[:], u[:]))
                link(dve.tensor_copy(v[:], ui[:]))
                link(dve.tensor_tensor(u[:], u[:], v[:], ALU.subtract))
                link(dve.scalar_tensor_tensor(u[:], u[:], -1.0, u[:], ALU.mult, ALU.max))
                link(dve.tensor_scalar(v[:], u[:], -1.0, 1.0, ALU.mult, ALU.add))
                link(dve.tensor_tensor(u[:], u[:], v[:], ALU.min))
                dve.sem_inc(turn_ready, 1)
                link(dve.tensor_scalar(inside[:], o.length[:], CUTOFF, 0.5, ALU.is_lt, ALU.mult))
                dve.wait_ge(sined, 1)
                link(dve.scalar_tensor_tensor(cut[:], v[:], 1.0, inside[:], ALU.add, ALU.mult))

            @block.scalar
            def _(act):
                act.wait_ge(turn_ready, 1)
                act.activation(v[:], u[:], ACT.Sin, bias=half_pi[:, 0:1], scale=-two_pi).then_inc(sined, 1)
                act.wait_ge(sined, 1)


def batch_norm_relu(nc, acc, k):
    with stage(nc, "batch_norm") as st:
        sq = st.sb("sq", [P, N])
        m, scale, ss = st.sb("m", [P, 1]), st.sb("scale", [P, 1]), st.sb("ss", [P, 1])
        steps, centred, squared, scaled, out = (st.sem(n) for n in ("steps", "centred", "squared", "scaled", "out"))
        var_ready, rooted = st.sem("var_ready"), st.sem("rooted")
        a = acc[:, 0:N]
        with nc.Block() as block:
            @block.vector
            def _(dve):
                link = Chain(dve, steps)
                link(dve.tensor_scalar(a, a, k["bias"], None, ALU.add))
                link(dve.tensor_reduce(m[:], a, AX.X, ALU.add))
                link(dve.tensor_scalar(m[:], m[:], 1.0 / N, None, ALU.mult))
                link(dve.tensor_scalar(a, a, m[:, 0:1], None, ALU.subtract))
                dve.sem_inc(centred, 1)
                dve.wait_ge(squared, 1)
                link(dve.tensor_scalar(scale[:], ss[:], 1.0 / N, LN_EPS, ALU.mult, ALU.add))
                link(dve.reciprocal(m[:], scale[:]))
                dve.sem_inc(var_ready, 1)
                dve.wait_ge(rooted, 1)
                link(dve.tensor_tensor(scale[:], scale[:], k["gamma"], ALU.mult))
                dve.sem_inc(scaled, 1)

            @block.scalar
            def _(act):
                act.wait_ge(centred, 1)
                act.activation(sq[:], a, ACT.Square, accum_out=ss[:, 0:1]).then_inc(squared, 1)
                act.wait_ge(squared, 1)
                act.wait_ge(var_ready, 1)
                act.activation(scale[:], m[:], ACT.Sqrt).then_inc(rooted, 1)
                act.wait_ge(scaled, 1)
                act.activation(a, a, ACT.Relu, bias=k["beta"], scale=scale[:, 0:1]).then_inc(out, 1)
                act.wait_ge(out, 1)


def node_update(nc, c, name, acc, x, mode, k):
    with stage(nc, name) as st:
        at, xs, xt = st.sb("at", [P, 2, P]), st.sb("xs", [P, 2, D]), st.sb("xt", [P, 2, D])
        h, y, z = st.sb("h", [P, 2, D]), st.sb("y", [P, 2, D]), st.sb("z", [P, 2, D])
        stats, mv, rs = st.sb("stats", [P, 6]), st.sb("mv", [P, 2]), st.sb("rs", [P, 1])
        ve, inverse = st.sb("ve", [P, 1]), st.sb("inverse", [P, 1])
        var_ready, rs_ready, stats_go = st.sem("var_ready"), st.sem("rs_ready"), st.sem("stats_go")
        ps_y, ps_t = st.ps("y", [P, 2, 512]), st.ps("t", [P, 2, 512])
        at_ready, xs_ready, turned, xt_ready, multiplied, steps, slot_free, z_ready = (
            st.sem(n) for n in ("at_ready", "xs_ready", "turned", "xt_ready", "multiplied", "steps", "slot_free",
                                "z_ready"))
        stored = [st.sem(f"stored{s}") for s in range(2)]
        own = mode in ("conv", "last")
        store = {"conv": k.get("table"), "last": k.get("out")}.get(mode)
        n_steps = {"attend": 14, "plain": 6, "conv": 2, "last": 7}[mode]
        n_norms = {"attend": 2, "plain": 1, "conv": 0, "last": 1}[mode]
        with nc.Block() as block:
            @block.scalar
            def _(act):
                with act.Fori(0, NB // 2) as i:
                    for s in range(2):
                        b = 2 * i + s
                        act.wait_ge(slot_free, b + 1)
                        act.copy(at[:, s], acc[:, bass.ds(b * P, P)]).then_inc(at_ready, 1)
                        if own:
                            act.copy(xs[:, s], k["own"][:, b, :]).then_inc(xs_ready, 1)
                            act.wait_ge(turned, b + 1)
                            act.copy(xt[:, s], ps_t[:, s, 0:P]).then_inc(xt_ready, 1)
                        for l in range(n_norms):
                            act.wait_ge(var_ready, b * n_norms + (l + 1))
                            act.activation(rs[:], inverse[:], ACT.Sqrt).then_inc(rs_ready, 1)

            @block.tensor
            def _(pe):
                with pe.Fori(0, NB // 2) as i:
                    for s in range(2):
                        b = 2 * i + s
                        pe.wait_ge(at_ready, b + 1)
                        if mode == "plain":
                            pe.transpose(ps_y[:, s, 0:D], at[:, s], c.ident[:]).then_inc(multiplied, 1)
                        elif mode == "attend":
                            pe.matmul(ps_y[:, s, 0:D], at[:, s], k["w"], start=True, stop=True).then_inc(multiplied, 1)
                        else:
                            pe.wait_ge(xs_ready, b + 1)
                            pe.transpose(ps_t[:, s, 0:P], xs[:, s], c.ident[:]).then_inc(turned, 1)
                            pe.wait_ge(xt_ready, b + 1)
                            pe.matmul(ps_y[:, s, 0:D], at[:, s], k["wr"], start=True, stop=False)
                            pe.matmul(ps_y[:, s, 0:D], xt[:, s], k["ws"], start=False, stop=True).then_inc(multiplied, 1)

            @block.vector
            def _(dve):
                dve.sem_inc(slot_free, 2)
                with dve.Fori(0, NB // 2) as i:
                    for s in range(2):
                        b = 2 * i + s
                        n, norms = [0], [0]

                        def link(ins):
                            n[0] += 1
                            ins.then_inc(steps, 1)
                            dve.wait_ge(steps, b * n_steps + n[0])

                        def layer_norm(dst, src):
                            link(dve.bn_stats(stats[:], src))
                            dve.sem_inc(stats_go, 1)
                            link(dve.bn_aggr(mv[:], stats[:]))
                            link(dve.tensor_scalar(ve[:], mv[:, 1:2], LN_EPS, None, ALU.add))
                            norms[0] += 1
                            dve.reciprocal(inverse[:], ve[:]).then_inc(var_ready, 1)
                            dve.wait_ge(rs_ready, b * n_norms + norms[0])
                            link(dve.tensor_scalar(dst, src, mv[:, 0:1], rs[:, 0:1], ALU.subtract, ALU.mult))

                        xb = x[:, b, :]
                        dve.wait_ge(multiplied, b + 1)
                        link(dve.tensor_tensor(h[:, s], ps_y[:, s, 0:D], k["b"], ALU.add)
                             if mode != "plain" or k.get("b") is not None else dve.tensor_copy(h[:, s], ps_y[:, s, 0:D]))
                        if mode == "attend":
                            link(dve.tensor_tensor(y[:, s], h[:, s], xb, ALU.add))
                            layer_norm(h[:, s], y[:, s])
                            link(dve.tensor_tensor(y[:, s], h[:, s], k["g"], ALU.mult))
                            link(dve.tensor_tensor(h[:, s], y[:, s], k["be"], ALU.add))
                            link(dve.tensor_tensor(y[:, s], h[:, s], xb, ALU.add))
                            link(dve.tensor_copy(z[:, s], y[:, s]))
                            layer_norm(xb, z[:, s])
                        elif mode == "plain":
                            link(dve.tensor_tensor(y[:, s], h[:, s], xb, ALU.add))
                            layer_norm(xb, y[:, s])
                        elif mode == "conv":
                            link(dve.tensor_scalar(k["nodes"][:, b, :], h[:, s], 0.0, None, ALU.max))
                            dve.tensor_scalar(z[:, s], h[:, s], 0.0, None, ALU.max).then_inc(z_ready, 1)
                            dve.wait_ge(z_ready, b + 1)
                        else:
                            link(dve.tensor_scalar(y[:, s], h[:, s], 0.0, None, ALU.max))
                            link(dve.tensor_tensor(h[:, s], y[:, s], xb, ALU.add))
                            layer_norm(z[:, s], h[:, s])
                            dve.sem_inc(z_ready, 1)
                        assert n[0] == n_steps, (mode, n[0])
                        if store is None:
                            dve.sem_inc(slot_free, 1)

            if store is not None:
                @block.sync
                def _(sp):
                    with sp.Fori(0, NB // 2) as i:
                        for s in range(2):
                            b = 2 * i + s
                            sp.wait_ge(z_ready, b + 1)
                            sp.dma_start(store[bass.ds(b * P, P), :], z[:, s]).then_inc(stored[s], 16)
                        for s in range(2):
                            sp.wait_ge(stored[s], 16 * (i + 1))
                            sp.sem_inc(slot_free, 1)


def gnn_kernel(nc, out, x_in, src, dst, length, edge_weight, real, p):
    with ExitStack() as keep:
        sb = lambda n, s, dt=F32: keep.enter_context(nc.sbuf_tensor(n, s, dt))
        dram = lambda n, s: nc.dram_tensor(n, s, F32).ap()
        c = constants(nc, keep)
        by_src, by_dst = Order(nc, "src", keep), Order(nc, "dst", keep)
        x, acc = sb("x_nodes", [P, NB, D]), sb("acc", [P, NP])
        scores = sb("scores", [P, T * H0])
        spill = dram("spill", [R * P, G * D])
        by_dst.real = None
        with ExitStack() as first_layer:
            lsb = lambda n, s, dt=F32: first_layer.enter_context(nc.sbuf_tensor(n, s, dt))
            by_src.real, by_src.length = lsb("real_row", [R, W]), lsb("length_row", [R, W])
            sort_edges(nc, c, by_src, src, dst, length, real)

            w_raw = lsb("w_raw", [P, 4, D])
            we2_raw, we2t = lsb("we2_raw", [H0, D]), lsb("we2t", [D, H0])
            qkv_w, qkv_b, wo_t = lsb("qkv_w", [P, 3 * D]), lsb("qkv_b", [P, 3 * D]), lsb("wo_t", [P, D])
            we1, be1, be2 = lsb("we1", [P, 1]), lsb("be1", [P, 1]), lsb("be2", [P, H0])
            bo, ln_g, ln_b = lsb("bo", [P, D]), lsb("ln_g", [P, D]), lsb("ln_b", [P, D])
            load_weights(nc, "load0", [
                (x[:], x_in.rearrange("(b p) d -> p b d", p=P)),
                (w_raw[:, 0], p["L0_gnn_Wq"]), (w_raw[:, 1], p["L0_gnn_Wk"]), (w_raw[:, 2], p["L0_gnn_Wv"]),
                (w_raw[:, 3], p["L0_gnn_Wo"]), (we2_raw[:], p["L0_gnn_We2"]), (we1[:], p["L0_gnn_We1"]),
                (be1[:], p["L0_gnn_be1"].rearrange("(d o) -> d o", o=1)),
                (be2[:], spread_row(p["L0_gnn_be2"], H0)),
                (qkv_b[:, 0:D], spread_row(p["L0_gnn_bq"], D)), (qkv_b[:, D:2 * D], spread_row(p["L0_gnn_bk"], D)),
                (qkv_b[:, 2 * D:], spread_row(p["L0_gnn_bv"], D)), (bo[:], spread_row(p["L0_gnn_bo"], D)),
                (ln_g[:], spread_row(p["L0_gnn_ln_g"], D)), (ln_b[:], spread_row(p["L0_gnn_ln_b"], D))])
            transpose_weights(nc, c, "turn0", [(qkv_w[:, n * D:(n + 1) * D], w_raw[:, n]) for n in range(3)]
                              + [(wo_t[:], w_raw[:, 3]), (we2t[:], we2_raw[:])])
            q_table, kv_table = dram("q_table", [NP, D]), dram("kv_table", [NP, 2 * D])
            node_tables(nc, c, "qkv", x, qkv_w[:], qkv_b[:], 3 * D, [(q_table, 0, D), (kv_table, D, 2 * D)])
            cut = lsb("cut", [R, W])
            cutoff(nc, by_src, cut)
            edge_scores(nc, c, by_src, "scores0", kv_table, 2 * D, q_table, D, spill, D, scores, H0, "dot",
                        {"we1": we1[:, 0:1], "be1": be1[:, 0:1], "we2t": we2t[:]})
            segment_softmax(nc, c, by_src, "softmax0", scores, H0,
                            {"real": by_src.real[:], "cut": cut[:], "be2": be2})
            weighted_sum(nc, c, by_src, "sum0", acc, scores, H0, spill=spill)
            node_update(nc, c, "update0", acc, x, "attend",
                        {"w": wo_t[:], "b": bo[:], "g": ln_g[:], "be": ln_b[:]})

        sort_edges(nc, c, by_dst, dst, src, edge_weight, real)
        scores1 = scores[:, 0:T * H1]

        lr_w, lr_b = sb("lr_w", [P, 2 * D]), sb("lr_b", [P, 2 * D])
        att, bias1 = sb("att", [P, D]), sb("bias1", [P, D])
        h_w, att_src, att_dst = sb("h_w", [P, D]), sb("att_src", [P, D]), sb("att_dst", [P, D])
        bias2, gamma, beta = sb("bias2", [P, 1]), sb("gamma", [P, 1]), sb("beta", [P, 1])
        conv_w, conv_b = sb("conv_w", [P, 4, D]), sb("conv_b", [P, 2, D])
        column = lambda v: v.rearrange("(d o) -> d o", o=1)
        load_weights(nc, "load1", [
            (lr_w[:, 0:D], p["L1_gnn_W_l"]), (lr_w[:, D:], p["L1_gnn_W_r"]),
            (lr_b[:, 0:D], spread_row(p["L1_gnn_b_l"], D)), (lr_b[:, D:], spread_row(p["L1_gnn_b_r"], D)),
            (att[:], spread_row(p["L1_gnn_att"].rearrange("h c -> (h c)"), D)),
            (bias1[:], spread_row(p["L1_gnn_bias"], D)),
            (h_w[:], p["L2_gnn_W"]), (att_src[:], spread_row(p["L2_gnn_att_src"], D)),
            (att_dst[:], spread_row(p["L2_gnn_att_dst"], D)), (bias2[:], column(p["L2_gnn_bias"])),
            (gamma[:], column(p["L2_gnn_gamma"])), (beta[:], column(p["L2_gnn_beta"])),
            (conv_w[:, 0], p["L3_gnn_Wr0"]), (conv_w[:, 1], p["L3_gnn_Ws0"]),
            (conv_w[:, 2], p["L3_gnn_Wr1"]), (conv_w[:, 3], p["L3_gnn_Ws1"]),
            (conv_b[:, 0], spread_row(p["L3_gnn_br0"], D)), (conv_b[:, 1], spread_row(p["L3_gnn_br1"], D))])
        xl_table, xr_table = dram("xl_table", [NP, D]), dram("xr_table", [NP, D])
        node_tables(nc, c, "lr", x, lr_w[:], lr_b[:], 2 * D, [(xl_table, 0, D), (xr_table, D, D)])
        edge_scores(nc, c, by_dst, "scores1", xl_table, D, xr_table, D, spill, 0, scores1, H1, "gat2", {"att": att[:]})
        segment_softmax(nc, c, by_dst, "softmax1", scores1, H1, None)
        weighted_sum(nc, c, by_dst, "sum1", acc, scores1, H1, spill=spill)
        node_update(nc, c, "update1", acc, x, "plain", {"b": bias1[:]})

        h_table, a_table = dram("h_table", [NP, D]), dram("a_table", [NP, 1])
        node_tables(nc, c, "h", x, h_w[:], None, D, [(h_table, 0, D)], (att_dst[:], a_table))
        scores2 = scores[:, 0:T]
        edge_scores(nc, c, by_dst, "scores2", h_table, D, a_table, 1, spill, 0, scores2, 1, "gat", {"att": att_src[:]})
        segment_softmax(nc, c, by_dst, "softmax2", scores2, 1, None)
        weighted_sum(nc, c, by_dst, "sum2", acc, scores2, 1, spill=spill)
        batch_norm_relu(nc, acc, {"bias": bias2[:, 0:1], "gamma": gamma[:], "beta": beta[:, 0:1]})
        node_update(nc, c, "update2", acc, x, "plain", {})

        x_table, conv_table = dram("x_table", [NP, D]), dram("conv_table", [NP, D])
        h_nodes, unit = sb("h_nodes", [P, NB, D]), sb("unit", [P, T])
        load_weights(nc, "store_x", [(x_table.rearrange("(b p) d -> p b d", p=P), x[:])])
        weighted_sum(nc, c, by_dst, "sum3", acc, by_dst.weight, 1, table=x_table)
        node_update(nc, c, "conv0", acc, x, "conv",
                    {"own": x, "wr": conv_w[:, 0], "ws": conv_w[:, 1], "b": conv_b[:, 0], "nodes": h_nodes,
                     "table": conv_table})
        columns_of_real(nc, c, by_dst, unit)
        weighted_sum(nc, c, by_dst, "sum4", acc, unit, 1, table=conv_table)
        node_update(nc, c, "conv1", acc, x, "last",
                    {"own": h_nodes, "wr": conv_w[:, 2], "ws": conv_w[:, 3], "b": conv_b[:, 1], "out": out})


def columns_of_real(nc, c, o, unit):
    with stage(nc, "real_rows") as st:
        rows, real = st.sb("rows", [R, W, 4]), st.sb("real", [R, W])
        loaded, taken = st.sem("loaded"), st.sem("taken")
        with nc.Block() as block:
            @block.sync
            def _(sp):
                sp.dma_start(rows[:].rearrange("r w f -> r (w f)"),
                             o.payload.rearrange("(r w) f -> r (w f)", w=W)).then_inc(loaded, 16)
                sp.wait_ge(loaded, 16)

            @block.vector
            def _(dve):
                dve.wait_ge(loaded, 16)
                dve.tensor_copy(real[:], rows[:, :, 3]).then_inc(taken, 1)
                dve.wait_ge(taken, 1)
        rows_to_columns(nc, c, "turn_real", [(real[:], [unit])])


_WEIGHTS = ["L0_gnn_Wq", "L0_gnn_bq", "L0_gnn_Wk", "L0_gnn_bk", "L0_gnn_Wv", "L0_gnn_bv", "L0_gnn_We1", "L0_gnn_be1",
            "L0_gnn_We2", "L0_gnn_be2", "L0_gnn_Wo", "L0_gnn_bo", "L0_gnn_ln_g", "L0_gnn_ln_b", "L1_gnn_W_l",
            "L1_gnn_b_l", "L1_gnn_W_r", "L1_gnn_b_r", "L1_gnn_att", "L1_gnn_bias", "L2_gnn_W", "L2_gnn_att_src",
            "L2_gnn_att_dst", "L2_gnn_bias", "L2_gnn_gamma", "L2_gnn_beta", "L3_gnn_Wr0", "L3_gnn_br0", "L3_gnn_Ws0",
            "L3_gnn_Wr1", "L3_gnn_br1", "L3_gnn_Ws1"]


def kernel(**inputs):
    import numpy as np
    import concourse.bacc as bacc
    from concourse.bass_utils import run_bass_kernel_spmd

    def columns(a, tail):
        whole = np.concatenate([np.asarray(a).reshape(-1), tail])
        return np.ascontiguousarray(whole.reshape(T, P).T)

    loops = np.full(EP - E, N, np.int32)
    loops[:N] = np.arange(N, dtype=np.int32)
    nothing = np.zeros(EP - E, np.float32)
    x = np.asarray(inputs["x"])
    arrays = {
        "x": np.concatenate([x, np.zeros((NP - N, D), x.dtype)]),
        "src": columns(inputs["src"], loops),
        "dst": columns(inputs["dst"], loops),
        "length": columns(inputs["edge_weight1"], nothing),
        "weight": columns(inputs["edge_weight"], nothing),
        "real": columns(np.ones(E, np.float32), nothing),
    }
    for name in _WEIGHTS:
        arrays[name] = np.ascontiguousarray(inputs[name])
    nc = bacc.Bacc("TRN2", target_bir_lowering=False, num_devices=1)
    aps = {}
    for name, a in arrays.items():
        aps[name] = nc.dram_tensor(f"in_{name}", a.shape, mybir.dt.from_np(a.dtype), kind="ExternalInput").ap()
    out = nc.dram_tensor("out_nodes", [NP, D], F32, kind="ExternalOutput").ap()
    gnn_kernel(nc, out, aps["x"], aps["src"], aps["dst"], aps["length"], aps["weight"], aps["real"],
               {name: aps[name] for name in _WEIGHTS})
    r = run_bass_kernel_spmd(nc, [{f"in_{name}": a for name, a in arrays.items()}], core_ids=[0])
    return r.results[0]["out_nodes"][:N]
```

```python
from contextlib import ExitStack, contextmanager

import concourse.bass as bass
from concourse import mybir

P = 128
N = 6250
E = 106250
D = 128
NB = 50
NP = NB * P
G = 7
R = 126
W = G * P
T = R * G
EP = T * P
SLOTS = 3
CB = 5
NC = NB // CB
assert EP >= E + N and NP >= N + P and R % SLOTS == 0 and R % 2 == 0 and NC * CB == NB and NC % 2 == 0
H0, H1 = 8, 4
HB = 50
BIG = 1e30
LN_EPS = 1e-5
CUTOFF = 5.0

ALU = mybir.AluOpType
ACT = mybir.ActivationFunctionType
AX = mybir.AxisListType
F32 = mybir.dt.float32
BF16 = mybir.dt.bfloat16
I32 = mybir.dt.int32
U32 = mybir.dt.uint32


class Stage:

    def __init__(self, nc, name, stack):
        self.nc, self.name, self.stack, self.sems = nc, name, stack, []

    def sem(self, name):
        s = self.nc.alloc_semaphore(f"{self.name}_{name}")
        self.sems.append(s)
        return s

    def sb(self, name, shape, dt=F32):
        return self.stack.enter_context(self.nc.sbuf_tensor(f"{self.name}_{name}", shape, dt))

    def ps(self, name, shape, dt=F32):
        return self.stack.enter_context(self.nc.psum_tensor(f"{self.name}_ps_{name}", shape, dt))


@contextmanager
def stage(nc, name):
    with ExitStack() as stack:
        st = Stage(nc, name, stack)
        yield st
    nc.clear_and_free_semaphores(st.sems)
    nc.all_engine_barrier()


class Chain:

    def __init__(self, eng, sem):
        self.eng, self.sem, self.n = eng, sem, 0

    def __call__(self, ins):
        self.n += 1
        ins.then_inc(self.sem, 1)
        self.eng.wait_ge(self.sem, self.n)


def pipelined(eng, rounds, slots, prepare, finish):
    def steps(i, more):
        for s in range(slots):
            if s + 1 < slots:
                prepare(i, s + 1)
            elif more:
                prepare(i + 1, 0)
            finish(i, s)

    prepare(0, 0)
    with eng.Fori(0, rounds - 1) as i:
        steps(i, True)
    steps(rounds - 1, False)


def over_tiles(ap, inner):
    g = ap.shape[1]
    return ap.rearrange("p (g o) -> p g o", o=1).to_broadcast([ap.shape[0], g, inner])


def per_tile(ap, g=G):
    return ap.rearrange("p (o n) -> p o n", o=1).to_broadcast([ap.shape[0], g, ap.shape[1]])


def group(col, gi, width=1):
    return col[:, bass.ds(gi * (G * width), G * width)]


class Order:

    def __init__(self, nc, name, keep):
        self.name = name
        self.payload = nc.dram_tensor(f"payload_{name}", [EP, 4], F32).ap()
        self.base_dram = nc.dram_tensor(f"base_{name}", [1, R * 8], I32).ap()
        self.rel_rows = nc.dram_tensor(f"rel_rows_{name}", [R, 8, P], BF16).ap()
        sb = lambda n, s, dt=F32: keep.enter_context(nc.sbuf_tensor(f"{name}_{n}", s, dt))
        self.other = sb("other", [P, T + SLOTS * G], I32)
        self.rel = sb("rel", [P, T])
        self.rel_bf = sb("rel_bf", [P, T], BF16)
        self.base = sb("base", [1, R * 8], I32)
        self.weight = sb("weight", [P, T])
        self.start = sb("start", [R, W])
        self.end = sb("end", [R, W])
        self.has_start = sb("has_start", [1, R])
        self.has_end = sb("has_end", [1, R])


def constants(nc, keep, orders):
    class C:
        pass
    c = C()
    sb = lambda n, s, dt=F32: keep.enter_context(nc.sbuf_tensor(f"const_{n}", s, dt))
    c.ident, c.ident_bf = sb("ident", [P, P]), sb("ident_bf", [P, P], BF16)
    c.lane, c.column = sb("lane", [P, 1]), sb("column", [P, P])
    c.before, c.after = sb("before", [P, P]), sb("after", [P, P])
    c.ones = sb("ones", [P, P])
    c.minus_pick = sb("minus_pick", [8, G, P], BF16)
    with stage(nc, "constants") as st:
        pick = st.sb("pick", [8, G, P])
        made, ones_ready, ident_ready, pick_ready, bf_ready = (
            st.sem(n) for n in ("made", "ones", "ident", "pick_ready", "bf"))
        with nc.Block() as block:
            @block.gpsimd
            def _(pool):
                pool.memset(c.ident[:], 0.0).then_inc(ident_ready, 1)
                pool.wait_ge(ident_ready, 1)
                pool.affine_select(out=c.ident[:], in_=c.ident[:], compare_op=ALU.not_equal, fill=1.0, base=0,
                                   pattern=[[-1, P]], channel_multiplier=1).then_inc(ident_ready, 1)
                pool.iota(c.lane[:], [[0, 1]], base=0, channel_multiplier=1,
                          allow_small_or_imprecise_dtypes=True).then_inc(made, 1)
                pool.iota(c.column[:], [[1, P]], base=0, channel_multiplier=0,
                          allow_small_or_imprecise_dtypes=True).then_inc(made, 1)
                pool.memset(c.ones[:], 1.0).then_inc(ones_ready, 1)
                pool.wait_ge(ones_ready, 1)
                pool.affine_select(out=c.before[:], in_=c.ones[:], compare_op=ALU.is_ge, fill=0.0, base=-1,
                                   pattern=[[-1, P]], channel_multiplier=1).then_inc(made, 1)
                pool.affine_select(out=c.after[:], in_=c.ones[:], compare_op=ALU.is_ge, fill=0.0, base=-1,
                                   pattern=[[1, P]], channel_multiplier=-1).then_inc(made, 1)
                pool.iota(pick[:], [[0, G], [1, P]], base=0, channel_multiplier=0,
                          allow_small_or_imprecise_dtypes=True).then_inc(pick_ready, 1)
                pool.wait_ge(pick_ready, 1)
                pool.affine_select(out=pick[:], in_=pick[:], compare_op=ALU.is_ge, fill=0.0, base=-7,
                                   pattern=[[0, G], [0, P]], channel_multiplier=1).then_inc(pick_ready, 1)
                pool.wait_ge(pick_ready, 2)
                pool.affine_select(out=pick[:], in_=pick[:], compare_op=ALU.not_equal, fill=-1.0, base=0,
                                   pattern=[[-1, G], [0, P]], channel_multiplier=1).then_inc(pick_ready, 1)
                pool.wait_ge(made, 4)

            @block.vector
            def _(dve):
                dve.wait_ge(ident_ready, 2)
                dve.wait_ge(made, 4)
                dve.tensor_copy(c.ident_bf[:], c.ident[:]).then_inc(bf_ready, 1)
                dve.wait_ge(pick_ready, 3)
                dve.tensor_copy(c.minus_pick[:], pick[:]).then_inc(bf_ready, 1)
                for o in orders:
                    dve.memset(o.other[:, T:], 0).then_inc(bf_ready, 1)
                dve.wait_ge(bf_ready, 2 + len(orders))
    return c


def sort_edges(nc, c, o, key_d, other_d, weight_d, real_d, counts, counted_before, count_next=None):
    with stage(nc, f"load_{o.name}") as st:
        key, other = st.sb("key", [P, T], I32), st.sb("other", [P, T], I32)
        weight, real = st.sb("weight", [P, T]), st.sb("real", [P, T])
        bits = st.sb("bits", [P, T], I32)
        lo_bf, hi, hi_bf = (st.sb(n, [P, T], BF16) for n in ("lo_bf", "hi", "hi_bf"))
        pay = st.sb("pay", [P, T, 4])
        totals = st.sb("totals", [P, HB])
        if count_next is not None:
            next_lo, next_hi = st.sb("next_lo", [P, T], BF16), st.sb("next_hi", [P, T], BF16)
        upto, first = st.sb("upto", [P, HB]), st.sb("first", [P, HB])
        one_lo, one_hi = st.sb("one_lo", [P, 2, P, G], BF16), st.sb("one_hi", [P, 2, HB, G], BF16)
        column_g = st.sb("column_g", [P, P, G], BF16)
        zero = st.sb("zero", [P, P], BF16)
        ps_counts, ps_sums = st.ps("counts", [P, 512]), st.ps("sums", [P, 512])
        loaded, steps, paid, split = (st.sem(n) for n in ("loaded", "steps", "paid", "split"))
        cleared, hot_ready, hot_used, counted, copied, summed = (
            st.sem(n) for n in ("cleared", "hot_ready", "hot_used", "counted", "copied", "summed"))

        with nc.Block() as block:
            @block.sync
            def _(sp):
                for buf, src in ((key, key_d), (other, other_d), (weight, weight_d), (real, real_d)):
                    sp.dma_start(buf[:], src).then_inc(loaded, 16)
                sp.wait_ge(loaded, 64)

            @block.scalar
            def _(act):
                act.wait_ge(loaded, 64)
                for f, buf in enumerate((key, other, weight, real)):
                    act.copy(pay[:, :, f], buf[:]).then_inc(paid, 1)
                act.wait_ge(paid, 4)
                if not counted_before:
                    act.wait_ge(counted, 1)
                    act.copy(counts[:], ps_counts[:, 0:HB]).then_inc(copied, 1)
                    act.wait_ge(copied, 1)

            @block.vector
            def _(dve):
                link = Chain(dve, steps)
                dve.memset(zero[:], 0.0).then_inc(cleared, 1)
                link(dve.tensor_copy(column_g[:], over_tiles(c.column[:], G)))
                dve.wait_ge(loaded, 64)
                link(dve.tensor_single_scalar(bits[:], key[:], P - 1, ALU.bitwise_and))
                link(dve.tensor_copy(lo_bf[:], bits[:]))
                link(dve.tensor_single_scalar(bits[:], key[:], 7, ALU.arith_shift_right))
                link(dve.tensor_copy(hi[:], bits[:]))
                link(dve.tensor_scalar(hi_bf[:], hi[:], float(P), None, ALU.mult))
                dve.wait_ge(paid, 4)
                if count_next is not None:
                    link(dve.tensor_single_scalar(bits[:], other[:], P - 1, ALU.bitwise_and))
                    link(dve.tensor_copy(next_lo[:], bits[:]))
                    link(dve.tensor_single_scalar(bits[:], other[:], 7, ALU.arith_shift_right))
                    link(dve.tensor_copy(next_hi[:], bits[:]))
                if not counted_before:
                    dve.sem_inc(hot_used, 2)
                    with dve.Fori(0, R // 2) as i:
                        for s in range(2):
                            gi = 2 * i + s
                            dve.wait_ge(hot_used, gi + 1)
                            dve.tensor_tensor(one_lo[:, s], column_g[:], per_tile(group(lo_bf, gi), P),
                                      ALU.is_equal).then_inc(hot_ready, 1)
                            dve.tensor_tensor(one_hi[:, s], column_g[:, 0:HB], per_tile(group(hi, gi), HB),
                                      ALU.is_equal).then_inc(hot_ready, 1)
                    dve.wait_ge(hot_ready, 2 * R)
                dve.wait_ge(summed, 1)
                link(dve.tensor_copy(totals[:], ps_sums[:, 64:64 + HB]))
                link(dve.tensor_tensor_scan(upto[:], c.ones[:, 0:HB], totals[:], 0.0, ALU.mult, ALU.add))
                link(dve.tensor_tensor(upto[:], upto[:], totals[:], ALU.subtract))
                link(dve.tensor_tensor(first[:], upto[:], ps_sums[:, 0:HB], ALU.add))

            @block.tensor
            def _(pe):
                pe.wait_ge(cleared, 1)
                pe.matmul(ps_counts[:, 0:HB], zero[:], zero[:, 0:HB], start=True, stop=True, skip_group_check=True)
                if not counted_before:
                    with pe.Fori(0, R // 2) as i:
                        for s in range(2):
                            gi = 2 * i + s
                            pe.wait_ge(hot_ready, 2 * gi + 2)
                            for j in range(G):
                                mm = pe.matmul(ps_counts[:, 0:HB], one_lo[:, s, :, j], one_hi[:, s, :, j],
                                               start=False, stop=True, skip_group_check=True)
                            mm.then_inc(hot_used, 1)
                    pe.matmul(ps_sums[:, 448:450], zero[:], zero[:, 0:2], start=True, stop=True).then_inc(counted, 1)
                    pe.wait_ge(copied, 1)
                pe.matmul(ps_sums[:, 0:HB], c.after[:], counts[:], start=True, stop=True)
                pe.matmul(ps_sums[:, 64:64 + HB], c.ones[:], counts[:], start=True, stop=True).then_inc(summed, 1)

        one_lo_t = st.sb("one_lo_t", [P, 2, G, P])
        same, rank, at = st.sb("same", [P, G, P]), st.sb("rank", [P, 2, G]), st.sb("at", [P, 2, G])
        picked = st.sb("picked", [P, G, HB])
        at_i = st.sb("at_i", [P, 2, G], I32)
        pay_slot = st.sb("pay_slot", [P, 2, G, 4])
        running = st.sb("running", [P, 2, HB])
        ps_lo, ps_key = st.ps("lo", [P, 8, P]), st.ps("key", [P, 8, P])
        ps_run, ps_look = st.ps("run", [P, 512]), st.ps("look", [P, G, 64])
        (spread, keys_read, lo_t_ready, ran, snapped, looked, picked_s, look_read, ranked, placed, staged, slot_free,
         pool_go, at_ready) = (
            st.sem(n) for n in ("spread", "keys_read", "lo_t", "ran", "snapped", "looked", "picked", "look_read",
                                "ranked", "placed", "staged", "slot_free", "pool_go", "at_ready"))
        hot2_ready = st.sem("hot2_ready")
        scattered = [st.sem(f"scattered{s}") for s in range(2)]
        if count_next is not None:
            next_one_lo, next_one_hi = st.sb("next_one_lo", [P, 2, P, G], BF16), st.sb("next_one_hi", [P, 2, HB, G], BF16)
            next_ready, next_copied = st.sem("next_ready"), st.sem("next_copied")

        with nc.Block() as block:
            @block.tensor
            def _(pe):
                def spread_keys(i, s):
                    gi = 2 * i + s
                    pe.wait_ge(keys_read, gi + 1)
                    for j in range(G):
                        col = bass.ds(gi * G + j, 1)
                        a = lo_bf[:, col].to_broadcast([P, P])
                        b = hi_bf[:, col].to_broadcast([P, P])
                        pe.matmul(ps_lo[:, j, :], a, c.ident_bf[:], start=True, stop=True)
                        pe.matmul(ps_key[:, j, :], a, c.ident_bf[:], start=True, stop=False)
                        mm = pe.matmul(ps_key[:, j, :], b, c.ident_bf[:], start=False, stop=True)
                    mm.then_inc(spread, 1)

                def look_up(i, s):
                    gi = 2 * i + s
                    pe.wait_ge(lo_t_ready, gi + 1)
                    pe.wait_ge(hot2_ready, 2 * gi + 2)
                    pe.wait_ge(look_read, gi + 1)
                    for j in range(G):
                        k = (s * G + j) % 2
                        pe.wait_ge(snapped, gi * G + (j + 1))
                        pe.matmul(ps_run[:, 0:HB], one_lo[:, s, :, j], one_hi[:, s, :, j], start=False, stop=True,
                                  skip_group_check=True).then_inc(ran, 1)
                        if count_next is not None:
                            if j == 0:
                                pe.wait_ge(next_ready, 2 * gi + 2)
                            pe.matmul(ps_counts[:, 0:HB], next_one_lo[:, s, :, j], next_one_hi[:, s, :, j], start=False,
                                      stop=True, skip_group_check=True)
                        pe.matmul(ps_look[:, j, 0:HB], one_lo_t[:, s, j, :], running[:, k, :],
                                  start=True, stop=True).then_inc(looked, 1)

                if count_next is not None:
                    pe.matmul(ps_counts[:, 0:HB], zero[:], zero[:, 0:HB], start=True, stop=True, skip_group_check=True)
                pe.matmul(ps_run[:, 0:HB], c.ident[:], first[:], start=True, stop=True,
                          skip_group_check=True).then_inc(ran, 1)
                pipelined(pe, R // 2, 2, spread_keys, look_up)

            @block.scalar
            def _(act):
                with act.Fori(0, R // 2) as i:
                    for s in range(2):
                        gi = 2 * i + s
                        act.wait_ge(slot_free, gi + 1)
                        act.copy(pay_slot[:, s].rearrange("p g f -> p (g f)"),
                                 group(pay[:].rearrange("p t f -> p (t f)"), gi, 4)).then_inc(staged, 1)
                        for j in range(G):
                            k = (s * G + j) % 2
                            act.wait_ge(ran, gi * G + (j + 1))
                            act.copy(running[:, k, :], ps_run[:, 0:HB]).then_inc(snapped, 1)

            @block.vector
            def _(dve):
                def compare(i, s):
                    gi = 2 * i + s
                    dve.tensor_tensor(one_lo[:, s], column_g[:], per_tile(group(lo_bf, gi), P),
                                      ALU.is_equal).then_inc(hot2_ready, 1)
                    dve.tensor_tensor(one_hi[:, s], column_g[:, 0:HB], per_tile(group(hi, gi), HB),
                                      ALU.is_equal).then_inc(hot2_ready, 1)
                    if count_next is not None:
                        dve.tensor_tensor(next_one_lo[:, s], column_g[:], per_tile(group(next_lo, gi), P),
                                      ALU.is_equal).then_inc(next_ready, 1)
                        dve.tensor_tensor(next_one_hi[:, s], column_g[:, 0:HB], per_tile(group(next_hi, gi), HB),
                                      ALU.is_equal).then_inc(next_ready, 1)
                    dve.wait_ge(spread, gi + 1)
                    dve.tensor_scalar(one_lo_t[:, s], ps_lo[:, 0:G, :], c.lane[:, 0:1], None,
                                      ALU.is_equal).then_inc(lo_t_ready, 1)
                    for j in range(G):
                        dve.scalar_tensor_tensor(same[:, j, :], ps_key[:, j, :], pay[:, bass.ds(gi * G + j, 1), 0],
                                                 c.before[:], ALU.is_equal, ALU.mult,
                                                 accum_out=rank[:, s, j:j + 1]).then_inc(ranked, 1)
                    dve.wait_ge(ranked, gi * G + G)
                    dve.sem_inc(keys_read, 1)

                def place(i, s):
                    gi = 2 * i + s
                    dve.wait_ge(looked, gi * G + G)
                    dve.tensor_tensor(picked[:], one_hi[:, s].rearrange("p h g -> p g h"), ps_look[:, :, 0:HB],
                                      ALU.mult).then_inc(look_read, 1)
                    dve.wait_ge(look_read, gi + 2)
                    dve.tensor_reduce(at[:, s], picked[:], AX.X, ALU.add).then_inc(picked_s, 1)
                    dve.wait_ge(picked_s, gi + 1)
                    dve.wait_ge(slot_free, gi + 1)
                    dve.tensor_tensor(at_i[:, s], at[:, s], rank[:, s], ALU.add).then_inc(at_ready, 1)
                    dve.wait_ge(at_ready, gi + 1)

                dve.sem_inc(keys_read, 1)
                dve.sem_inc(look_read, 1)
                pipelined(dve, R // 2, 2, compare, place)
                if count_next is not None:
                    dve.tensor_copy(count_next[:], ps_counts[:, 0:HB]).then_inc(next_copied, 1)
                    dve.wait_ge(next_copied, 1)

            @block.gpsimd
            def _(pool):
                with pool.Fori(0, R // 2) as i:
                    for s in range(2):
                        gi = 2 * i + s
                        pool.wait_ge(staged, gi + 1)
                        pool.wait_ge(at_ready, gi + 1)
                        pool.sem_inc(pool_go, 1)
                        for j in range(G):
                            pool.indirect_dma_start(
                                o.payload, bass.IndirectOffsetOnAxis(ap=at_i[:, s, j:j + 1].bitcast(U32), axis=0),
                                pay_slot[:, s, j, :], None).then_inc(scattered[s], 16)

            @block.sync
            def _(sp):
                sp.sem_inc(slot_free, 2)
                with sp.Fori(0, R // 2) as i:
                    for s in range(2):
                        sp.wait_ge(scattered[s], 16 * G * (i + 1))
                        sp.sem_inc(slot_free, 1)

    with stage(nc, f"rows_{o.name}") as st:
        rows = st.sb("rows", [R, W, 4])
        key, rel = st.sb("key", [R, W]), st.sb("rel", [R, W])
        last_key, next_key = st.sb("last_key", [P, 1]), st.sb("next_key", [P, 1])
        base_i = st.sb("base_i", [R, 8], I32)
        flag = st.sb("flag", [R, 2])
        rel_ones = st.sb("rel_ones", [R, 8, P], BF16)
        loaded, steps, based, based2, turned = (st.sem(n) for n in ("loaded", "steps", "based", "based2", "turned"))
        edge_keys = o.payload.rearrange("(r w) f -> r w f", w=W)
        ps_flag = st.ps("flag", [P, 2, P])
        with nc.Block() as block:
            @block.sync
            def _(sp):
                sp.dma_start(rows[:].rearrange("r w f -> r (w f)"),
                             o.payload.rearrange("(r w) f -> r (w f)", w=W)).then_inc(loaded, 16)
                sp.wait_ge(steps, 2)
                with nc.allow_non_contiguous_dma(reason="one key per row"):
                    sp.dma_start(last_key[1:R, :], edge_keys[0:R - 1, W - 1, 0:1]).then_inc(loaded, 16)
                    sp.dma_start(next_key[0:R - 1, :], edge_keys[1:R, 0, 0:1]).then_inc(loaded, 16)
                sp.wait_ge(based, 1)
                sp.dma_start(o.base_dram.rearrange("o (r g) -> (o r) g", g=8), base_i[:]).then_inc(based2, 16)
                sp.wait_ge(based2, 16)
                sp.dma_start(o.base[:], o.base_dram).then_inc(based2, 16)
                sp.wait_ge(based2, 32)
                sp.wait_ge(steps, 8)
                sp.dma_start(o.rel_rows.rearrange("r g e -> r (g e)"),
                             rel_ones[:].rearrange("r g e -> r (g e)")).then_inc(based2, 16)
                sp.wait_ge(based2, 48)

            @block.vector
            def _(dve):
                link = Chain(dve, steps)
                link(dve.memset(last_key[:], -1.0))
                link(dve.memset(next_key[:], -1.0))
                link(dve.memset(base_i[:], 0))
                link(dve.memset(rel_ones[:], 1.0))
                dve.wait_ge(loaded, 48)
                link(dve.tensor_copy(key[:], rows[:, :, 0]))
                firsts = key[:].rearrange("r (g e) -> r g e", e=P)[:, :, 0]
                link(dve.tensor_copy(base_i[:, 0:G], firsts))
                dve.sem_inc(based, 1)
                link(dve.tensor_tensor(rel[:].rearrange("r (g e) -> r g e", e=P),
                                       key[:].rearrange("r (g e) -> r g e", e=P), over_tiles(firsts, P), ALU.subtract))
                link(dve.tensor_copy(rel_ones[:, 0:G, :], rel[:].rearrange("r (g e) -> r g e", e=P)))
                link(dve.tensor_tensor(o.start[:, 1:W], key[:, 1:W], key[:, 0:W - 1], ALU.not_equal))
                link(dve.tensor_tensor(o.start[:, 0:1], key[:, 0:1], last_key[0:R, :], ALU.not_equal))
                link(dve.tensor_tensor(o.end[:, 0:W - 1], key[:, 1:W], key[:, 0:W - 1], ALU.not_equal))
                link(dve.tensor_tensor(o.end[:, W - 1:W], key[:, W - 1:W], next_key[0:R, :], ALU.not_equal))
                link(dve.tensor_reduce(flag[:, 0:1], o.start[:], AX.X, ALU.max))
                link(dve.tensor_reduce(flag[:, 1:2], o.end[:], AX.X, ALU.max))
                dve.wait_ge(turned, 1)
                link(dve.tensor_copy(o.has_start[:], ps_flag[0:1, 0, 0:R]))
                link(dve.tensor_copy(o.has_end[:], ps_flag[0:1, 1, 0:R]))

            @block.tensor
            def _(pe):
                pe.wait_ge(steps, 14)
                pe.transpose(ps_flag[0:1, 0, 0:R], flag[:, 0:1], c.ident[0:R, 0:R])
                pe.transpose(ps_flag[0:1, 1, 0:R], flag[:, 1:2], c.ident[0:R, 0:R]).then_inc(turned, 1)

        rows_to_columns(nc, c, f"turn_{o.name}", [
            (rows[:, :, 1], [o.other[:, 0:T]]), (rel[:], [o.rel[:], o.rel_bf[:]]), (rows[:, :, 2], [o.weight[:]])])
        if o.real is not None:
            with stage(nc, f"real_{o.name}") as st2:
                done = st2.sem("done")
                with nc.Block() as block:
                    @block.vector
                    def _(dve):
                        dve.tensor_copy(o.real[:], rows[:, :, 3]).then_inc(done, 1)
                        dve.tensor_copy(o.length[:], rows[:, :, 2]).then_inc(done, 1)
                        dve.wait_ge(done, 2)


def rows_to_columns(nc, c, name, pairs):
    with stage(nc, name) as st:
        ps = st.ps("turn", [P, 2, 8, P])
        turned, copied = st.sem("turned"), st.sem("copied")
        with nc.Block() as block:
            @block.tensor
            def _(pe):
                done = 0
                for n, (row, cols) in enumerate(pairs):
                    if n >= 2:
                        pe.wait_ge(copied, sum(len(x) for _, x in pairs[:n - 1]))
                    for g in range(G):
                        mm = pe.transpose(ps[:, n % 2, g, 0:R], row[:, g * P:(g + 1) * P], c.ident[0:R, 0:R])
                    mm.then_inc(turned, 1)

            @block.scalar
            def _(act):
                for n, (row, cols) in enumerate(pairs):
                    act.wait_ge(turned, n + 1)
                    for col in cols:
                        act.copy(col.rearrange("p (r g) -> p g r", g=G),
                                 ps[:, n % 2, 0:G, 0:R]).then_inc(copied, 1)
                act.wait_ge(copied, sum(len(x) for _, x in pairs))


def load_weights(nc, name, loads):
    with stage(nc, name) as st:
        loaded = st.sem("loaded")
        with nc.Block() as block:
            @block.sync
            def _(sp):
                with nc.allow_non_contiguous_dma(reason="vectors across partitions, once"):
                    for dst, src in loads:
                        sp.dma_start(dst, src).then_inc(loaded, 16)
                sp.wait_ge(loaded, 16 * len(loads))


def spread_row(vec, n):
    return vec.rearrange("(o n) -> o n", o=1).to_broadcast([P, n])


def transpose_weights(nc, c, name, pairs):
    with stage(nc, name) as st:
        ps = st.ps("turn", [P, len(pairs), 512])
        turned, copied = st.sem("turned"), st.sem("copied")
        with nc.Block() as block:
            @block.tensor
            def _(pe):
                for n, (dst, src) in enumerate(pairs):
                    k, m = src.shape
                    pe.transpose(ps[0:m, n, 0:k], src, c.ident[0:k, 0:k]).then_inc(turned, 1)

            @block.vector
            def _(dve):
                for n, (dst, src) in enumerate(pairs):
                    k, m = src.shape
                    dve.wait_ge(turned, n + 1)
                    dve.tensor_copy(dst, ps[0:m, n, 0:k]).then_inc(copied, 1)
                dve.wait_ge(copied, len(pairs))


def node_tables(nc, c, name, x, weight, bias, out_w, tables, dots=None):
    with stage(nc, name) as st:
        xs, xt, y = st.sb("xs", [P, 2, CB, D]), st.sb("xt", [P, 2, CB, D]), st.sb("y", [P, 2, CB, out_w])
        prod, dot = st.sb("prod", [P, CB, D]), st.sb("dot", [P, 2, CB])
        ps_t, ps_y = st.ps("t", [P, 8, P]), st.ps("y", [P, CB, 512])
        xs_ready, turned, xt_ready, multiplied, y_ready, dot_ready, slot_free = (
            st.sem(n) for n in ("xs_ready", "turned", "xt_ready", "multiplied", "y_ready", "dot_ready", "slot_free"))
        stored = [st.sem(f"stored{s}") for s in range(2)]
        n_st = len(tables) + (dots is not None)
        with nc.Block() as block:
            @block.scalar
            def _(act):
                with act.Fori(0, NC // 2) as i:
                    for s in range(2):
                        n = 2 * i + s
                        act.wait_ge(multiplied, n + 1)
                        act.copy(xs[:, s], x[:, bass.ds(n * CB, CB), :]).then_inc(xs_ready, 1)
                        act.wait_ge(turned, n + 1)
                        act.copy(xt[:, s], ps_t[:, 0:CB, :]).then_inc(xt_ready, 1)

            @block.tensor
            def _(pe):
                pe.sem_inc(multiplied, 2)
                with pe.Fori(0, NC // 2) as i:
                    for s in range(2):
                        n = 2 * i + s
                        pe.wait_ge(xs_ready, n + 1)
                        for q in range(CB):
                            mm = pe.transpose(ps_t[:, q, :], xs[:, s, q, :], c.ident[:])
                        mm.then_inc(turned, 1)
                        pe.wait_ge(xt_ready, n + 1)
                        pe.wait_ge(y_ready, n + 1)
                        for q in range(CB):
                            mm = pe.matmul(ps_y[:, q, 0:out_w], xt[:, s, q, :], weight, start=True, stop=True)
                        mm.then_inc(multiplied, 1)

            @block.vector
            def _(dve):
                dve.sem_inc(y_ready, 1)
                with dve.Fori(0, NC // 2) as i:
                    for s in range(2):
                        n = 2 * i + s
                        dve.wait_ge(multiplied, n + 3)
                        dve.wait_ge(slot_free, n + 1)
                        if bias is None:
                            dve.tensor_copy(y[:, s], ps_y[:, :, 0:out_w]).then_inc(y_ready, 1)
                        else:
                            dve.tensor_tensor(y[:, s], ps_y[:, :, 0:out_w], per_tile(bias, CB), ALU.add).then_inc(y_ready, 1)
                        if dots is not None:
                            dve.wait_ge(y_ready, n + 2)
                            dve.tensor_tensor(prod[:], y[:, s, :, 0:D], per_tile(dots[0], CB),
                                              ALU.mult).then_inc(dot_ready, 1)
                            dve.wait_ge(dot_ready, 2 * n + 1)
                            dve.tensor_reduce(dot[:, s], prod[:], AX.X, ALU.add).then_inc(dot_ready, 1)

            @block.sync
            def _(sp):
                sp.sem_inc(slot_free, 2)
                with sp.Fori(0, NC // 2) as i:
                    for s in range(2):
                        n = 2 * i + s
                        sp.wait_ge(y_ready, n + 2)
                        if dots is not None:
                            sp.wait_ge(dot_ready, 2 * n + 2)
                        for table, c0, w in tables:
                            sp.dma_start(table[bass.ds(n * (CB * P), CB * P), :].rearrange("(q p) d -> p q d", p=P),
                                         y[:, s, :, c0:c0 + w]).then_inc(stored[s], 16)
                        if dots is not None:
                            with nc.allow_non_contiguous_dma(reason="one value per node"):
                                sp.dma_start(dots[1][bass.ds(n * (CB * P), CB * P), :].rearrange("(q p) o -> p (q o)", p=P),
                                             dot[:, s]).then_inc(stored[s], 16)
                    for s in range(2):
                        sp.wait_ge(stored[s], (16 * n_st) * (i + 1))
                        sp.sem_inc(slot_free, 1)


def edge_scores(nc, c, o, name, table, table_w, window, window_w, spill, spill_at, scores, heads, mode, k):
    with stage(nc, name) as st:
        idx = st.sb("idx", [P, SLOTS, G], I32)
        rel = st.sb("rel", [P, SLOTS, G], BF16)
        rows = st.sb("rows", [P, SLOTS, G, table_w])
        win = st.sb("win", [P, SLOTS, G, window_w])
        hot_t = st.sb("hot_t", [P, SLOTS, G, P])
        prod, act_m = st.sb("prod", [P, G, D]), st.sb("act_m", [P, G, D])
        red = st.sb("red", [P, G * heads])
        ps_rel, ps_x = st.ps("rel", [P, 8, P]), st.ps("x", [P, 8, P])
        (idx_staged, rel_staged, spread, hot_ready, expanded, consumed, reduced, scored, spill_done, pool_go, multiplied,
         leaked) = (
            st.sem(n) for n in ("idx_staged", "rel_staged", "spread", "hot_ready", "expanded", "consumed", "reduced",
                                "scored", "spill_done", "pool_go", "multiplied", "leaked"))
        gathered, win_loaded, spilled = ([st.sem(f"{n}{s}") for s in range(SLOTS)]
                                         for n in ("gathered", "win_loaded", "spilled"))
        bias_mode = mode == "dot"
        if bias_mode:
            length = st.sb("length", [P, SLOTS, G])
            hidden, warm = st.sb("hidden", [P, G, P]), st.sb("warm", [P, 1])
            warmed = st.sem("warmed")
            ps_len, ps_bias = st.ps("len", [P, 8, P]), st.ps("bias", [P, G, H0])
            len_staged, len_spread, hid_ready, biased = (
                st.sem(n) for n in ("len_staged", "len_spread", "hid_ready", "biased"))
        with nc.Block() as block:
            @block.scalar
            def _(act):
                def columns_and_windows(i, s):
                    gi = SLOTS * i + s
                    act.wait_ge(consumed, gi + 1)
                    act.copy(rel[:, s], group(o.rel_bf, gi)).then_inc(rel_staged, 1)
                    if bias_mode:
                        act.copy(length[:, s], group(o.weight, gi)).then_inc(len_staged, 1)
                    _, base = nc.values_load_multi_w_load_instructions(
                        o.base[0:1, bass.ds(gi * 8, 8)], engines=[act.engine], min_val=0, max_val=N,
                        skip_runtime_bounds_check_because="keys are node numbers")
                    with nc.allow_non_contiguous_dma(reason="a row of one value per node"):
                        for j in range(G):
                            act.dma_start(win[:, s, j, :], window[bass.ds(base[j], P), :]).then_inc(win_loaded[s], 16)

                def hidden_layer(i, s):
                    gi = SLOTS * i + s
                    if bias_mode:
                        act.wait_ge(len_spread, gi + 1)
                        act.wait_ge(biased, gi + 1)
                        act.activation(hidden[:], ps_len[:, 0:G, :], ACT.Silu, bias=k["be1"],
                                       scale=k["we1"]).then_inc(hid_ready, 1)

                if bias_mode:
                    act.activation(warm[:], k["be1"], ACT.Silu).then_inc(warmed, 1)
                    act.wait_ge(warmed, 1)
                    act.sem_inc(hid_ready, 1)
                pipelined(act, R // SLOTS, SLOTS, columns_and_windows, hidden_layer)

            @block.gpsimd
            def _(pool):
                with pool.Fori(0, R // SLOTS) as i:
                    for s in range(SLOTS):
                        gi = SLOTS * i + s
                        pool.wait_ge(idx_staged, gi + 1)
                        pool.wait_ge(consumed, gi + 1)
                        pool.wait_ge(spill_done, gi + 1)
                        pool.sem_inc(pool_go, 1)
                        for j in range(G):
                            pool.indirect_dma_start(
                                rows[:, s, j, :], None, table,
                                bass.IndirectOffsetOnAxis(ap=idx[:, s, j:j + 1].bitcast(U32), axis=0)
                            ).then_inc(gathered[s], 16)

            @block.sync
            def _(sp):
                sp.sem_inc(spill_done, SLOTS)
                with sp.Fori(0, R // SLOTS) as i:
                    for s in range(SLOTS):
                        gi = SLOTS * i + s
                        sp.wait_ge(gathered[s], (16 * G) * (i + 1))
                        sp.dma_start(spill[bass.ds(gi * P, P), :].rearrange("p (g d) -> p g d", g=G),
                                     rows[:, s, :, spill_at:spill_at + D]).then_inc(spilled[s], 16)
                        if s > 0:
                            sp.wait_ge(spilled[s - 1], 16 * (i + 1))
                            sp.sem_inc(spill_done, 1)
                    sp.wait_ge(spilled[SLOTS - 1], 16 * (i + 1))
                    sp.sem_inc(spill_done, 1)

            @block.tensor
            def _(pe):
                def spread_columns(i, s):
                    gi = SLOTS * i + s
                    pe.wait_ge(rel_staged, gi + 1)
                    pe.wait_ge(hot_ready, gi + 1)
                    for j in range(G):
                        mm = pe.matmul(ps_rel[:, j, :], rel[:, s, j:j + 1].to_broadcast([P, P]), c.ident_bf[:],
                                       start=True, stop=True)
                    mm.then_inc(spread, 1)
                    if bias_mode:
                        pe.wait_ge(len_staged, gi + 1)
                        pe.wait_ge(hid_ready, gi + 1)
                        for j in range(G):
                            mm = pe.matmul(ps_len[:, j, :], length[:, s, j:j + 1].to_broadcast([P, P]), c.ident[:],
                                           start=True, stop=True)
                        mm.then_inc(len_spread, 1)

                def expand_windows(i, s):
                    gi = SLOTS * i + s
                    pe.wait_ge(hot_ready, gi + 2)
                    pe.wait_ge(win_loaded[s], (16 * G) * (i + 1))
                    pe.wait_ge(consumed, gi + SLOTS)
                    for j in range(G):
                        mm = pe.matmul(ps_x[:, j, 0:window_w], hot_t[:, s, j, :], win[:, s, j, :], start=True, stop=True)
                    mm.then_inc(expanded, 1)
                    if bias_mode:
                        pe.wait_ge(hid_ready, gi + 2)
                        pe.wait_ge(scored, gi + 1)
                        for j in range(G):
                            mm = pe.matmul(ps_bias[:, j, :], hidden[:, j, :], k["we2t"], start=True, stop=True)
                        mm.then_inc(biased, 1)

                if bias_mode:
                    pe.sem_inc(biased, 1)
                pipelined(pe, R // SLOTS, SLOTS, spread_columns, expand_windows)

            @block.vector
            def _(dve):
                def one_hot(i, s):
                    gi = SLOTS * i + s
                    dve.wait_ge(spread, gi + 1)
                    dve.tensor_scalar(hot_t[:, s], ps_rel[:, 0:G, :], c.lane[:, 0:1], None,
                                      ALU.is_equal).then_inc(hot_ready, 1)

                def score(i, s):
                    gi = SLOTS * i + s
                    dve.wait_ge(scored, gi + 1)
                    dve.wait_ge(expanded, gi + 1)
                    dve.wait_ge(gathered[s], (16 * G) * (i + 1))
                    dve.tensor_copy(idx[:, s], group(o.other, gi + SLOTS)).then_inc(idx_staged, 1)
                    out = scores[:, bass.ds(gi * (G * heads), G * heads)]
                    if mode == "dot":
                        dve.tensor_tensor(prod[:], ps_x[:, 0:G, :], rows[:, s, :, 0:D], ALU.mult).then_inc(consumed, 1)
                        dve.wait_ge(consumed, gi + (SLOTS + 1))
                        dve.tensor_reduce(red[:], prod[:].rearrange("p g (h d) -> p (g h) d", h=heads),
                                          AX.X, ALU.add).then_inc(reduced, 1)
                        dve.wait_ge(reduced, gi + 1)
                        dve.wait_ge(biased, gi + 2)
                        dve.scalar_tensor_tensor(out, red[:], 1.0 / (D // heads) ** 0.5,
                                                 ps_bias[:].rearrange("p g h -> p (g h)"),
                                                 ALU.mult, ALU.add).then_inc(scored, 1)
                    elif mode == "gat2":
                        dve.tensor_tensor(prod[:], ps_x[:, 0:G, :], rows[:, s], ALU.add).then_inc(consumed, 1)
                        dve.wait_ge(consumed, gi + (SLOTS + 1))
                        dve.scalar_tensor_tensor(act_m[:], prod[:], 0.2, prod[:], ALU.mult, ALU.max).then_inc(leaked, 1)
                        dve.wait_ge(leaked, gi + 1)
                        dve.tensor_tensor(prod[:], act_m[:], per_tile(k["att"]), ALU.mult).then_inc(multiplied, 1)
                        dve.wait_ge(multiplied, gi + 1)
                        dve.tensor_reduce(out, prod[:].rearrange("p g (h d) -> p (g h) d", h=heads),
                                          AX.X, ALU.add).then_inc(scored, 1)
                    else:
                        dve.tensor_tensor(prod[:], rows[:, s], per_tile(k["att"]), ALU.mult).then_inc(multiplied, 1)
                        dve.wait_ge(multiplied, gi + 1)
                        dve.tensor_reduce(red[:], prod[:], AX.X, ALU.add).then_inc(reduced, 1)
                        dve.wait_ge(reduced, gi + 1)
                        dve.tensor_tensor(act_m[:, 0, 0:G], ps_x[:, 0:G, 0], red[:], ALU.add).then_inc(consumed, 1)
                        dve.wait_ge(consumed, gi + (SLOTS + 1))
                        dve.scalar_tensor_tensor(out, act_m[:, 0, 0:G], 0.2, act_m[:, 0, 0:G],
                                                 ALU.mult, ALU.max).then_inc(scored, 1)

                for s in range(SLOTS):
                    dve.tensor_copy(idx[:, s], group(o.other, s)).then_inc(idx_staged, 1)
                dve.sem_inc(consumed, SLOTS)
                dve.sem_inc(hot_ready, 1)
                dve.sem_inc(scored, 1)
                pipelined(dve, R // SLOTS, SLOTS, one_hot, score)
                dve.wait_ge(scored, R + 1)


def weighted_sum(nc, c, o, name, acc, alpha, heads, spill=None, table=None):
    with stage(nc, name) as st:
        rows = st.sb("rows", [P, SLOTS, G, D])
        hot, msg = st.sb("hot", [P, SLOTS, G, P]), st.sb("msg", [P, SLOTS, G, D])
        idx = st.sb("idx", [P, SLOTS, G], I32)
        ps_sum = st.ps("sum", [P, SLOTS, 8, P])
        per_slot = lambda n: [st.sem(f"{n}{s}") for s in range(SLOTS)]
        loaded, ready, hot_ready, summed = (per_slot(n) for n in ("loaded", "ready", "hot_ready", "summed"))
        pool_go, joined = st.sem("pool_go"), st.sem("joined")
        parts = [acc, st.sb("odd", [P, NP])]
        added = [[st.sem(f"added{s}_{j}") for j in range(G)] for s in range(SLOTS)]
        last_of = [(G - 1) // 2 * 2, (G - 2) // 2 * 2 + 1]
        if spill is not None:
            ps_diff = st.ps("diff", [P, 8, P])
            rel_rows = st.sb("rel_rows", [8, SLOTS, P], BF16)
            differed, rel_loaded, squared = per_slot("differed"), per_slot("rel_loaded"), st.sem("squared")
        else:
            idx_staged = per_slot("idx_staged")

        def messages(eng, i, s):
            w = alpha[:, bass.ds((SLOTS * i + s) * (G * heads), G * heads)]
            eng.tensor_tensor(msg[:, s].rearrange("p g (h d) -> p (g h) d", h=heads),
                              rows[:, s].rearrange("p g (h d) -> p (g h) d", h=heads),
                              over_tiles(w, D // heads), ALU.mult).then_inc(ready[s], 1)

        with nc.Block() as block:
            if spill is not None:
                @block.sync
                def _(sp):
                    with sp.Fori(0, R // SLOTS) as i:
                        for s in range(SLOTS):
                            sp.wait_ge(differed[s], i + 1)
                            sp.dma_start(rel_rows[:, s, :], o.rel_rows[bass.ds(SLOTS * i + s, 1)]
                                         .rearrange("r g e -> (r g) e")).then_inc(rel_loaded[s], 16)
                            sp.wait_ge(ready[s], i + 1)
                            sp.dma_start(rows[:, s].rearrange("p g d -> p (g d)"),
                                         spill[bass.ds((SLOTS * i + s) * P, P), :]).then_inc(loaded[s], 16)

                @block.gpsimd
                def _(pool):
                    for s in range(SLOTS):
                        pool.sem_inc(ready[s], 1)
                    with pool.Fori(0, R // SLOTS) as i:
                        for s in range(SLOTS):
                            pool.wait_ge(summed[s], i + 1)
                            pool.wait_ge(loaded[s], 16 * (i + 1))
                            pool.sem_inc(pool_go, 1)
                            messages(pool, i, s)
                    for s in range(SLOTS):
                        pool.wait_ge(ready[s], R // SLOTS + 1)

                @block.scalar
                def _(act):
                    with act.Fori(0, R // SLOTS) as i:
                        for s in range(SLOTS):
                            gi = SLOTS * i + s
                            act.wait_ge(differed[s], i + 2)
                            act.wait_ge(summed[s], i + 1)
                            act.activation(hot[:, s], ps_diff[:, 0:G, :], ACT.Square).then_inc(squared, 1)
                            act.wait_ge(squared, gi + 2)
                            act.activation(hot[:, s], hot[:, s], ACT.Relu, bias=c.ones[:, 0:1],
                                           scale=-1.0).then_inc(hot_ready[s], 1)
            else:
                @block.scalar
                def _(act):
                    with act.Fori(0, R // SLOTS) as i:
                        for s in range(SLOTS):
                            act.wait_ge(ready[s], i + 1)
                            act.copy(idx[:, s], group(o.other, SLOTS * i + s)).then_inc(idx_staged[s], 1)

                @block.gpsimd
                def _(pool):
                    with pool.Fori(0, R // SLOTS) as i:
                        for s in range(SLOTS):
                            pool.wait_ge(idx_staged[s], i + 1)
                            pool.sem_inc(pool_go, 1)
                            for j in range(G):
                                pool.indirect_dma_start(
                                    rows[:, s, j, :], None, table,
                                    bass.IndirectOffsetOnAxis(ap=idx[:, s, j:j + 1].bitcast(U32), axis=0)
                                ).then_inc(loaded[s], 16)

            @block.vector
            def _(dve):
                def gathered_messages(i, s):
                    dve.tensor_tensor(hot[:, s], per_tile(c.column[:]), over_tiles(group(o.rel, SLOTS * i + s), P),
                                      ALU.is_equal).then_inc(hot_ready[s], 1)
                    dve.wait_ge(loaded[s], (16 * G) * (i + 1))
                    messages(dve, i, s)

                def add(i, s):
                    _, base = nc.values_load_multi_w_load_instructions(
                        o.base[0:1, bass.ds((SLOTS * i + s) * 8, 8)], engines=[dve.engine], min_val=0, max_val=N,
                        skip_runtime_bounds_check_because="keys are node numbers")
                    dve.wait_ge(summed[s], i + 2)
                    for j in range(G):
                        at = parts[j % 2][:, bass.ds(base[j], P)]
                        if j >= 2:
                            dve.wait_ge(added[s][j - 2], i + (2 if j - 2 in last_of else 1))
                        else:
                            dve.wait_ge(added[s - 1][last_of[j]], i + (2 if s else 1))
                        dve.tensor_tensor(at, at, ps_sum[:, s, j, :], ALU.add).then_inc(added[s][j], 1)

                for part, last in zip(parts, last_of):
                    dve.memset(part[:], 0.0).then_inc(added[SLOTS - 1][last], 1)
                    for s in range(SLOTS - 1):
                        dve.sem_inc(added[s][last], 1)
                if spill is None:
                    for s in range(SLOTS):
                        dve.sem_inc(ready[s], 1)
                    pipelined(dve, R // SLOTS, SLOTS, gathered_messages, add)
                else:
                    with dve.Fori(0, R // SLOTS) as i:
                        for s in range(SLOTS):
                            add(i, s)
                for last in last_of:
                    dve.wait_ge(added[SLOTS - 1][last], R // SLOTS + 1)
                dve.tensor_tensor(acc[:], acc[:], parts[1][:], ALU.add).then_inc(joined, 1)
                dve.wait_ge(joined, 1)

            @block.tensor
            def _(pe):
                def differences(i, s):
                    gi = SLOTS * i + s
                    pe.wait_ge(rel_loaded[s], 16 * (i + 1))
                    pe.wait_ge(squared, gi + 1)
                    for g0, g1 in ((0, 4), (4, G)):
                        mm = pe.matmul(ps_diff[:, g0:g1, :], rel_rows[:, s, :], c.minus_pick[:, g0:g1, :],
                                       start=True, stop=True)
                    mm.then_inc(differed[s], 1)

                def sums(i, s):
                    pe.wait_ge(hot_ready[s], i + 1)
                    pe.wait_ge(ready[s], i + 2)
                    for last in last_of:
                        pe.wait_ge(added[s][last], i + 1)
                    for j in range(G):
                        mm = pe.matmul(ps_sum[:, s, j, :], msg[:, s, j, :], hot[:, s, j, :], start=True, stop=True)
                    mm.then_inc(summed[s], 1)

                for s in range(SLOTS):
                    pe.sem_inc(summed[s], 1)
                if spill is None:
                    with pe.Fori(0, R // SLOTS) as i:
                        for s in range(SLOTS):
                            sums(i, s)
                else:
                    for s in range(SLOTS):
                        pe.sem_inc(differed[s], 1)
                    pe.sem_inc(squared, 1)
                    pipelined(pe, R // SLOTS, SLOTS, differences, sums)


def segment_softmax(nc, c, o, name, scores, heads, first):
    with stage(nc, name) as st:
        e, f, g = st.sb("e", [R, heads, W]), st.sb("f", [R, W]), st.sb("g", [R, W])
        keep, keep_end, neg = st.sb("keep", [R, W]), st.sb("keep_end", [R, W]), st.sb("neg", [R, W])
        r_keep, r_keep_end, r_neg = st.sb("r_keep", [1, R]), st.sb("r_keep_end", [1, R]), st.sb("r_neg", [1, R])
        last, carry = st.sb("last", [R, 1]), st.sb("carry", [R, 1])
        chain_row = st.sb("chain_row", [1, R + 1])
        col_max, max_row, neg_max = st.sb("col_max", [R, H0]), st.sb("max_row", [1, H0]), st.sb("neg_max", [R, H0])
        ps_row, ps_col, ps_turn = st.ps("row", [P, 512]), st.ps("col", [P, 512]), st.ps("turn", [P, 2, 8, P])
        (steps, turned, copied, last_ready, row_turned, row_ready, col_turned, exp_in, exp_out, max_in, max_t, max_row_s,
         max_all, done) = (
            st.sem(n) for n in ("steps", "turned", "copied", "last_ready", "row_turned", "row_ready", "col_turned",
                                "exp_in", "exp_out", "max_in", "max_t", "max_row", "max_all", "done"))
        n_carry = heads * (2 if first else 4)
        cols = scores[:].rearrange("p (r g h) -> p g h r", g=G, h=heads)
        with nc.Block() as block:
            @block.tensor
            def _(pe):
                for h in range(heads):
                    if h >= 2:
                        pe.wait_ge(copied, h - 1)
                    for t in range(G):
                        mm = pe.transpose(ps_turn[0:R, h % 2, t, :], cols[:, t, h, :], c.ident[:])
                    mm.then_inc(turned, 1)
                if first:
                    for h in range(heads):
                        pe.wait_ge(max_in, 1)
                        mm = pe.transpose(ps_col[0:1, 0:R] if h % 2 else ps_row[0:1, 0:R], col_max[:, h:h + 1],
                                          c.ident[0:R, 0:R])
                        mm.then_inc(max_t, 1)
                        pe.wait_ge(max_row_s, h + 1)
                    pe.matmul(ps_row[0:R, 0:heads], c.ones[0:1, 0:R], max_row[0:1, 0:heads],
                              start=True, stop=True).then_inc(max_all, 1)
                    pe.wait_ge(done, 1)
                for n in range(n_carry):
                    pe.wait_ge(last_ready, n + 1)
                    pe.transpose(ps_row[0:1, 0:R], last[:], c.ident[0:R, 0:R]).then_inc(row_turned, 1)
                    pe.wait_ge(row_ready, n + 1)
                    row = chain_row[0:1, 0:R] if n % 2 == 0 else chain_row[0:1, 1:R + 1]
                    pe.transpose(ps_col[0:R, 0:1], row, c.ident[0:1, 0:1]).then_inc(col_turned, 1)

            @block.scalar
            def _(act):
                for h in range(heads):
                    act.wait_ge(turned, h + 1)
                    act.copy(e[:, h].rearrange("r (g j) -> r g j", g=G), ps_turn[0:R, h % 2, 0:G, :]).then_inc(copied, 1)
                for h in range(heads):
                    act.wait_ge(exp_in, h + 1)
                    if first:
                        act.activation(e[:, h], e[:, h], ACT.Exp, bias=neg_max[:, h:h + 1]).then_inc(exp_out, 1)
                    else:
                        act.activation(e[:, h], e[:, h], ACT.Exp).then_inc(exp_out, 1)
                act.wait_ge(exp_out, heads)

            @block.vector
            def _(dve):
                link = Chain(dve, steps)
                n = [0]

                def scanned(out, a, b, start, op0, op1, row_flags, backward):
                    way = slice(None, None, -1) if backward else slice(None)
                    link(dve.tensor_tensor_scan(out[:, way], a[:, way], b[:, way], start, op0, op1))
                    dve.tensor_copy(last[:], out[:, 0:1] if backward else out[:, W - 1:W]).then_inc(last_ready, 1)
                    dve.wait_ge(row_turned, n[0] + 1)
                    if backward:
                        link(dve.memset(chain_row[0:1, R:R + 1], start))
                        dve.tensor_tensor_scan(chain_row[0:1, 0:R][:, ::-1], row_flags[0:1, ::-1], ps_row[0:1, 0:R][:, ::-1],
                                               start, op0, op1).then_inc(row_ready, 1)
                    else:
                        link(dve.memset(chain_row[0:1, 0:1], start))
                        dve.tensor_tensor_scan(chain_row[0:1, 1:R + 1], row_flags, ps_row[0:1, 0:R],
                                               start, op0, op1).then_inc(row_ready, 1)
                    n[0] += 1
                    dve.wait_ge(col_turned, n[0])
                    link(dve.tensor_copy(carry[:], ps_col[0:R, 0:1]))
                    link(dve.tensor_tensor_scan(out[:, way], a[:, way], b[:, way], carry[:, 0:1], op0, op1))

                def whole(out, tmp):
                    link(dve.tensor_tensor(tmp, tmp, o.end[:], ALU.mult))
                    scanned(out, keep_end, tmp, 0.0, ALU.mult, ALU.add, r_keep_end[:], True)

                link(dve.tensor_scalar(keep[:], o.start[:], -1.0, 1.0, ALU.mult, ALU.add))
                link(dve.tensor_scalar(keep_end[:], o.end[:], -1.0, 1.0, ALU.mult, ALU.add))
                link(dve.tensor_scalar(neg[:], o.start[:], -BIG, None, ALU.mult))
                link(dve.tensor_scalar(r_keep[:], o.has_start[:], -1.0, 1.0, ALU.mult, ALU.add))
                link(dve.tensor_scalar(r_keep_end[:], o.has_end[:], -1.0, 1.0, ALU.mult, ALU.add))
                link(dve.tensor_scalar(r_neg[:], o.has_start[:], -BIG, None, ALU.mult))
                dve.wait_ge(copied, heads)
                if first:
                    link(dve.tensor_scalar(neg[:], first["real"], BIG, -BIG, ALU.mult, ALU.add))
                    for h in range(heads):
                        link(dve.scalar_tensor_tensor(e[:, h], e[:, h], first["be2"][0:R, h:h + 1], first["cut"],
                                                      ALU.add, ALU.mult))
                        link(dve.tensor_tensor(e[:, h], e[:, h], neg[:], ALU.add))
                        link(dve.tensor_reduce(col_max[:, h:h + 1], e[:, h], AX.X, ALU.max))
                    dve.sem_inc(max_in, 1)
                    for h in range(heads):
                        dve.wait_ge(max_t, h + 1)
                        dve.tensor_reduce(max_row[0:1, h:h + 1], (ps_col if h % 2 else ps_row)[0:1, 0:R], AX.X,
                                          ALU.max).then_inc(max_row_s, 1)
                    dve.wait_ge(max_all, 1)
                    dve.tensor_scalar(neg_max[:], ps_row[0:R, 0:heads], -1.0, None, ALU.mult).then_inc(done, 1)
                    dve.wait_ge(done, 1)
                    dve.sem_inc(exp_in, heads)
                else:
                    for h in range(heads):
                        scanned(f, neg, e[:, h], -BIG, ALU.add, ALU.max, r_neg[:], False)
                        whole(g, f[:])
                        dve.tensor_tensor(e[:, h], e[:, h], g[:], ALU.subtract).then_inc(exp_in, 1)
                        dve.wait_ge(exp_in, h + 1)
                for h in range(heads):
                    dve.wait_ge(exp_out, h + 1)
                    scanned(f, keep, e[:, h], 0.0, ALU.mult, ALU.add, r_keep[:], False)
                    whole(g, f[:])
                    if first:
                        link(dve.tensor_scalar(g[:], g[:], 1e-8, None, ALU.add))
                    link(dve.reciprocal(f[:], g[:]))
                    link(dve.tensor_tensor(e[:, h], e[:, h], f[:], ALU.mult))
        with stage(nc, name + "_turn") as st2:
            back, out = st2.sem("back"), st2.sem("out")
            with nc.Block() as block:
                @block.tensor
                def _(pe):
                    for h in range(heads):
                        if h >= 2:
                            pe.wait_ge(out, h - 1)
                        for t in range(G):
                            mm = pe.transpose(ps_turn[:, h % 2, t, 0:R], e[:, h, t * P:(t + 1) * P], c.ident[0:R, 0:R])
                        mm.then_inc(back, 1)

                @block.scalar
                def _(act):
                    for h in range(heads):
                        act.wait_ge(back, h + 1)
                        act.copy(cols[:, :, h, :], ps_turn[:, h % 2, 0:G, 0:R]).then_inc(out, 1)
                    act.wait_ge(out, heads)


def cutoff(nc, o, cut):
    with stage(nc, "cutoff") as st:
        u, ui = st.sb("u", [R, W]), st.sb("ui", [R, W], I32)
        v, inside = st.sb("v", [R, W]), st.sb("inside", [R, W])
        half_pi = st.sb("half_pi", [R, 1])
        steps, turn_ready, sined = st.sem("steps"), st.sem("turn_ready"), st.sem("sined")
        two_pi = 6.283185307179586
        with nc.Block() as block:
            @block.vector
            def _(dve):
                link = Chain(dve, steps)
                link(dve.memset(half_pi[:], two_pi / 4))
                link(dve.tensor_scalar(u[:], o.length[:], 0.5 / CUTOFF, None, ALU.mult))
                link(dve.tensor_copy(ui[:], u[:]))
                link(dve.tensor_copy(v[:], ui[:]))
                link(dve.tensor_tensor(u[:], u[:], v[:], ALU.subtract))
                link(dve.scalar_tensor_tensor(u[:], u[:], -1.0, u[:], ALU.mult, ALU.max))
                link(dve.tensor_scalar(v[:], u[:], -1.0, 1.0, ALU.mult, ALU.add))
                link(dve.tensor_tensor(u[:], u[:], v[:], ALU.min))
                dve.sem_inc(turn_ready, 1)
                link(dve.tensor_scalar(inside[:], o.length[:], CUTOFF, 0.5, ALU.is_lt, ALU.mult))
                dve.wait_ge(sined, 1)
                link(dve.scalar_tensor_tensor(cut[:], v[:], 1.0, inside[:], ALU.add, ALU.mult))

            @block.scalar
            def _(act):
                act.wait_ge(turn_ready, 1)
                act.activation(v[:], u[:], ACT.Sin, bias=half_pi[:, 0:1], scale=-two_pi).then_inc(sined, 1)
                act.wait_ge(sined, 1)


def batch_norm_relu(nc, acc, k):
    with stage(nc, "batch_norm") as st:
        sq = st.sb("sq", [P, N])
        m, scale, ss = st.sb("m", [P, 1]), st.sb("scale", [P, 1]), st.sb("ss", [P, 1])
        steps, centred, squared, scaled, out = (st.sem(n) for n in ("steps", "centred", "squared", "scaled", "out"))
        var_ready, rooted = st.sem("var_ready"), st.sem("rooted")
        a = acc[:, 0:N]
        with nc.Block() as block:
            @block.vector
            def _(dve):
                link = Chain(dve, steps)
                link(dve.tensor_scalar(a, a, k["bias"], None, ALU.add))
                link(dve.tensor_reduce(m[:], a, AX.X, ALU.add))
                link(dve.tensor_scalar(m[:], m[:], 1.0 / N, None, ALU.mult))
                link(dve.tensor_scalar(a, a, m[:, 0:1], None, ALU.subtract))
                dve.sem_inc(centred, 1)
                dve.wait_ge(squared, 1)
                link(dve.tensor_scalar(scale[:], ss[:], 1.0 / N, LN_EPS, ALU.mult, ALU.add))
                link(dve.reciprocal(m[:], scale[:]))
                dve.sem_inc(var_ready, 1)
                dve.wait_ge(rooted, 1)
                link(dve.tensor_tensor(scale[:], scale[:], k["gamma"], ALU.mult))
                dve.sem_inc(scaled, 1)

            @block.scalar
            def _(act):
                act.wait_ge(centred, 1)
                act.activation(sq[:], a, ACT.Square, accum_out=ss[:, 0:1]).then_inc(squared, 1)
                act.wait_ge(squared, 1)
                act.wait_ge(var_ready, 1)
                act.activation(scale[:], m[:], ACT.Sqrt).then_inc(rooted, 1)
                act.wait_ge(scaled, 1)
                act.activation(a, a, ACT.Relu, bias=k["beta"], scale=scale[:, 0:1]).then_inc(out, 1)
                act.wait_ge(out, 1)


def node_update(nc, c, name, acc, x, mode, k):
    with stage(nc, name) as st:
        at, xs, xt = (st.sb(n, [P, 2, CB, D]) for n in ("at", "xs", "xt"))
        h, y, z = st.sb("h", [P, CB, D]), st.sb("y", [P, CB, D]), st.sb("z", [P, 2, CB, D])
        stats, mv = st.sb("stats", [P, CB, 6]), st.sb("mv", [P, CB, 2])
        ve, inverse, rs = st.sb("ve", [P, CB]), st.sb("inverse", [P, CB]), st.sb("rs", [P, CB])
        var_ready, rs_ready, stats_go = st.sem("var_ready"), st.sem("rs_ready"), st.sem("stats_go")
        ps_y, ps_t = st.ps("y", [P, 2, 8, P]), st.ps("t", [P, 2, 8, P])
        at_ready, xs_ready, turned, xt_ready, multiplied, steps, slot_free, z_ready = (
            st.sem(n) for n in ("at_ready", "xs_ready", "turned", "xt_ready", "multiplied", "steps", "slot_free",
                                "z_ready"))
        z_free = st.sem("z_free")
        stored = [st.sem(f"stored{s}") for s in range(2)]
        own = mode in ("conv", "last")
        store = {"conv": k.get("table"), "last": k.get("out")}.get(mode)
        n_norms = {"attend": 2, "plain": 1, "conv": 0, "last": 1}[mode]
        n_steps = {"attend": 5, "plain": 1 + (k.get("b") is not None), "conv": 3, "last": 3}[mode] + n_norms * (2 * CB + 3)
        with nc.Block() as block:
            @block.scalar
            def _(act):
                def operands(i, s):
                    n = 2 * i + s
                    act.wait_ge(slot_free, n + 1)
                    act.copy(at[:, s].rearrange("p q d -> p (q d)"),
                             acc[:, bass.ds(n * (CB * P), CB * P)]).then_inc(at_ready, 1)
                    if own:
                        act.copy(xs[:, s], k["own"][:, bass.ds(n * CB, CB), :]).then_inc(xs_ready, 1)
                        act.wait_ge(turned, n + 1)
                        act.copy(xt[:, s], ps_t[:, s, 0:CB, :]).then_inc(xt_ready, 1)

                def roots(i, s):
                    n = 2 * i + s
                    for l in range(n_norms):
                        act.wait_ge(var_ready, n * n_norms + (l + 1))
                        act.activation(rs[:], inverse[:], ACT.Sqrt).then_inc(rs_ready, 1)

                pipelined(act, NC // 2, 2, operands, roots)

            @block.tensor
            def _(pe):
                with pe.Fori(0, NC // 2) as i:
                    for s in range(2):
                        n = 2 * i + s
                        pe.wait_ge(at_ready, n + 1)
                        if own:
                            pe.wait_ge(xs_ready, n + 1)
                            for q in range(CB):
                                mm = pe.transpose(ps_t[:, s, q, :], xs[:, s, q, :], c.ident[:])
                            mm.then_inc(turned, 1)
                            pe.wait_ge(xt_ready, n + 1)
                        for q in range(CB):
                            out_q = ps_y[:, s, q, :]
                            if mode == "plain":
                                mm = pe.transpose(out_q, at[:, s, q, :], c.ident[:])
                            elif mode == "attend":
                                mm = pe.matmul(out_q, at[:, s, q, :], k["w"], start=True, stop=True)
                            else:
                                pe.matmul(out_q, at[:, s, q, :], k["wr"], start=True, stop=False)
                                mm = pe.matmul(out_q, xt[:, s, q, :], k["ws"], start=False, stop=True)
                        mm.then_inc(multiplied, 1)

            @block.vector
            def _(dve):
                dve.sem_inc(slot_free, 2)
                with dve.Fori(0, NC // 2) as i:
                    for s in range(2):
                        n = 2 * i + s
                        count, norms = [0], [0]

                        def link(*several):
                            for ins in several:
                                count[0] += 1
                                ins.then_inc(steps, 1)
                            dve.wait_ge(steps, n * n_steps + count[0])

                        def layer_norm(dst, src):
                            link(*[dve.bn_stats(stats[:, q, :], src[:, q, :]) for q in range(CB)])
                            dve.sem_inc(stats_go, 1)
                            link(*[dve.bn_aggr(mv[:, q, :], stats[:, q, :]) for q in range(CB)])
                            link(dve.tensor_scalar(ve[:], mv[:, :, 1], LN_EPS, None, ALU.add))
                            norms[0] += 1
                            dve.reciprocal(inverse[:], ve[:]).then_inc(var_ready, 1)
                            dve.wait_ge(rs_ready, n * n_norms + norms[0])
                            link(dve.tensor_tensor(dst, src, over_tiles(mv[:, :, 0], D), ALU.subtract))
                            link(dve.tensor_tensor(dst, dst, over_tiles(rs[:], D), ALU.mult))

                        xb = x[:, bass.ds(n * CB, CB), :]
                        product = ps_y[:, s, 0:CB, :]
                        dve.wait_ge(multiplied, n + 1)
                        if k.get("b") is not None:
                            link(dve.tensor_tensor(h[:], product, per_tile(k["b"], CB), ALU.add))
                            product = h[:]
                        if mode == "attend":
                            link(dve.tensor_tensor(y[:], product, xb, ALU.add))
                            layer_norm(h[:], y[:])
                            link(dve.tensor_tensor(y[:], h[:], per_tile(k["g"], CB), ALU.mult))
                            link(dve.tensor_tensor(h[:], y[:], per_tile(k["be"], CB), ALU.add))
                            link(dve.tensor_tensor(y[:], h[:], xb, ALU.add))
                            layer_norm(xb, y[:])
                        elif mode == "plain":
                            link(dve.tensor_tensor(y[:], product, xb, ALU.add))
                            layer_norm(xb, y[:])
                        elif mode == "conv":
                            dve.wait_ge(z_free, n + 1)
                            link(dve.tensor_scalar(k["nodes"][:, bass.ds(n * CB, CB), :], product, 0.0, None, ALU.max))
                            link(dve.tensor_scalar(z[:, s], product, 0.0, None, ALU.max))
                            dve.sem_inc(z_ready, 1)
                        else:
                            dve.wait_ge(z_free, n + 1)
                            link(dve.tensor_scalar(y[:], product, 0.0, None, ALU.max))
                            link(dve.tensor_tensor(h[:], y[:], xb, ALU.add))
                            layer_norm(z[:, s], h[:])
                            dve.sem_inc(z_ready, 1)
                        assert count[0] == n_steps, (mode, count[0], n_steps)
                        dve.sem_inc(slot_free, 1)

            if store is not None:
                @block.sync
                def _(sp):
                    sp.sem_inc(z_free, 2)
                    with sp.Fori(0, NC // 2) as i:
                        for s in range(2):
                            n = 2 * i + s
                            sp.wait_ge(z_ready, n + 1)
                            sp.dma_start(store[bass.ds(n * (CB * P), CB * P), :].rearrange("(q p) d -> p q d", p=P),
                                         z[:, s]).then_inc(stored[s], 16)
                        for s in range(2):
                            sp.wait_ge(stored[s], 16 * (i + 1))
                            sp.sem_inc(z_free, 1)


def gnn_kernel(nc, out, x_in, src, dst, length, edge_weight, real, p):
    with ExitStack() as keep:
        sb = lambda n, s, dt=F32: keep.enter_context(nc.sbuf_tensor(n, s, dt))
        dram = lambda n, s: nc.dram_tensor(n, s, F32).ap()
        by_src, by_dst = Order(nc, "src", keep), Order(nc, "dst", keep)
        c = constants(nc, keep, (by_src, by_dst))
        x, acc = sb("x_nodes", [P, NB, D]), sb("acc", [P, NP])
        scores = sb("scores", [P, T * H0])
        src_counts, dst_counts = sb("src_counts", [P, HB]), sb("dst_counts", [P, HB])
        spill = dram("spill", [R * P, G * D])
        by_dst.real = None
        with ExitStack() as first_layer:
            lsb = lambda n, s, dt=F32: first_layer.enter_context(nc.sbuf_tensor(n, s, dt))
            by_src.real, by_src.length = lsb("real_row", [R, W]), lsb("length_row", [R, W])
            sort_edges(nc, c, by_src, src, dst, length, real, src_counts, False, dst_counts)

            w_raw = lsb("w_raw", [P, 4, D])
            we2_raw, we2t = lsb("we2_raw", [H0, D]), lsb("we2t", [D, H0])
            qkv_w, qkv_b, wo_t = lsb("qkv_w", [P, 3 * D]), lsb("qkv_b", [P, 3 * D]), lsb("wo_t", [P, D])
            we1, be1, be2 = lsb("we1", [P, 1]), lsb("be1", [P, 1]), lsb("be2", [P, H0])
            bo, ln_g, ln_b = lsb("bo", [P, D]), lsb("ln_g", [P, D]), lsb("ln_b", [P, D])
            load_weights(nc, "load0", [
                (x[:], x_in.rearrange("(b p) d -> p b d", p=P)),
                (w_raw[:, 0], p["L0_gnn_Wq"]), (w_raw[:, 1], p["L0_gnn_Wk"]), (w_raw[:, 2], p["L0_gnn_Wv"]),
                (w_raw[:, 3], p["L0_gnn_Wo"]), (we2_raw[:], p["L0_gnn_We2"]), (we1[:], p["L0_gnn_We1"]),
                (be1[:], p["L0_gnn_be1"].rearrange("(d o) -> d o", o=1)),
                (be2[:], spread_row(p["L0_gnn_be2"], H0)),
                (qkv_b[:, 0:D], spread_row(p["L0_gnn_bq"], D)), (qkv_b[:, D:2 * D], spread_row(p["L0_gnn_bk"], D)),
                (qkv_b[:, 2 * D:], spread_row(p["L0_gnn_bv"], D)), (bo[:], spread_row(p["L0_gnn_bo"], D)),
                (ln_g[:], spread_row(p["L0_gnn_ln_g"], D)), (ln_b[:], spread_row(p["L0_gnn_ln_b"], D))])
            transpose_weights(nc, c, "turn0", [(qkv_w[:, n * D:(n + 1) * D], w_raw[:, n]) for n in range(3)]
                              + [(wo_t[:], w_raw[:, 3]), (we2t[:], we2_raw[:])])
            q_table, kv_table = dram("q_table", [NP, D]), dram("kv_table", [NP, 2 * D])
            node_tables(nc, c, "qkv", x, qkv_w[:], qkv_b[:], 3 * D, [(q_table, 0, D), (kv_table, D, 2 * D)])
            cut = lsb("cut", [R, W])
            cutoff(nc, by_src, cut)
            edge_scores(nc, c, by_src, "scores0", kv_table, 2 * D, q_table, D, spill, D, scores, H0, "dot",
                        {"we1": we1[:, 0:1], "be1": be1[:, 0:1], "we2t": we2t[:]})
            segment_softmax(nc, c, by_src, "softmax0", scores, H0,
                            {"real": by_src.real[:], "cut": cut[:], "be2": be2})
            weighted_sum(nc, c, by_src, "sum0", acc, scores, H0, spill=spill)
            node_update(nc, c, "update0", acc, x, "attend",
                        {"w": wo_t[:], "b": bo[:], "g": ln_g[:], "be": ln_b[:]})

        sort_edges(nc, c, by_dst, dst, src, edge_weight, real, dst_counts, True)
        scores1 = scores[:, 0:T * H1]

        lr_w, lr_b = sb("lr_w", [P, 2 * D]), sb("lr_b", [P, 2 * D])
        att, bias1 = sb("att", [P, D]), sb("bias1", [P, D])
        h_w, att_src, att_dst = sb("h_w", [P, D]), sb("att_src", [P, D]), sb("att_dst", [P, D])
        bias2, gamma, beta = sb("bias2", [P, 1]), sb("gamma", [P, 1]), sb("beta", [P, 1])
        conv_w, conv_b = sb("conv_w", [P, 4, D]), sb("conv_b", [P, 2, D])
        column = lambda v: v.rearrange("(d o) -> d o", o=1)
        load_weights(nc, "load1", [
            (lr_w[:, 0:D], p["L1_gnn_W_l"]), (lr_w[:, D:], p["L1_gnn_W_r"]),
            (lr_b[:, 0:D], spread_row(p["L1_gnn_b_l"], D)), (lr_b[:, D:], spread_row(p["L1_gnn_b_r"], D)),
            (att[:], spread_row(p["L1_gnn_att"].rearrange("h c -> (h c)"), D)),
            (bias1[:], spread_row(p["L1_gnn_bias"], D)),
            (h_w[:], p["L2_gnn_W"]), (att_src[:], spread_row(p["L2_gnn_att_src"], D)),
            (att_dst[:], spread_row(p["L2_gnn_att_dst"], D)), (bias2[:], column(p["L2_gnn_bias"])),
            (gamma[:], column(p["L2_gnn_gamma"])), (beta[:], column(p["L2_gnn_beta"])),
            (conv_w[:, 0], p["L3_gnn_Wr0"]), (conv_w[:, 1], p["L3_gnn_Ws0"]),
            (conv_w[:, 2], p["L3_gnn_Wr1"]), (conv_w[:, 3], p["L3_gnn_Ws1"]),
            (conv_b[:, 0], spread_row(p["L3_gnn_br0"], D)), (conv_b[:, 1], spread_row(p["L3_gnn_br1"], D))])
        xl_table, xr_table = dram("xl_table", [NP, D]), dram("xr_table", [NP, D])
        node_tables(nc, c, "lr", x, lr_w[:], lr_b[:], 2 * D, [(xl_table, 0, D), (xr_table, D, D)])
        edge_scores(nc, c, by_dst, "scores1", xl_table, D, xr_table, D, spill, 0, scores1, H1, "gat2", {"att": att[:]})
        segment_softmax(nc, c, by_dst, "softmax1", scores1, H1, None)
        weighted_sum(nc, c, by_dst, "sum1", acc, scores1, H1, spill=spill)
        node_update(nc, c, "update1", acc, x, "plain", {"b": bias1[:]})

        h_table, a_table = dram("h_table", [NP, D]), dram("a_table", [NP, 1])
        node_tables(nc, c, "h", x, h_w[:], None, D, [(h_table, 0, D)], (att_dst[:], a_table))
        scores2 = scores[:, 0:T]
        edge_scores(nc, c, by_dst, "scores2", h_table, D, a_table, 1, spill, 0, scores2, 1, "gat", {"att": att_src[:]})
        segment_softmax(nc, c, by_dst, "softmax2", scores2, 1, None)
        weighted_sum(nc, c, by_dst, "sum2", acc, scores2, 1, spill=spill)
        batch_norm_relu(nc, acc, {"bias": bias2[:, 0:1], "gamma": gamma[:], "beta": beta[:, 0:1]})
        node_update(nc, c, "update2", acc, x, "plain", {})

        x_table, conv_table = dram("x_table", [NP, D]), dram("conv_table", [NP, D])
        h_nodes = scores[:, 0:NB * D].rearrange("p (b d) -> p b d", d=D)
        unit = sb("unit", [P, T])
        load_weights(nc, "store_x", [(x_table.rearrange("(b p) d -> p b d", p=P), x[:])])
        weighted_sum(nc, c, by_dst, "sum3", acc, by_dst.weight, 1, table=x_table)
        node_update(nc, c, "conv0", acc, x, "conv",
                    {"own": x, "wr": conv_w[:, 0], "ws": conv_w[:, 1], "b": conv_b[:, 0], "nodes": h_nodes,
                     "table": conv_table})
        columns_of_real(nc, c, by_dst, unit)
        weighted_sum(nc, c, by_dst, "sum4", acc, unit, 1, table=conv_table)
        node_update(nc, c, "conv1", acc, x, "last",
                    {"own": h_nodes, "wr": conv_w[:, 2], "ws": conv_w[:, 3], "b": conv_b[:, 1], "out": out})


def columns_of_real(nc, c, o, unit):
    with stage(nc, "real_rows") as st:
        rows, real = st.sb("rows", [R, W, 4]), st.sb("real", [R, W])
        loaded, taken = st.sem("loaded"), st.sem("taken")
        with nc.Block() as block:
            @block.sync
            def _(sp):
                sp.dma_start(rows[:].rearrange("r w f -> r (w f)"),
                             o.payload.rearrange("(r w) f -> r (w f)", w=W)).then_inc(loaded, 16)
                sp.wait_ge(loaded, 16)

            @block.vector
            def _(dve):
                dve.wait_ge(loaded, 16)
                dve.tensor_copy(real[:], rows[:, :, 3]).then_inc(taken, 1)
                dve.wait_ge(taken, 1)
        rows_to_columns(nc, c, "turn_real", [(real[:], [unit[:]])])


_WEIGHTS = ["L0_gnn_Wq", "L0_gnn_bq", "L0_gnn_Wk", "L0_gnn_bk", "L0_gnn_Wv", "L0_gnn_bv", "L0_gnn_We1", "L0_gnn_be1",
            "L0_gnn_We2", "L0_gnn_be2", "L0_gnn_Wo", "L0_gnn_bo", "L0_gnn_ln_g", "L0_gnn_ln_b", "L1_gnn_W_l",
            "L1_gnn_b_l", "L1_gnn_W_r", "L1_gnn_b_r", "L1_gnn_att", "L1_gnn_bias", "L2_gnn_W", "L2_gnn_att_src",
            "L2_gnn_att_dst", "L2_gnn_bias", "L2_gnn_gamma", "L2_gnn_beta", "L3_gnn_Wr0", "L3_gnn_br0", "L3_gnn_Ws0",
            "L3_gnn_Wr1", "L3_gnn_br1", "L3_gnn_Ws1"]


def kernel(**inputs):
    import numpy as np
    import concourse.bacc as bacc
    from concourse.bass_utils import run_bass_kernel_spmd

    def columns(a, tail):
        whole = np.concatenate([np.asarray(a).reshape(-1), tail])
        return np.ascontiguousarray(whole.reshape(T, P).T)

    loops = np.full(EP - E, N, np.int32)
    loops[:N] = np.arange(N, dtype=np.int32)
    nothing = np.zeros(EP - E, np.float32)
    x = np.asarray(inputs["x"])
    arrays = {
        "x": np.concatenate([x, np.zeros((NP - N, D), x.dtype)]),
        "src": columns(inputs["src"], loops),
        "dst": columns(inputs["dst"], loops),
        "length": columns(inputs["edge_weight1"], nothing),
        "weight": columns(inputs["edge_weight"], nothing),
        "real": columns(np.ones(E, np.float32), nothing),
    }
    for name in _WEIGHTS:
        arrays[name] = np.ascontiguousarray(inputs[name])
    nc = bacc.Bacc("TRN2", target_bir_lowering=False, num_devices=1)
    aps = {}
    for name, a in arrays.items():
        aps[name] = nc.dram_tensor(f"in_{name}", a.shape, mybir.dt.from_np(a.dtype), kind="ExternalInput").ap()
    out = nc.dram_tensor("out_nodes", [NP, D], F32, kind="ExternalOutput").ap()
    gnn_kernel(nc, out, aps["x"], aps["src"], aps["dst"], aps["length"], aps["weight"], aps["real"],
               {name: aps[name] for name in _WEIGHTS})
    r = run_bass_kernel_spmd(nc, [{f"in_{name}": a for name, a in arrays.items()}], core_ids=[0])
    return r.results[0]["out_nodes"][:N]
```

```python
from contextlib import ExitStack, contextmanager

import concourse.bass as bass
from concourse import mybir

P = 128
N = 6250
E = 106250
D = 128
NB = 50
NP = NB * P
G = 7
R = 126
W = G * P
T = R * G
EP = T * P
SLOTS = 3
CB = 5
NC = NB // CB
assert EP >= E + N and NP >= N + P and R % SLOTS == 0 and R % 2 == 0 and NC * CB == NB and NC % 2 == 0
H0, H1 = 8, 4
HB = 50
BIG = 1e30
LN_EPS = 1e-5
CUTOFF = 5.0

ALU = mybir.AluOpType
ACT = mybir.ActivationFunctionType
AX = mybir.AxisListType
F32 = mybir.dt.float32
BF16 = mybir.dt.bfloat16
I32 = mybir.dt.int32
U32 = mybir.dt.uint32


class Stage:

    def __init__(self, nc, name, stack):
        self.nc, self.name, self.stack, self.sems = nc, name, stack, []

    def sem(self, name):
        s = self.nc.alloc_semaphore(f"{self.name}_{name}")
        self.sems.append(s)
        return s

    def sb(self, name, shape, dt=F32):
        return self.stack.enter_context(self.nc.sbuf_tensor(f"{self.name}_{name}", shape, dt))

    def ps(self, name, shape, dt=F32):
        return self.stack.enter_context(self.nc.psum_tensor(f"{self.name}_ps_{name}", shape, dt))


@contextmanager
def stage(nc, name):
    with ExitStack() as stack:
        st = Stage(nc, name, stack)
        yield st
    nc.clear_and_free_semaphores(st.sems)
    nc.all_engine_barrier()


class Chain:

    def __init__(self, eng, sem):
        self.eng, self.sem, self.n = eng, sem, 0

    def __call__(self, ins):
        self.n += 1
        ins.then_inc(self.sem, 1)
        self.eng.wait_ge(self.sem, self.n)


def pipelined(eng, rounds, slots, prepare, finish):
    def steps(i, more):
        for s in range(slots):
            if s + 1 < slots:
                prepare(i, s + 1)
            elif more:
                prepare(i + 1, 0)
            finish(i, s)

    prepare(0, 0)
    with eng.Fori(0, rounds - 1) as i:
        steps(i, True)
    steps(rounds - 1, False)


def over_tiles(ap, inner):
    g = ap.shape[1]
    return ap.rearrange("p (g o) -> p g o", o=1).to_broadcast([ap.shape[0], g, inner])


def per_tile(ap, g=G):
    return ap.rearrange("p (o n) -> p o n", o=1).to_broadcast([ap.shape[0], g, ap.shape[1]])


def group(col, gi, width=1):
    return col[:, bass.ds(gi * (G * width), G * width)]


class Order:

    def __init__(self, nc, name, keep):
        self.name = name
        self.payload = nc.dram_tensor(f"payload_{name}", [EP, 4], F32).ap()
        self.base_dram = nc.dram_tensor(f"base_{name}", [1, R * 8], I32).ap()
        self.rel_rows = nc.dram_tensor(f"rel_rows_{name}", [R, 8, P], BF16).ap()
        sb = lambda n, s, dt=F32: keep.enter_context(nc.sbuf_tensor(f"{name}_{n}", s, dt))
        self.other = sb("other", [P, T + SLOTS * G], I32)
        self.rel = sb("rel", [P, T])
        self.rel_bf = sb("rel_bf", [P, T], BF16)
        self.base = sb("base", [1, R * 8], I32)
        self.weight = sb("weight", [P, T])
        self.start = sb("start", [R, W])
        self.end = sb("end", [R, W])
        self.has_start = sb("has_start", [1, R])
        self.has_end = sb("has_end", [1, R])


def constants(nc, keep, orders):
    class C:
        pass
    c = C()
    sb = lambda n, s, dt=F32: keep.enter_context(nc.sbuf_tensor(f"const_{n}", s, dt))
    c.ident, c.ident_bf = sb("ident", [P, P]), sb("ident_bf", [P, P], BF16)
    c.lane, c.column = sb("lane", [P, 1]), sb("column", [P, P])
    c.before, c.after = sb("before", [P, P]), sb("after", [P, P])
    c.ones = sb("ones", [P, P])
    c.minus_pick = sb("minus_pick", [8, G, P], BF16)
    with stage(nc, "constants") as st:
        pick = st.sb("pick", [8, G, P])
        made, ones_ready, ident_ready, pick_ready, bf_ready = (
            st.sem(n) for n in ("made", "ones", "ident", "pick_ready", "bf"))
        with nc.Block() as block:
            @block.gpsimd
            def _(pool):
                pool.memset(c.ident[:], 0.0).then_inc(ident_ready, 1)
                pool.wait_ge(ident_ready, 1)
                pool.affine_select(out=c.ident[:], in_=c.ident[:], compare_op=ALU.not_equal, fill=1.0, base=0,
                                   pattern=[[-1, P]], channel_multiplier=1).then_inc(ident_ready, 1)
                pool.iota(c.lane[:], [[0, 1]], base=0, channel_multiplier=1,
                          allow_small_or_imprecise_dtypes=True).then_inc(made, 1)
                pool.iota(c.column[:], [[1, P]], base=0, channel_multiplier=0,
                          allow_small_or_imprecise_dtypes=True).then_inc(made, 1)
                pool.memset(c.ones[:], 1.0).then_inc(ones_ready, 1)
                pool.wait_ge(ones_ready, 1)
                pool.affine_select(out=c.before[:], in_=c.ones[:], compare_op=ALU.is_ge, fill=0.0, base=-1,
                                   pattern=[[-1, P]], channel_multiplier=1).then_inc(made, 1)
                pool.affine_select(out=c.after[:], in_=c.ones[:], compare_op=ALU.is_ge, fill=0.0, base=-1,
                                   pattern=[[1, P]], channel_multiplier=-1).then_inc(made, 1)
                pool.iota(pick[:], [[0, G], [1, P]], base=0, channel_multiplier=0,
                          allow_small_or_imprecise_dtypes=True).then_inc(pick_ready, 1)
                pool.wait_ge(pick_ready, 1)
                pool.affine_select(out=pick[:], in_=pick[:], compare_op=ALU.is_ge, fill=0.0, base=-7,
                                   pattern=[[0, G], [0, P]], channel_multiplier=1).then_inc(pick_ready, 1)
                pool.wait_ge(pick_ready, 2)
                pool.affine_select(out=pick[:], in_=pick[:], compare_op=ALU.not_equal, fill=-1.0, base=0,
                                   pattern=[[-1, G], [0, P]], channel_multiplier=1).then_inc(pick_ready, 1)
                pool.wait_ge(made, 4)

            @block.vector
            def _(dve):
                dve.wait_ge(ident_ready, 2)
                dve.wait_ge(made, 4)
                dve.tensor_copy(c.ident_bf[:], c.ident[:]).then_inc(bf_ready, 1)
                dve.wait_ge(pick_ready, 3)
                dve.tensor_copy(c.minus_pick[:], pick[:]).then_inc(bf_ready, 1)
                for o in orders:
                    dve.memset(o.other[:, T:], 0).then_inc(bf_ready, 1)
                dve.wait_ge(bf_ready, 2 + len(orders))
    return c


def sort_edges(nc, c, o, key_d, other_d, weight_d, real_d, counts, counted_before, count_next=None):
    with stage(nc, f"load_{o.name}") as st:
        key, other = st.sb("key", [P, T], I32), st.sb("other", [P, T], I32)
        weight, real = st.sb("weight", [P, T]), st.sb("real", [P, T])
        bits = st.sb("bits", [P, T], I32)
        lo_bf, hi, hi_bf = (st.sb(n, [P, T], BF16) for n in ("lo_bf", "hi", "hi_bf"))
        pay = st.sb("pay", [P, T, 4])
        totals = st.sb("totals", [P, HB])
        if count_next is not None:
            next_lo, next_hi = st.sb("next_lo", [P, T], BF16), st.sb("next_hi", [P, T], BF16)
        upto, first = st.sb("upto", [P, HB]), st.sb("first", [P, HB])
        one_lo, one_hi = st.sb("one_lo", [P, 2, P, G], BF16), st.sb("one_hi", [P, 2, HB, G], BF16)
        column_g = st.sb("column_g", [P, P, G], BF16)
        zero = st.sb("zero", [P, P], BF16)
        ps_counts, ps_sums = st.ps("counts", [P, 512]), st.ps("sums", [P, 512])
        loaded, steps, paid, split = (st.sem(n) for n in ("loaded", "steps", "paid", "split"))
        cleared, hot_ready, hot_used, counted, copied, summed = (
            st.sem(n) for n in ("cleared", "hot_ready", "hot_used", "counted", "copied", "summed"))

        with nc.Block() as block:
            @block.sync
            def _(sp):
                for buf, src in ((key, key_d), (other, other_d), (weight, weight_d), (real, real_d)):
                    sp.dma_start(buf[:], src).then_inc(loaded, 16)
                sp.wait_ge(loaded, 64)

            @block.scalar
            def _(act):
                act.wait_ge(loaded, 64)
                for f, buf in enumerate((key, other, weight, real)):
                    act.copy(pay[:, :, f], buf[:]).then_inc(paid, 1)
                act.wait_ge(paid, 4)
                if not counted_before:
                    act.wait_ge(counted, 1)
                    act.copy(counts[:], ps_counts[:, 0:HB]).then_inc(copied, 1)
                    act.wait_ge(copied, 1)

            @block.vector
            def _(dve):
                link = Chain(dve, steps)
                dve.memset(zero[:], 0.0).then_inc(cleared, 1)
                link(dve.tensor_copy(column_g[:], over_tiles(c.column[:], G)))
                dve.wait_ge(loaded, 64)
                link(dve.tensor_single_scalar(bits[:], key[:], P - 1, ALU.bitwise_and))
                link(dve.tensor_copy(lo_bf[:], bits[:]))
                link(dve.tensor_single_scalar(bits[:], key[:], 7, ALU.arith_shift_right))
                link(dve.tensor_copy(hi[:], bits[:]))
                link(dve.tensor_scalar(hi_bf[:], hi[:], float(P), None, ALU.mult))
                dve.wait_ge(paid, 4)
                if count_next is not None:
                    link(dve.tensor_single_scalar(bits[:], other[:], P - 1, ALU.bitwise_and))
                    link(dve.tensor_copy(next_lo[:], bits[:]))
                    link(dve.tensor_single_scalar(bits[:], other[:], 7, ALU.arith_shift_right))
                    link(dve.tensor_copy(next_hi[:], bits[:]))
                if not counted_before:
                    dve.sem_inc(hot_used, 2)
                    with dve.Fori(0, R // 2) as i:
                        for s in range(2):
                            gi = 2 * i + s
                            dve.wait_ge(hot_used, gi + 1)
                            dve.tensor_tensor(one_lo[:, s], column_g[:], per_tile(group(lo_bf, gi), P),
                                      ALU.is_equal).then_inc(hot_ready, 1)
                            dve.tensor_tensor(one_hi[:, s], column_g[:, 0:HB], per_tile(group(hi, gi), HB),
                                      ALU.is_equal).then_inc(hot_ready, 1)
                    dve.wait_ge(hot_ready, 2 * R)
                dve.wait_ge(summed, 1)
                link(dve.tensor_copy(totals[:], ps_sums[:, 64:64 + HB]))
                link(dve.tensor_tensor_scan(upto[:], c.ones[:, 0:HB], totals[:], 0.0, ALU.mult, ALU.add))
                link(dve.tensor_tensor(upto[:], upto[:], totals[:], ALU.subtract))
                link(dve.tensor_tensor(first[:], upto[:], ps_sums[:, 0:HB], ALU.add))

            @block.tensor
            def _(pe):
                pe.wait_ge(cleared, 1)
                pe.matmul(ps_counts[:, 0:HB], zero[:], zero[:, 0:HB], start=True, stop=True, skip_group_check=True)
                if not counted_before:
                    with pe.Fori(0, R // 2) as i:
                        for s in range(2):
                            gi = 2 * i + s
                            pe.wait_ge(hot_ready, 2 * gi + 2)
                            for j in range(G):
                                mm = pe.matmul(ps_counts[:, 0:HB], one_lo[:, s, :, j], one_hi[:, s, :, j],
                                               start=False, stop=True, skip_group_check=True)
                            mm.then_inc(hot_used, 1)
                    pe.matmul(ps_sums[:, 448:450], zero[:], zero[:, 0:2], start=True, stop=True).then_inc(counted, 1)
                    pe.wait_ge(copied, 1)
                pe.matmul(ps_sums[:, 0:HB], c.after[:], counts[:], start=True, stop=True)
                pe.matmul(ps_sums[:, 64:64 + HB], c.ones[:], counts[:], start=True, stop=True).then_inc(summed, 1)

        one_lo_t = st.sb("one_lo_t", [P, 2, G, P])
        same, rank, at = st.sb("same", [P, G, P]), st.sb("rank", [P, 2, G]), st.sb("at", [P, 2, G])
        picked = st.sb("picked", [P, G, HB])
        at_i = st.sb("at_i", [P, 2, G], I32)
        pay_slot = st.sb("pay_slot", [P, 2, G, 4])
        running = st.sb("running", [P, 2, HB])
        ps_lo, ps_key = st.ps("lo", [P, 8, P]), st.ps("key", [P, 8, P])
        ps_run, ps_look = st.ps("run", [P, 512]), st.ps("look", [P, G, 64])
        (spread, keys_read, lo_t_ready, ran, snapped, looked, picked_s, look_read, ranked, staged, slot_free,
         pool_go, at_ready) = (
            st.sem(n) for n in ("spread", "keys_read", "lo_t", "ran", "snapped", "looked", "picked", "look_read",
                                "ranked", "staged", "slot_free", "pool_go", "at_ready"))
        hot2_ready = st.sem("hot2_ready")
        scattered = [st.sem(f"scattered{s}") for s in range(2)]
        if count_next is not None:
            next_one_lo, next_one_hi = st.sb("next_one_lo", [P, 2, P, G], BF16), st.sb("next_one_hi", [P, 2, HB, G], BF16)
            next_ready, next_copied = st.sem("next_ready"), st.sem("next_copied")

        with nc.Block() as block:
            @block.tensor
            def _(pe):
                def spread_keys(i, s):
                    gi = 2 * i + s
                    pe.wait_ge(keys_read, gi + 1)
                    for j in range(G):
                        col = bass.ds(gi * G + j, 1)
                        a = lo_bf[:, col].to_broadcast([P, P])
                        b = hi_bf[:, col].to_broadcast([P, P])
                        pe.matmul(ps_lo[:, j, :], a, c.ident_bf[:], start=True, stop=True)
                        pe.matmul(ps_key[:, j, :], a, c.ident_bf[:], start=True, stop=False)
                        mm = pe.matmul(ps_key[:, j, :], b, c.ident_bf[:], start=False, stop=True)
                    mm.then_inc(spread, 1)

                def look_up(i, s):
                    gi = 2 * i + s
                    pe.wait_ge(lo_t_ready, gi + 1)
                    pe.wait_ge(hot2_ready, 2 * gi + 2)
                    pe.wait_ge(look_read, gi + 1)
                    for j in range(G):
                        k = (s * G + j) % 2
                        pe.wait_ge(snapped, gi * G + (j + 1))
                        pe.matmul(ps_run[:, 0:HB], one_lo[:, s, :, j], one_hi[:, s, :, j], start=False, stop=True,
                                  skip_group_check=True).then_inc(ran, 1)
                        if count_next is not None:
                            if j == 0:
                                pe.wait_ge(next_ready, 2 * gi + 2)
                            pe.matmul(ps_counts[:, 0:HB], next_one_lo[:, s, :, j], next_one_hi[:, s, :, j], start=False,
                                      stop=True, skip_group_check=True)
                        pe.matmul(ps_look[:, j, 0:HB], one_lo_t[:, s, j, :], running[:, k, :],
                                  start=True, stop=True).then_inc(looked, 1)

                if count_next is not None:
                    pe.matmul(ps_counts[:, 0:HB], zero[:], zero[:, 0:HB], start=True, stop=True, skip_group_check=True)
                pe.matmul(ps_run[:, 0:HB], c.ident[:], first[:], start=True, stop=True,
                          skip_group_check=True).then_inc(ran, 1)
                pipelined(pe, R // 2, 2, spread_keys, look_up)

            @block.scalar
            def _(act):
                with act.Fori(0, R // 2) as i:
                    for s in range(2):
                        gi = 2 * i + s
                        act.wait_ge(slot_free, gi + 1)
                        act.copy(pay_slot[:, s].rearrange("p g f -> p (g f)"),
                                 group(pay[:].rearrange("p t f -> p (t f)"), gi, 4)).then_inc(staged, 1)
                        for j in range(G):
                            k = (s * G + j) % 2
                            act.wait_ge(ran, gi * G + (j + 1))
                            act.copy(running[:, k, :], ps_run[:, 0:HB]).then_inc(snapped, 1)

            @block.vector
            def _(dve):
                def compare(i, s):
                    gi = 2 * i + s
                    dve.tensor_tensor(one_lo[:, s], column_g[:], per_tile(group(lo_bf, gi), P),
                                      ALU.is_equal).then_inc(hot2_ready, 1)
                    dve.tensor_tensor(one_hi[:, s], column_g[:, 0:HB], per_tile(group(hi, gi), HB),
                                      ALU.is_equal).then_inc(hot2_ready, 1)
                    if count_next is not None:
                        dve.tensor_tensor(next_one_lo[:, s], column_g[:], per_tile(group(next_lo, gi), P),
                                      ALU.is_equal).then_inc(next_ready, 1)
                        dve.tensor_tensor(next_one_hi[:, s], column_g[:, 0:HB], per_tile(group(next_hi, gi), HB),
                                      ALU.is_equal).then_inc(next_ready, 1)
                    dve.wait_ge(spread, gi + 1)
                    dve.tensor_scalar(one_lo_t[:, s], ps_lo[:, 0:G, :], c.lane[:, 0:1], None,
                                      ALU.is_equal).then_inc(lo_t_ready, 1)
                    for j in range(G):
                        dve.scalar_tensor_tensor(same[:, j, :], ps_key[:, j, :], pay[:, bass.ds(gi * G + j, 1), 0],
                                                 c.before[:], ALU.is_equal, ALU.mult,
                                                 accum_out=rank[:, s, j:j + 1]).then_inc(ranked, 1)
                    dve.wait_ge(ranked, gi * G + G)
                    dve.sem_inc(keys_read, 1)

                def place(i, s):
                    gi = 2 * i + s
                    dve.wait_ge(looked, gi * G + G)
                    dve.tensor_tensor(picked[:], one_hi[:, s].rearrange("p h g -> p g h"), ps_look[:, :, 0:HB],
                                      ALU.mult).then_inc(look_read, 1)
                    dve.wait_ge(look_read, gi + 2)
                    dve.tensor_reduce(at[:, s], picked[:], AX.X, ALU.add).then_inc(picked_s, 1)
                    dve.wait_ge(picked_s, gi + 1)
                    dve.wait_ge(slot_free, gi + 1)
                    dve.tensor_tensor(at_i[:, s], at[:, s], rank[:, s], ALU.add).then_inc(at_ready, 1)
                    dve.wait_ge(at_ready, gi + 1)

                dve.sem_inc(keys_read, 1)
                dve.sem_inc(look_read, 1)
                pipelined(dve, R // 2, 2, compare, place)
                if count_next is not None:
                    dve.tensor_copy(count_next[:], ps_counts[:, 0:HB]).then_inc(next_copied, 1)
                    dve.wait_ge(next_copied, 1)

            @block.gpsimd
            def _(pool):
                with pool.Fori(0, R // 2) as i:
                    for s in range(2):
                        gi = 2 * i + s
                        pool.wait_ge(staged, gi + 1)
                        pool.wait_ge(at_ready, gi + 1)
                        pool.sem_inc(pool_go, 1)
                        for j in range(G):
                            pool.indirect_dma_start(
                                o.payload, bass.IndirectOffsetOnAxis(ap=at_i[:, s, j:j + 1].bitcast(U32), axis=0),
                                pay_slot[:, s, j, :], None).then_inc(scattered[s], 16)

            @block.sync
            def _(sp):
                sp.sem_inc(slot_free, 2)
                with sp.Fori(0, R // 2) as i:
                    for s in range(2):
                        sp.wait_ge(scattered[s], 16 * G * (i + 1))
                        sp.sem_inc(slot_free, 1)

    with stage(nc, f"rows_{o.name}") as st:
        rows = st.sb("rows", [R, W, 4])
        key, rel = st.sb("key", [R, W]), st.sb("rel", [R, W])
        last_key, next_key = st.sb("last_key", [P, 1]), st.sb("next_key", [P, 1])
        base_i = st.sb("base_i", [R, 8], I32)
        flag = st.sb("flag", [R, 2])
        rel_ones = st.sb("rel_ones", [R, 8, P], BF16)
        loaded, steps, based, based2, turned = (st.sem(n) for n in ("loaded", "steps", "based", "based2", "turned"))
        edge_keys = o.payload.rearrange("(r w) f -> r w f", w=W)
        ps_flag = st.ps("flag", [P, 2, P])
        with nc.Block() as block:
            @block.sync
            def _(sp):
                sp.dma_start(rows[:].rearrange("r w f -> r (w f)"),
                             o.payload.rearrange("(r w) f -> r (w f)", w=W)).then_inc(loaded, 16)
                sp.wait_ge(steps, 2)
                with nc.allow_non_contiguous_dma(reason="one key per row"):
                    sp.dma_start(last_key[1:R, :], edge_keys[0:R - 1, W - 1, 0:1]).then_inc(loaded, 16)
                    sp.dma_start(next_key[0:R - 1, :], edge_keys[1:R, 0, 0:1]).then_inc(loaded, 16)
                sp.wait_ge(based, 1)
                sp.dma_start(o.base_dram.rearrange("o (r g) -> (o r) g", g=8), base_i[:]).then_inc(based2, 16)
                sp.wait_ge(based2, 16)
                sp.dma_start(o.base[:], o.base_dram).then_inc(based2, 16)
                sp.wait_ge(based2, 32)
                sp.wait_ge(steps, 8)
                sp.dma_start(o.rel_rows.rearrange("r g e -> r (g e)"),
                             rel_ones[:].rearrange("r g e -> r (g e)")).then_inc(based2, 16)
                sp.wait_ge(based2, 48)

            @block.vector
            def _(dve):
                link = Chain(dve, steps)
                link(dve.memset(last_key[:], -1.0))
                link(dve.memset(next_key[:], -1.0))
                link(dve.memset(base_i[:], 0))
                link(dve.memset(rel_ones[:], 1.0))
                dve.wait_ge(loaded, 48)
                link(dve.tensor_copy(key[:], rows[:, :, 0]))
                firsts = key[:].rearrange("r (g e) -> r g e", e=P)[:, :, 0]
                link(dve.tensor_copy(base_i[:, 0:G], firsts))
                dve.sem_inc(based, 1)
                link(dve.tensor_tensor(rel[:].rearrange("r (g e) -> r g e", e=P),
                                       key[:].rearrange("r (g e) -> r g e", e=P), over_tiles(firsts, P), ALU.subtract))
                link(dve.tensor_copy(rel_ones[:, 0:G, :], rel[:].rearrange("r (g e) -> r g e", e=P)))
                link(dve.tensor_tensor(o.start[:, 1:W], key[:, 1:W], key[:, 0:W - 1], ALU.not_equal))
                link(dve.tensor_tensor(o.start[:, 0:1], key[:, 0:1], last_key[0:R, :], ALU.not_equal))
                link(dve.tensor_tensor(o.end[:, 0:W - 1], key[:, 1:W], key[:, 0:W - 1], ALU.not_equal))
                link(dve.tensor_tensor(o.end[:, W - 1:W], key[:, W - 1:W], next_key[0:R, :], ALU.not_equal))
                link(dve.tensor_reduce(flag[:, 0:1], o.start[:], AX.X, ALU.max))
                link(dve.tensor_reduce(flag[:, 1:2], o.end[:], AX.X, ALU.max))
                dve.wait_ge(turned, 1)
                link(dve.tensor_copy(o.has_start[:], ps_flag[0:1, 0, 0:R]))
                link(dve.tensor_copy(o.has_end[:], ps_flag[0:1, 1, 0:R]))

            @block.tensor
            def _(pe):
                pe.wait_ge(steps, 14)
                pe.transpose(ps_flag[0:1, 0, 0:R], flag[:, 0:1], c.ident[0:R, 0:R])
                pe.transpose(ps_flag[0:1, 1, 0:R], flag[:, 1:2], c.ident[0:R, 0:R]).then_inc(turned, 1)

        rows_to_columns(nc, c, f"turn_{o.name}", [
            (rows[:, :, 1], [o.other[:, 0:T]]), (rel[:], [o.rel[:], o.rel_bf[:]]), (rows[:, :, 2], [o.weight[:]])])
        if o.real is not None:
            with stage(nc, f"real_{o.name}") as st2:
                done = st2.sem("done")
                with nc.Block() as block:
                    @block.vector
                    def _(dve):
                        dve.tensor_copy(o.real[:], rows[:, :, 3]).then_inc(done, 1)
                        dve.tensor_copy(o.length[:], rows[:, :, 2]).then_inc(done, 1)
                        dve.wait_ge(done, 2)


def rows_to_columns(nc, c, name, pairs):
    with stage(nc, name) as st:
        ps = st.ps("turn", [P, 2, 8, P])
        turned, copied = st.sem("turned"), st.sem("copied")
        with nc.Block() as block:
            @block.tensor
            def _(pe):
                done = 0
                for n, (row, cols) in enumerate(pairs):
                    if n >= 2:
                        pe.wait_ge(copied, sum(len(x) for _, x in pairs[:n - 1]))
                    for g in range(G):
                        mm = pe.transpose(ps[:, n % 2, g, 0:R], row[:, g * P:(g + 1) * P], c.ident[0:R, 0:R])
                    mm.then_inc(turned, 1)

            @block.scalar
            def _(act):
                for n, (row, cols) in enumerate(pairs):
                    act.wait_ge(turned, n + 1)
                    for col in cols:
                        act.copy(col.rearrange("p (r g) -> p g r", g=G),
                                 ps[:, n % 2, 0:G, 0:R]).then_inc(copied, 1)
                act.wait_ge(copied, sum(len(x) for _, x in pairs))


def load_weights(nc, name, loads):
    with stage(nc, name) as st:
        loaded = st.sem("loaded")
        with nc.Block() as block:
            @block.sync
            def _(sp):
                with nc.allow_non_contiguous_dma(reason="vectors across partitions, once"):
                    for dst, src in loads:
                        sp.dma_start(dst, src).then_inc(loaded, 16)
                sp.wait_ge(loaded, 16 * len(loads))


def spread_row(vec, n):
    return vec.rearrange("(o n) -> o n", o=1).to_broadcast([P, n])


def transpose_weights(nc, c, name, pairs):
    with stage(nc, name) as st:
        ps = st.ps("turn", [P, len(pairs), 512])
        turned, copied = st.sem("turned"), st.sem("copied")
        with nc.Block() as block:
            @block.tensor
            def _(pe):
                for n, (dst, src) in enumerate(pairs):
                    k, m = src.shape
                    pe.transpose(ps[0:m, n, 0:k], src, c.ident[0:k, 0:k]).then_inc(turned, 1)

            @block.vector
            def _(dve):
                for n, (dst, src) in enumerate(pairs):
                    k, m = src.shape
                    dve.wait_ge(turned, n + 1)
                    dve.tensor_copy(dst, ps[0:m, n, 0:k]).then_inc(copied, 1)
                dve.wait_ge(copied, len(pairs))


def node_tables(nc, c, name, x, weight, bias, out_w, tables, dots=None):
    with stage(nc, name) as st:
        xs, xt, y = st.sb("xs", [P, 2, CB, D]), st.sb("xt", [P, 2, CB, D]), st.sb("y", [P, 2, CB, out_w])
        prod, dot = st.sb("prod", [P, CB, D]), st.sb("dot", [P, 2, CB])
        ps_t, ps_y = st.ps("t", [P, 8, P]), st.ps("y", [P, CB, 512])
        xs_ready, turned, xt_ready, multiplied, y_ready, dot_ready = (
            st.sem(n) for n in ("xs_ready", "turned", "xt_ready", "multiplied", "y_ready", "dot_ready"))
        stored = [st.sem(f"stored{s}") for s in range(2)]
        n_st = len(tables) + (dots is not None)
        with nc.Block() as block:
            @block.scalar
            def _(act):
                def rows_in(i, s):
                    act.copy(xs[:, s], x[:, bass.ds((2 * i + s) * CB, CB), :]).then_inc(xs_ready, 1)

                def turned_in(i, s):
                    n = 2 * i + s
                    act.wait_ge(turned, n + 1)
                    act.wait_ge(multiplied, n + 1)
                    act.copy(xt[:, s], ps_t[:, 0:CB, :]).then_inc(xt_ready, 1)

                pipelined(act, NC // 2, 2, rows_in, turned_in)

            @block.tensor
            def _(pe):
                def turns(i, s):
                    pe.wait_ge(xs_ready, 2 * i + s + 1)
                    pe.wait_ge(xt_ready, 2 * i + s + 1)
                    for q in range(CB):
                        mm = pe.transpose(ps_t[:, q, :], xs[:, s, q, :], c.ident[:])
                    mm.then_inc(turned, 1)

                def products(i, s):
                    n = 2 * i + s
                    pe.wait_ge(xt_ready, n + 2)
                    pe.wait_ge(y_ready, n + 1)
                    for q in range(CB):
                        mm = pe.matmul(ps_y[:, q, 0:out_w], xt[:, s, q, :], weight, start=True, stop=True)
                    mm.then_inc(multiplied, 1)

                pe.sem_inc(multiplied, 2)
                pe.sem_inc(xt_ready, 1)
                pipelined(pe, NC // 2, 2, turns, products)

            @block.vector
            def _(dve):
                dve.sem_inc(y_ready, 1)
                with dve.Fori(0, NC // 2) as i:
                    for s in range(2):
                        n = 2 * i + s
                        dve.wait_ge(multiplied, n + 3)
                        dve.wait_ge(stored[s], (16 * n_st) * (i + 1))
                        if bias is None:
                            dve.tensor_copy(y[:, s], ps_y[:, :, 0:out_w]).then_inc(y_ready, 1)
                        else:
                            dve.tensor_tensor(y[:, s], ps_y[:, :, 0:out_w], per_tile(bias, CB), ALU.add).then_inc(y_ready, 1)
                        if dots is not None:
                            dve.wait_ge(y_ready, n + 2)
                            dve.tensor_tensor(prod[:], y[:, s, :, 0:D], per_tile(dots[0], CB),
                                              ALU.mult).then_inc(dot_ready, 1)
                            dve.wait_ge(dot_ready, 2 * n + 1)
                            dve.tensor_reduce(dot[:, s], prod[:], AX.X, ALU.add).then_inc(dot_ready, 1)

            @block.sync
            def _(sp):
                for s in range(2):
                    sp.sem_inc(stored[s], 16 * n_st)
                with sp.Fori(0, NC // 2) as i:
                    for s in range(2):
                        n = 2 * i + s
                        sp.wait_ge(y_ready, n + 2)
                        if dots is not None:
                            sp.wait_ge(dot_ready, 2 * n + 2)
                        for table, c0, w in tables:
                            sp.dma_start(table[bass.ds(n * (CB * P), CB * P), :].rearrange("(q p) d -> p q d", p=P),
                                         y[:, s, :, c0:c0 + w]).then_inc(stored[s], 16)
                        if dots is not None:
                            with nc.allow_non_contiguous_dma(reason="one value per node"):
                                sp.dma_start(dots[1][bass.ds(n * (CB * P), CB * P), :].rearrange("(q p) o -> p (q o)", p=P),
                                             dot[:, s]).then_inc(stored[s], 16)
                for s in range(2):
                    sp.wait_ge(stored[s], (16 * n_st) * (NC // 2 + 1))


def edge_scores(nc, c, o, name, table, table_w, window, window_w, spill, spill_at, scores, heads, mode, k):
    with stage(nc, name) as st:
        idx = st.sb("idx", [P, SLOTS, G], I32)
        rel = st.sb("rel", [P, SLOTS, G], BF16)
        rows = st.sb("rows", [P, SLOTS, G, table_w])
        win = st.sb("win", [P, SLOTS, G, window_w])
        hot_t = st.sb("hot_t", [P, SLOTS, G, P])
        prod, act_m = st.sb("prod", [P, G, D]), st.sb("act_m", [P, G, D])
        red = st.sb("red", [P, G * heads])
        ps_rel, ps_x = st.ps("rel", [P, 8, P]), st.ps("x", [P, 8, P])
        (idx_staged, rel_staged, spread, hot_ready, expanded, consumed, reduced, scored, spill_done, pool_go, multiplied,
         leaked) = (
            st.sem(n) for n in ("idx_staged", "rel_staged", "spread", "hot_ready", "expanded", "consumed", "reduced",
                                "scored", "spill_done", "pool_go", "multiplied", "leaked"))
        gathered, win_loaded, spilled = ([st.sem(f"{n}{s}") for s in range(SLOTS)]
                                         for n in ("gathered", "win_loaded", "spilled"))
        bias_mode = mode == "dot"
        if bias_mode:
            length = st.sb("length", [P, SLOTS, G])
            hidden, warm = st.sb("hidden", [P, G, P]), st.sb("warm", [P, 1])
            warmed = st.sem("warmed")
            ps_len, ps_bias = st.ps("len", [P, 8, P]), st.ps("bias", [P, G, H0])
            len_staged, len_spread, hid_ready, biased = (
                st.sem(n) for n in ("len_staged", "len_spread", "hid_ready", "biased"))
        with nc.Block() as block:
            @block.scalar
            def _(act):
                def columns_and_windows(i, s):
                    gi = SLOTS * i + s
                    act.wait_ge(consumed, gi + 1)
                    act.copy(rel[:, s], group(o.rel_bf, gi)).then_inc(rel_staged, 1)
                    if bias_mode:
                        act.copy(length[:, s], group(o.weight, gi)).then_inc(len_staged, 1)
                    _, base = nc.values_load_multi_w_load_instructions(
                        o.base[0:1, bass.ds(gi * 8, 8)], engines=[act.engine], min_val=0, max_val=N,
                        skip_runtime_bounds_check_because="keys are node numbers")
                    with nc.allow_non_contiguous_dma(reason="a row of one value per node"):
                        for j in range(G):
                            act.dma_start(win[:, s, j, :], window[bass.ds(base[j], P), :]).then_inc(win_loaded[s], 16)

                def hidden_layer(i, s):
                    gi = SLOTS * i + s
                    if bias_mode:
                        act.wait_ge(len_spread, gi + 1)
                        act.wait_ge(biased, gi + 1)
                        act.activation(hidden[:], ps_len[:, 0:G, :], ACT.Silu, bias=k["be1"],
                                       scale=k["we1"]).then_inc(hid_ready, 1)

                if bias_mode:
                    act.activation(warm[:], k["be1"], ACT.Silu).then_inc(warmed, 1)
                    act.wait_ge(warmed, 1)
                    act.sem_inc(hid_ready, 1)
                pipelined(act, R // SLOTS, SLOTS, columns_and_windows, hidden_layer)

            @block.gpsimd
            def _(pool):
                with pool.Fori(0, R // SLOTS) as i:
                    for s in range(SLOTS):
                        gi = SLOTS * i + s
                        pool.wait_ge(idx_staged, gi + 1)
                        pool.wait_ge(consumed, gi + 1)
                        pool.wait_ge(spill_done, gi + 1)
                        pool.sem_inc(pool_go, 1)
                        for j in range(G):
                            pool.indirect_dma_start(
                                rows[:, s, j, :], None, table,
                                bass.IndirectOffsetOnAxis(ap=idx[:, s, j:j + 1].bitcast(U32), axis=0)
                            ).then_inc(gathered[s], 16)

            @block.sync
            def _(sp):
                sp.sem_inc(spill_done, SLOTS)
                with sp.Fori(0, R // SLOTS) as i:
                    for s in range(SLOTS):
                        gi = SLOTS * i + s
                        sp.wait_ge(gathered[s], (16 * G) * (i + 1))
                        sp.dma_start(spill[bass.ds(gi * P, P), :].rearrange("p (g d) -> p g d", g=G),
                                     rows[:, s, :, spill_at:spill_at + D]).then_inc(spilled[s], 16)
                        if s > 0:
                            sp.wait_ge(spilled[s - 1], 16 * (i + 1))
                            sp.sem_inc(spill_done, 1)
                    sp.wait_ge(spilled[SLOTS - 1], 16 * (i + 1))
                    sp.sem_inc(spill_done, 1)

            @block.tensor
            def _(pe):
                def spread_columns(i, s):
                    gi = SLOTS * i + s
                    pe.wait_ge(rel_staged, gi + 1)
                    pe.wait_ge(hot_ready, gi + 1)
                    for j in range(G):
                        mm = pe.matmul(ps_rel[:, j, :], rel[:, s, j:j + 1].to_broadcast([P, P]), c.ident_bf[:],
                                       start=True, stop=True)
                    mm.then_inc(spread, 1)
                    if bias_mode:
                        pe.wait_ge(len_staged, gi + 1)
                        pe.wait_ge(hid_ready, gi + 1)
                        for j in range(G):
                            mm = pe.matmul(ps_len[:, j, :], length[:, s, j:j + 1].to_broadcast([P, P]), c.ident[:],
                                           start=True, stop=True)
                        mm.then_inc(len_spread, 1)

                def expand_windows(i, s):
                    gi = SLOTS * i + s
                    pe.wait_ge(hot_ready, gi + 2)
                    pe.wait_ge(win_loaded[s], (16 * G) * (i + 1))
                    pe.wait_ge(consumed, gi + SLOTS)
                    for j in range(G):
                        mm = pe.matmul(ps_x[:, j, 0:window_w], hot_t[:, s, j, :], win[:, s, j, :], start=True, stop=True)
                    mm.then_inc(expanded, 1)
                    if bias_mode:
                        pe.wait_ge(hid_ready, gi + 2)
                        pe.wait_ge(scored, gi + 1)
                        for j in range(G):
                            mm = pe.matmul(ps_bias[:, j, :], hidden[:, j, :], k["we2t"], start=True, stop=True)
                        mm.then_inc(biased, 1)

                if bias_mode:
                    pe.sem_inc(biased, 1)
                pipelined(pe, R // SLOTS, SLOTS, spread_columns, expand_windows)

            @block.vector
            def _(dve):
                def one_hot(i, s):
                    gi = SLOTS * i + s
                    dve.wait_ge(spread, gi + 1)
                    dve.tensor_scalar(hot_t[:, s], ps_rel[:, 0:G, :], c.lane[:, 0:1], None,
                                      ALU.is_equal).then_inc(hot_ready, 1)

                def score(i, s):
                    gi = SLOTS * i + s
                    dve.wait_ge(scored, gi + 1)
                    dve.wait_ge(expanded, gi + 1)
                    dve.wait_ge(gathered[s], (16 * G) * (i + 1))
                    dve.tensor_copy(idx[:, s], group(o.other, gi + SLOTS)).then_inc(idx_staged, 1)
                    out = scores[:, bass.ds(gi * (G * heads), G * heads)]
                    if mode == "dot":
                        dve.tensor_tensor(prod[:], ps_x[:, 0:G, :], rows[:, s, :, 0:D], ALU.mult).then_inc(consumed, 1)
                        dve.wait_ge(consumed, gi + (SLOTS + 1))
                        dve.tensor_reduce(red[:], prod[:].rearrange("p g (h d) -> p (g h) d", h=heads),
                                          AX.X, ALU.add).then_inc(reduced, 1)
                        dve.wait_ge(reduced, gi + 1)
                        dve.wait_ge(biased, gi + 2)
                        dve.scalar_tensor_tensor(out, red[:], 1.0 / (D // heads) ** 0.5,
                                                 ps_bias[:].rearrange("p g h -> p (g h)"),
                                                 ALU.mult, ALU.add).then_inc(scored, 1)
                    elif mode == "gat2":
                        dve.tensor_tensor(prod[:], ps_x[:, 0:G, :], rows[:, s], ALU.add).then_inc(consumed, 1)
                        dve.wait_ge(consumed, gi + (SLOTS + 1))
                        dve.scalar_tensor_tensor(act_m[:], prod[:], 0.2, prod[:], ALU.mult, ALU.max).then_inc(leaked, 1)
                        dve.wait_ge(leaked, gi + 1)
                        dve.tensor_tensor(prod[:], act_m[:], per_tile(k["att"]), ALU.mult).then_inc(multiplied, 1)
                        dve.wait_ge(multiplied, gi + 1)
                        dve.tensor_reduce(out, prod[:].rearrange("p g (h d) -> p (g h) d", h=heads),
                                          AX.X, ALU.add).then_inc(scored, 1)
                    else:
                        dve.tensor_tensor(prod[:], rows[:, s], per_tile(k["att"]), ALU.mult).then_inc(multiplied, 1)
                        dve.wait_ge(multiplied, gi + 1)
                        dve.tensor_reduce(red[:], prod[:], AX.X, ALU.add).then_inc(reduced, 1)
                        dve.wait_ge(reduced, gi + 1)
                        dve.tensor_tensor(act_m[:, 0, 0:G], ps_x[:, 0:G, 0], red[:], ALU.add).then_inc(consumed, 1)
                        dve.wait_ge(consumed, gi + (SLOTS + 1))
                        dve.scalar_tensor_tensor(out, act_m[:, 0, 0:G], 0.2, act_m[:, 0, 0:G],
                                                 ALU.mult, ALU.max).then_inc(scored, 1)

                for s in range(SLOTS):
                    dve.tensor_copy(idx[:, s], group(o.other, s)).then_inc(idx_staged, 1)
                dve.sem_inc(consumed, SLOTS)
                dve.sem_inc(hot_ready, 1)
                dve.sem_inc(scored, 1)
                pipelined(dve, R // SLOTS, SLOTS, one_hot, score)
                dve.wait_ge(scored, R + 1)


def weighted_sum(nc, c, o, name, acc, alpha, heads, spill=None, table=None):
    with stage(nc, name) as st:
        rows = st.sb("rows", [P, SLOTS, G, D])
        hot, msg = st.sb("hot", [P, SLOTS, G, P]), st.sb("msg", [P, SLOTS, G, D])
        idx = st.sb("idx", [P, SLOTS, G], I32)
        ps_sum = st.ps("sum", [P, SLOTS, 8, P])
        per_slot = lambda n: [st.sem(f"{n}{s}") for s in range(SLOTS)]
        loaded, ready, hot_ready, summed = (per_slot(n) for n in ("loaded", "ready", "hot_ready", "summed"))
        pool_go, joined = st.sem("pool_go"), st.sem("joined")
        parts = [acc, st.sb("odd", [P, NP])]
        added = [[st.sem(f"added{s}_{j}") for j in range(G)] for s in range(SLOTS)]
        last_of = [(G - 1) // 2 * 2, (G - 2) // 2 * 2 + 1]
        if spill is not None:
            ps_diff = st.ps("diff", [P, 8, P])
            rel_rows = st.sb("rel_rows", [8, SLOTS, P], BF16)
            differed, rel_loaded, squared = per_slot("differed"), per_slot("rel_loaded"), st.sem("squared")
        else:
            idx_staged = per_slot("idx_staged")

        def messages(eng, i, s):
            w = alpha[:, bass.ds((SLOTS * i + s) * (G * heads), G * heads)]
            eng.tensor_tensor(msg[:, s].rearrange("p g (h d) -> p (g h) d", h=heads),
                              rows[:, s].rearrange("p g (h d) -> p (g h) d", h=heads),
                              over_tiles(w, D // heads), ALU.mult).then_inc(ready[s], 1)

        with nc.Block() as block:
            if spill is not None:
                @block.sync
                def _(sp):
                    with sp.Fori(0, R // SLOTS) as i:
                        for s in range(SLOTS):
                            sp.wait_ge(differed[s], i + 1)
                            sp.dma_start(rel_rows[:, s, :], o.rel_rows[bass.ds(SLOTS * i + s, 1)]
                                         .rearrange("r g e -> (r g) e")).then_inc(rel_loaded[s], 16)
                            sp.wait_ge(ready[s], i + 1)
                            sp.dma_start(rows[:, s].rearrange("p g d -> p (g d)"),
                                         spill[bass.ds((SLOTS * i + s) * P, P), :]).then_inc(loaded[s], 16)

                @block.gpsimd
                def _(pool):
                    for s in range(SLOTS):
                        pool.sem_inc(ready[s], 1)
                    with pool.Fori(0, R // SLOTS) as i:
                        for s in range(SLOTS):
                            pool.wait_ge(summed[s], i + 1)
                            pool.wait_ge(loaded[s], 16 * (i + 1))
                            pool.sem_inc(pool_go, 1)
                            messages(pool, i, s)
                    for s in range(SLOTS):
                        pool.wait_ge(ready[s], R // SLOTS + 1)

                @block.scalar
                def _(act):
                    with act.Fori(0, R // SLOTS) as i:
                        for s in range(SLOTS):
                            gi = SLOTS * i + s
                            act.wait_ge(differed[s], i + 2)
                            act.wait_ge(summed[s], i + 1)
                            act.activation(hot[:, s], ps_diff[:, 0:G, :], ACT.Square).then_inc(squared, 1)
                            act.wait_ge(squared, gi + 2)
                            act.activation(hot[:, s], hot[:, s], ACT.Relu, bias=c.ones[:, 0:1],
                                           scale=-1.0).then_inc(hot_ready[s], 1)
            else:
                @block.scalar
                def _(act):
                    with act.Fori(0, R // SLOTS) as i:
                        for s in range(SLOTS):
                            act.wait_ge(ready[s], i + 1)
                            act.copy(idx[:, s], group(o.other, SLOTS * i + s)).then_inc(idx_staged[s], 1)

                @block.gpsimd
                def _(pool):
                    with pool.Fori(0, R // SLOTS) as i:
                        for s in range(SLOTS):
                            pool.wait_ge(idx_staged[s], i + 1)
                            pool.sem_inc(pool_go, 1)
                            for j in range(G):
                                pool.indirect_dma_start(
                                    rows[:, s, j, :], None, table,
                                    bass.IndirectOffsetOnAxis(ap=idx[:, s, j:j + 1].bitcast(U32), axis=0)
                                ).then_inc(loaded[s], 16)

            @block.vector
            def _(dve):
                def gathered_messages(i, s):
                    dve.tensor_tensor(hot[:, s], per_tile(c.column[:]), over_tiles(group(o.rel, SLOTS * i + s), P),
                                      ALU.is_equal).then_inc(hot_ready[s], 1)
                    dve.wait_ge(loaded[s], (16 * G) * (i + 1))
                    messages(dve, i, s)

                def first_keys(gi, groups):
                    _, base = nc.values_load_multi_w_load_instructions(
                        o.base[0:1, bass.ds(gi * 8, groups * 8)], engines=[dve.engine], min_val=0, max_val=N,
                        skip_runtime_bounds_check_because="keys are node numbers")
                    return base

                def add(i, s, base=None):
                    base = base or first_keys(SLOTS * i + s, 1)
                    dve.wait_ge(summed[s], i + 2)
                    for j in range(G):
                        at = parts[j % 2][:, bass.ds(base[j], P)]
                        if j >= 2:
                            dve.wait_ge(added[s][j - 2], i + (2 if j - 2 in last_of else 1))
                        else:
                            dve.wait_ge(added[s - 1][last_of[j]], i + (2 if s else 1))
                        dve.tensor_tensor(at, at, ps_sum[:, s, j, :], ALU.add).then_inc(added[s][j], 1)

                for part, last in zip(parts, last_of):
                    dve.memset(part[:], 0.0).then_inc(added[SLOTS - 1][last], 1)
                    for s in range(SLOTS - 1):
                        dve.sem_inc(added[s][last], 1)
                if spill is None:
                    for s in range(SLOTS):
                        dve.sem_inc(ready[s], 1)
                    pipelined(dve, R // SLOTS, SLOTS, gathered_messages, add)
                else:
                    with dve.Fori(0, R // SLOTS) as i:
                        base = first_keys(SLOTS * i, SLOTS)
                        for s in range(SLOTS):
                            add(i, s, base[8 * s:8 * s + G])
                for last in last_of:
                    dve.wait_ge(added[SLOTS - 1][last], R // SLOTS + 1)
                dve.tensor_tensor(acc[:], acc[:], parts[1][:], ALU.add).then_inc(joined, 1)
                dve.wait_ge(joined, 1)

            @block.tensor
            def _(pe):
                def differences(i, s):
                    gi = SLOTS * i + s
                    pe.wait_ge(rel_loaded[s], 16 * (i + 1))
                    pe.wait_ge(squared, gi + 1)
                    for g0, g1 in ((0, 4), (4, G)):
                        mm = pe.matmul(ps_diff[:, g0:g1, :], rel_rows[:, s, :], c.minus_pick[:, g0:g1, :],
                                       start=True, stop=True)
                    mm.then_inc(differed[s], 1)

                def sums(i, s):
                    pe.wait_ge(hot_ready[s], i + 1)
                    pe.wait_ge(ready[s], i + 2)
                    for last in last_of:
                        pe.wait_ge(added[s][last], i + 1)
                    for j in range(G):
                        mm = pe.matmul(ps_sum[:, s, j, :], msg[:, s, j, :], hot[:, s, j, :], start=True, stop=True)
                    mm.then_inc(summed[s], 1)

                for s in range(SLOTS):
                    pe.sem_inc(summed[s], 1)
                if spill is None:
                    with pe.Fori(0, R // SLOTS) as i:
                        for s in range(SLOTS):
                            sums(i, s)
                else:
                    for s in range(SLOTS):
                        pe.sem_inc(differed[s], 1)
                    pe.sem_inc(squared, 1)
                    pipelined(pe, R // SLOTS, SLOTS, differences, sums)


def segment_softmax(nc, c, o, name, scores, heads, first, spare):
    with stage(nc, name) as st:
        e, f, g = st.sb("e", [R, heads, W]), st.sb("f", [R, W]), st.sb("g", [R, W])
        held = [spare[0:R, h * W:(h + 1) * W] for h in range(min(heads, NP // W))]
        held += [f[:]] * (heads - len(held))
        assert heads - NP // W <= 1
        keep, keep_end, neg = st.sb("keep", [R, W]), st.sb("keep_end", [R, W]), st.sb("neg", [R, W])
        prefix, suffix = st.sb("prefix", [R, W]), st.sb("suffix", [R, W])
        r_keep, r_keep_end, r_neg = (st.sb(n, [heads, R]) for n in ("r_keep", "r_keep_end", "r_neg"))
        last, carry = st.sb("last", [R, heads]), st.sb("carry", [R, heads])
        chain_row = st.sb("chain_row", [heads, R + 1])
        col_max, neg_max = st.sb("col_max", [R, heads]), st.sb("neg_max", [R, heads])
        head_max, max_diag = st.sb("head_max", [heads, 1]), st.sb("max_diag", [heads, heads])
        ps_row, ps_col, ps_turn = st.ps("row", [P, 512]), st.ps("col", [P, 512]), st.ps("turn", [P, 2, 8, P])
        ps_flags = [ps_row[0:heads, n * P:n * P + R] for n in (2, 3)]
        (steps, turned, copied, flags_spread, last_ready, row_turned, row_ready, col_turned, exp_in, exp_out, max_in, max_t,
         diag_ready, max_all, inverse_ready, scaled, back, out) = (
            st.sem(n) for n in ("steps", "turned", "copied", "flags_spread", "last_ready", "row_turned", "row_ready",
                                "col_turned", "exp_in", "exp_out", "max_in", "max_t", "diag_ready", "max_all",
                                "inverse_ready", "scaled", "back", "out"))
        n_carry = 2 if first else 4
        cols = scores[:].rearrange("p (r g h) -> p g h r", g=G, h=heads)
        with nc.Block() as block:
            @block.tensor
            def _(pe):
                for to, flag in zip(ps_flags, (o.has_start, o.has_end)):
                    pe.matmul(to, c.ones[0:1, 0:heads], flag[:], start=True, stop=True).then_inc(flags_spread, 1)
                for h in range(heads):
                    if h >= 2:
                        pe.wait_ge(copied, h - 1)
                    for t in range(G):
                        mm = pe.transpose(ps_turn[0:R, h % 2, t, :], cols[:, t, h, :], c.ident[:])
                    mm.then_inc(turned, 1)
                if first:
                    pe.wait_ge(max_in, 1)
                    pe.transpose(ps_row[0:heads, 0:R], col_max[:], c.ident[0:R, 0:R]).then_inc(max_t, 1)
                    pe.wait_ge(diag_ready, 1)
                    pe.matmul(ps_col[0:R, 0:heads], c.ones[0:heads, 0:R], max_diag[:],
                              start=True, stop=True).then_inc(max_all, 1)
                for n in range(n_carry):
                    pe.wait_ge(last_ready, n + 1)
                    pe.transpose(ps_row[0:heads, 0:R], last[:], c.ident[0:R, 0:R]).then_inc(row_turned, 1)
                    pe.wait_ge(row_ready, n + 1)
                    row = chain_row[:, 0:R] if n % 2 == 0 else chain_row[:, 1:R + 1]
                    pe.transpose(ps_col[0:R, 0:heads], row, c.ident[0:heads, 0:heads]).then_inc(col_turned, 1)
                pe.wait_ge(copied, heads)
                for h in range(heads):
                    pe.wait_ge(scaled, h + 1)
                    if h >= 2:
                        pe.wait_ge(out, h - 1)
                    for t in range(G):
                        mm = pe.transpose(ps_turn[:, h % 2, t, 0:R], e[:, h, t * P:(t + 1) * P], c.ident[0:R, 0:R])
                    mm.then_inc(back, 1)

            @block.scalar
            def _(act):
                for h in range(heads):
                    act.wait_ge(turned, h + 1)
                    act.copy(e[:, h].rearrange("r (g j) -> r g j", g=G), ps_turn[0:R, h % 2, 0:G, :]).then_inc(copied, 1)
                for h in range(heads):
                    act.wait_ge(exp_in, h + 1)
                    if first:
                        act.activation(e[:, h], e[:, h], ACT.Exp, bias=neg_max[:, h:h + 1]).then_inc(exp_out, 1)
                    else:
                        act.activation(e[:, h], e[:, h], ACT.Exp).then_inc(exp_out, 1)
                for h in range(heads):
                    act.wait_ge(back, h + 1)
                    act.copy(cols[:, :, h, :], ps_turn[:, h % 2, 0:G, 0:R]).then_inc(out, 1)
                act.wait_ge(out, heads)

            @block.gpsimd
            def _(pool):
                for h in range(heads):
                    pool.wait_ge(inverse_ready, h + 1)
                    pool.tensor_tensor(e[:, h], e[:, h], held[h], ALU.mult).then_inc(scaled, 1)
                pool.wait_ge(scaled, heads)

            @block.vector
            def _(dve):
                link = Chain(dve, steps)
                carries = [0]

                def scan_rows(h, a, b, start, op0, op1, backward=False):
                    way = slice(None, None, -1) if backward else slice(None)
                    link(dve.tensor_tensor_scan(held[h][:, way], a[:, way], b[:, way], start, op0, op1))
                    link(dve.tensor_copy(last[:, h:h + 1], held[h][:, 0:1] if backward else held[h][:, W - 1:W]))

                def carry_over(start, op0, op1, row_flags, backward=False):
                    dve.sem_inc(last_ready, 1)
                    link(dve.memset(chain_row[:, R:R + 1] if backward else chain_row[:, 0:1], start))
                    dve.wait_ge(row_turned, carries[0] + 1)
                    if backward:
                        dve.tensor_tensor_scan(chain_row[:, 0:R][:, ::-1], row_flags[:, ::-1], ps_row[0:heads, 0:R][:, ::-1],
                                               start, op0, op1).then_inc(row_ready, 1)
                    else:
                        dve.tensor_tensor_scan(chain_row[:, 1:R + 1], row_flags[:], ps_row[0:heads, 0:R],
                                               start, op0, op1).then_inc(row_ready, 1)
                    carries[0] += 1
                    dve.wait_ge(col_turned, carries[0])
                    link(dve.tensor_copy(carry[:], ps_col[0:R, 0:heads]))

                def last_to_whole(h, guard=0.0):
                    if guard:
                        link(dve.scalar_tensor_tensor(g[:], held[h], guard, o.end[:], ALU.add, ALU.mult))
                    else:
                        link(dve.tensor_tensor(g[:], held[h], o.end[:], ALU.mult))
                    scan_rows(h, keep_end, g, 0.0, ALU.mult, ALU.add, backward=True)

                def add_carry(h, where):
                    link(dve.scalar_tensor_tensor(held[h], where[:], carry[:, h:h + 1], held[h], ALU.mult, ALU.add))

                link(dve.tensor_scalar(keep[:], o.start[:], -1.0, 1.0, ALU.mult, ALU.add))
                link(dve.tensor_scalar(keep_end[:], o.end[:], -1.0, 1.0, ALU.mult, ALU.add))
                link(dve.memset(g[:], 0.0))
                link(dve.tensor_tensor_scan(prefix[:], keep[:], g[:], 1.0, ALU.mult, ALU.add))
                link(dve.tensor_tensor_scan(suffix[:, ::-1], keep_end[:, ::-1], g[:, ::-1], 1.0, ALU.mult, ALU.add))
                dve.wait_ge(flags_spread, 2)
                link(dve.tensor_scalar(r_keep[:], ps_flags[0], -1.0, 1.0, ALU.mult, ALU.add))
                link(dve.tensor_scalar(r_keep_end[:], ps_flags[1], -1.0, 1.0, ALU.mult, ALU.add))
                if first:
                    link(dve.tensor_scalar(neg[:], first["real"], BIG, -BIG, ALU.mult, ALU.add))
                    for h in range(heads):
                        dve.wait_ge(copied, h + 1)
                        link(dve.scalar_tensor_tensor(e[:, h], e[:, h], first["be2"][0:R, h:h + 1], first["cut"],
                                                      ALU.add, ALU.mult))
                        link(dve.tensor_tensor(e[:, h], e[:, h], neg[:], ALU.add))
                        link(dve.tensor_reduce(col_max[:, h:h + 1], e[:, h], AX.X, ALU.max))
                    dve.sem_inc(max_in, 1)
                    dve.wait_ge(max_t, 1)
                    link(dve.tensor_reduce(head_max[:], ps_row[0:heads, 0:R], AX.X, ALU.max))
                    link(dve.tensor_scalar(max_diag[:], c.ident[0:heads, 0:heads], head_max[:, 0:1], None, ALU.mult))
                    dve.sem_inc(diag_ready, 1)
                    dve.wait_ge(max_all, 1)
                    link(dve.tensor_scalar(neg_max[:], ps_col[0:R, 0:heads], -1.0, None, ALU.mult))
                    dve.sem_inc(exp_in, heads)
                else:
                    link(dve.tensor_scalar(neg[:], o.start[:], -BIG, None, ALU.mult))
                    link(dve.tensor_scalar(r_neg[:], ps_flags[0], -BIG, None, ALU.mult))
                    for h in range(heads):
                        dve.wait_ge(copied, h + 1)
                        scan_rows(h, neg, e[:, h], -BIG, ALU.add, ALU.max)
                    carry_over(-BIG, ALU.add, ALU.max, r_neg)
                    link(dve.tensor_scalar(neg[:], prefix[:], BIG, -BIG, ALU.mult, ALU.add))
                    for h in range(heads):
                        link(dve.scalar_tensor_tensor(held[h], neg[:], carry[:, h:h + 1], held[h], ALU.add, ALU.max))
                        last_to_whole(h)
                    carry_over(0.0, ALU.mult, ALU.add, r_keep_end, backward=True)
                    for h in range(heads):
                        add_carry(h, suffix)
                        dve.tensor_tensor(e[:, h], e[:, h], held[h], ALU.subtract).then_inc(exp_in, 1)
                        dve.wait_ge(exp_in, h + 1)
                for h in range(heads):
                    dve.wait_ge(exp_out, h + 1)
                    scan_rows(h, keep, e[:, h], 0.0, ALU.mult, ALU.add)
                carry_over(0.0, ALU.mult, ALU.add, r_keep)
                for h in range(heads):
                    add_carry(h, prefix)
                    last_to_whole(h, 1e-8 if first else 0.0)
                carry_over(0.0, ALU.mult, ALU.add, r_keep_end, backward=True)
                for h in range(heads):
                    add_carry(h, suffix)
                    link(dve.reciprocal(held[h], held[h]))
                    dve.sem_inc(inverse_ready, 1)


def cutoff(nc, o, cut):
    with stage(nc, "cutoff") as st:
        u, ui = st.sb("u", [R, W]), st.sb("ui", [R, W], I32)
        v, inside = st.sb("v", [R, W]), st.sb("inside", [R, W])
        half_pi = st.sb("half_pi", [R, 1])
        steps, turn_ready, sined = st.sem("steps"), st.sem("turn_ready"), st.sem("sined")
        two_pi = 6.283185307179586
        with nc.Block() as block:
            @block.vector
            def _(dve):
                link = Chain(dve, steps)
                link(dve.memset(half_pi[:], two_pi / 4))
                link(dve.tensor_scalar(u[:], o.length[:], 0.5 / CUTOFF, None, ALU.mult))
                link(dve.tensor_copy(ui[:], u[:]))
                link(dve.tensor_copy(v[:], ui[:]))
                link(dve.tensor_tensor(u[:], u[:], v[:], ALU.subtract))
                link(dve.scalar_tensor_tensor(u[:], u[:], -1.0, u[:], ALU.mult, ALU.max))
                link(dve.tensor_scalar(v[:], u[:], -1.0, 1.0, ALU.mult, ALU.add))
                link(dve.tensor_tensor(u[:], u[:], v[:], ALU.min))
                dve.sem_inc(turn_ready, 1)
                link(dve.tensor_scalar(inside[:], o.length[:], CUTOFF, 0.5, ALU.is_lt, ALU.mult))
                dve.wait_ge(sined, 1)
                link(dve.scalar_tensor_tensor(cut[:], v[:], 1.0, inside[:], ALU.add, ALU.mult))

            @block.scalar
            def _(act):
                act.wait_ge(turn_ready, 1)
                act.activation(v[:], u[:], ACT.Sin, bias=half_pi[:, 0:1], scale=-two_pi).then_inc(sined, 1)
                act.wait_ge(sined, 1)


def batch_norm_relu(nc, acc, k):
    with stage(nc, "batch_norm") as st:
        sq = st.sb("sq", [P, N])
        m, scale, ss = st.sb("m", [P, 1]), st.sb("scale", [P, 1]), st.sb("ss", [P, 1])
        steps, centred, squared, scaled, out = (st.sem(n) for n in ("steps", "centred", "squared", "scaled", "out"))
        var_ready, rooted = st.sem("var_ready"), st.sem("rooted")
        a = acc[:, 0:N]
        with nc.Block() as block:
            @block.vector
            def _(dve):
                link = Chain(dve, steps)
                link(dve.tensor_scalar(a, a, k["bias"], None, ALU.add))
                link(dve.tensor_reduce(m[:], a, AX.X, ALU.add))
                link(dve.tensor_scalar(m[:], m[:], 1.0 / N, None, ALU.mult))
                link(dve.tensor_scalar(a, a, m[:, 0:1], None, ALU.subtract))
                dve.sem_inc(centred, 1)
                dve.wait_ge(squared, 1)
                link(dve.tensor_scalar(scale[:], ss[:], 1.0 / N, LN_EPS, ALU.mult, ALU.add))
                link(dve.reciprocal(m[:], scale[:]))
                dve.sem_inc(var_ready, 1)
                dve.wait_ge(rooted, 1)
                link(dve.tensor_tensor(scale[:], scale[:], k["gamma"], ALU.mult))
                dve.sem_inc(scaled, 1)

            @block.scalar
            def _(act):
                act.wait_ge(centred, 1)
                act.activation(sq[:], a, ACT.Square, accum_out=ss[:, 0:1]).then_inc(squared, 1)
                act.wait_ge(squared, 1)
                act.wait_ge(var_ready, 1)
                act.activation(scale[:], m[:], ACT.Sqrt).then_inc(rooted, 1)
                act.wait_ge(scaled, 1)
                act.activation(a, a, ACT.Relu, bias=k["beta"], scale=scale[:, 0:1]).then_inc(out, 1)
                act.wait_ge(out, 1)


def node_update(nc, c, name, acc, x, mode, k):
    with stage(nc, name) as st:
        at, h, y = (st.sb(n, [P, 2, CB, D]) for n in ("at", "h", "y"))
        stats, mv = st.sb("stats", [P, 2, CB, 6]), st.sb("mv", [P, 2, CB, 2])
        ve, inverse, rs = (st.sb(n, [P, 2, CB]) for n in ("ve", "inverse", "rs"))
        var_ready, rs_ready, stats_go = st.sem("var_ready"), st.sem("rs_ready"), st.sem("stats_go")
        ps_y = st.ps("y", [P, 2, 8, P])
        at_ready, multiplied, steps, product_used = (
            st.sem(n) for n in ("at_ready", "multiplied", "steps", "product_used"))
        own = mode in ("conv", "last")
        if own:
            xs, xt, z = (st.sb(n, [P, 2, CB, D]) for n in ("xs", "xt", "z"))
            ps_t = st.ps("t", [P, 2, 8, P])
            xs_ready, turned, xt_ready, z_ready = (st.sem(n) for n in ("xs_ready", "turned", "xt_ready", "z_ready"))
            stored = [st.sem(f"stored{s}") for s in range(2)]
        store = {"conv": k.get("table"), "last": k.get("out")}.get(mode)
        n_norms = {"attend": 2, "plain": 1, "conv": 0, "last": 1}[mode]
        n_steps = (2 * {"attend": 5, "plain": 1 + (k.get("b") is not None), "conv": 3, "last": 3}[mode]
                   + n_norms * (4 * CB + 5))
        with nc.Block() as block:
            @block.scalar
            def _(act):
                def operands(i, _):
                    for s in range(2):
                        n = 2 * i + s
                        act.wait_ge(multiplied, n + 1)
                        act.copy(at[:, s].rearrange("p q d -> p (q d)"),
                                 acc[:, bass.ds(n * (CB * P), CB * P)]).then_inc(at_ready, 1)
                        if own:
                            act.copy(xs[:, s], k["own"][:, bass.ds(n * CB, CB), :]).then_inc(xs_ready, 1)
                    if own:
                        for s in range(2):
                            act.wait_ge(turned, 2 * i + s + 1)
                            act.copy(xt[:, s], ps_t[:, s, 0:CB, :]).then_inc(xt_ready, 1)

                def roots(i, _):
                    for l in range(n_norms):
                        act.wait_ge(var_ready, i * n_norms + (l + 1))
                        act.activation(rs[:], inverse[:], ACT.Sqrt).then_inc(rs_ready, 1)

                pipelined(act, NC // 2, 1, operands, roots)

            @block.tensor
            def _(pe):
                pe.sem_inc(multiplied, 2)
                with pe.Fori(0, NC // 2) as i:
                    if own:
                        for s in range(2):
                            pe.wait_ge(xs_ready, 2 * i + s + 1)
                            for q in range(CB):
                                mm = pe.transpose(ps_t[:, s, q, :], xs[:, s, q, :], c.ident[:])
                            mm.then_inc(turned, 1)
                    for s in range(2):
                        n = 2 * i + s
                        pe.wait_ge(at_ready, n + 1)
                        if own:
                            pe.wait_ge(xt_ready, n + 1)
                        pe.wait_ge(product_used, i + 1)
                        for q in range(CB):
                            out_q = ps_y[:, s, q, :]
                            if mode == "plain":
                                mm = pe.transpose(out_q, at[:, s, q, :], c.ident[:])
                            elif mode == "attend":
                                mm = pe.matmul(out_q, at[:, s, q, :], k["w"], start=True, stop=True)
                            else:
                                pe.matmul(out_q, at[:, s, q, :], k["wr"], start=True, stop=False)
                                mm = pe.matmul(out_q, xt[:, s, q, :], k["ws"], start=False, stop=True)
                        mm.then_inc(multiplied, 1)

            @block.vector
            def _(dve):
                dve.sem_inc(product_used, 1)
                with dve.Fori(0, NC // 2) as i:
                    count, norms = [0], [0]

                    def link(*several):
                        for ins in several:
                            count[0] += 1
                            ins.then_inc(steps, 1)
                        dve.wait_ge(steps, i * n_steps + count[0])

                    def both(step):
                        link(*[step(s) for s in range(2)])

                    def layer_norm(dst, src):
                        blocks = [(s, q) for s in range(2) for q in range(CB)]
                        link(*[dve.bn_stats(stats[:, s, q, :], src(s)[:, q, :]) for s, q in blocks])
                        dve.sem_inc(stats_go, 1)
                        link(*[dve.bn_aggr(mv[:, s, q, :], stats[:, s, q, :]) for s, q in blocks])
                        link(dve.tensor_scalar(ve[:], mv[:, :, :, 1], LN_EPS, None, ALU.add))
                        norms[0] += 1
                        dve.reciprocal(inverse[:], ve[:]).then_inc(var_ready, 1)
                        both(lambda s: dve.tensor_tensor(dst(s), src(s), over_tiles(mv[:, s, :, 0], D), ALU.subtract))
                        dve.wait_ge(rs_ready, i * n_norms + norms[0])
                        both(lambda s: dve.tensor_tensor(dst(s), dst(s), over_tiles(rs[:, s], D), ALU.mult))

                    xb = lambda s: x[:, bass.ds((2 * i + s) * CB, CB), :]
                    h_of, y_of = (lambda s: h[:, s]), (lambda s: y[:, s])
                    product = lambda s: ps_y[:, s, 0:CB, :]
                    dve.wait_ge(multiplied, 2 * i + 4)
                    if k.get("b") is not None:
                        both(lambda s: dve.tensor_tensor(h[:, s], ps_y[:, s, 0:CB, :], per_tile(k["b"], CB), ALU.add))
                        dve.sem_inc(product_used, 1)
                        product = h_of
                    if mode == "attend":
                        both(lambda s: dve.tensor_tensor(y[:, s], product(s), xb(s), ALU.add))
                        layer_norm(h_of, y_of)
                        both(lambda s: dve.tensor_tensor(y[:, s], h[:, s], per_tile(k["g"], CB), ALU.mult))
                        both(lambda s: dve.tensor_tensor(h[:, s], y[:, s], per_tile(k["be"], CB), ALU.add))
                        both(lambda s: dve.tensor_tensor(y[:, s], h[:, s], xb(s), ALU.add))
                        layer_norm(xb, y_of)
                    elif mode == "plain":
                        both(lambda s: dve.tensor_tensor(y[:, s], product(s), xb(s), ALU.add))
                        if k.get("b") is None:
                            dve.sem_inc(product_used, 1)
                        layer_norm(xb, y_of)
                    elif mode == "conv":
                        for s in range(2):
                            dve.wait_ge(stored[s], 16 * (i + 1))
                        both(lambda s: dve.tensor_scalar(k["nodes"][:, bass.ds((2 * i + s) * CB, CB), :], product(s), 0.0,
                                                         None, ALU.max))
                        both(lambda s: dve.tensor_scalar(z[:, s], product(s), 0.0, None, ALU.max))
                        dve.sem_inc(z_ready, 2)
                    else:
                        both(lambda s: dve.tensor_scalar(y[:, s], product(s), 0.0, None, ALU.max))
                        both(lambda s: dve.tensor_tensor(h[:, s], y[:, s], xb(s), ALU.add))
                        for s in range(2):
                            dve.wait_ge(stored[s], 16 * (i + 1))
                        layer_norm(lambda s: z[:, s], h_of)
                        dve.sem_inc(z_ready, 2)
                    assert count[0] == n_steps, (mode, count[0], n_steps)

            if store is not None:
                @block.sync
                def _(sp):
                    for s in range(2):
                        sp.sem_inc(stored[s], 16)
                    with sp.Fori(0, NC // 2) as i:
                        for s in range(2):
                            n = 2 * i + s
                            sp.wait_ge(z_ready, n + 1)
                            sp.dma_start(store[bass.ds(n * (CB * P), CB * P), :].rearrange("(q p) d -> p q d", p=P),
                                         z[:, s]).then_inc(stored[s], 16)
                    for s in range(2):
                        sp.wait_ge(stored[s], 16 * (NC // 2 + 1))


def gnn_kernel(nc, out, x_in, src, dst, length, edge_weight, real, p):
    with ExitStack() as keep:
        sb = lambda n, s, dt=F32: keep.enter_context(nc.sbuf_tensor(n, s, dt))
        dram = lambda n, s: nc.dram_tensor(n, s, F32).ap()
        by_src, by_dst = Order(nc, "src", keep), Order(nc, "dst", keep)
        c = constants(nc, keep, (by_src, by_dst))
        x, acc = sb("x_nodes", [P, NB, D]), sb("acc", [P, NP])
        scores = sb("scores", [P, T * H0])
        src_counts, dst_counts = sb("src_counts", [P, HB]), sb("dst_counts", [P, HB])
        spill = dram("spill", [R * P, G * D])
        by_dst.real = None
        with ExitStack() as first_layer:
            lsb = lambda n, s, dt=F32: first_layer.enter_context(nc.sbuf_tensor(n, s, dt))
            by_src.real, by_src.length = lsb("real_row", [R, W]), lsb("length_row", [R, W])
            sort_edges(nc, c, by_src, src, dst, length, real, src_counts, False, dst_counts)

            w_raw = lsb("w_raw", [P, 4, D])
            we2_raw, we2t = lsb("we2_raw", [H0, D]), lsb("we2t", [D, H0])
            qkv_w, qkv_b, wo_t = lsb("qkv_w", [P, 3 * D]), lsb("qkv_b", [P, 3 * D]), lsb("wo_t", [P, D])
            we1, be1, be2 = lsb("we1", [P, 1]), lsb("be1", [P, 1]), lsb("be2", [P, H0])
            bo, ln_g, ln_b = lsb("bo", [P, D]), lsb("ln_g", [P, D]), lsb("ln_b", [P, D])
            load_weights(nc, "load0", [
                (x[:], x_in.rearrange("(b p) d -> p b d", p=P)),
                (w_raw[:, 0], p["L0_gnn_Wq"]), (w_raw[:, 1], p["L0_gnn_Wk"]), (w_raw[:, 2], p["L0_gnn_Wv"]),
                (w_raw[:, 3], p["L0_gnn_Wo"]), (we2_raw[:], p["L0_gnn_We2"]), (we1[:], p["L0_gnn_We1"]),
                (be1[:], p["L0_gnn_be1"].rearrange("(d o) -> d o", o=1)),
                (be2[:], spread_row(p["L0_gnn_be2"], H0)),
                (qkv_b[:, 0:D], spread_row(p["L0_gnn_bq"], D)), (qkv_b[:, D:2 * D], spread_row(p["L0_gnn_bk"], D)),
                (qkv_b[:, 2 * D:], spread_row(p["L0_gnn_bv"], D)), (bo[:], spread_row(p["L0_gnn_bo"], D)),
                (ln_g[:], spread_row(p["L0_gnn_ln_g"], D)), (ln_b[:], spread_row(p["L0_gnn_ln_b"], D))])
            transpose_weights(nc, c, "turn0", [(qkv_w[:, n * D:(n + 1) * D], w_raw[:, n]) for n in range(3)]
                              + [(wo_t[:], w_raw[:, 3]), (we2t[:], we2_raw[:])])
            q_table, kv_table = dram("q_table", [NP, D]), dram("kv_table", [NP, 2 * D])
            node_tables(nc, c, "qkv", x, qkv_w[:], qkv_b[:], 3 * D, [(q_table, 0, D), (kv_table, D, 2 * D)])
            cut = lsb("cut", [R, W])
            cutoff(nc, by_src, cut)
            edge_scores(nc, c, by_src, "scores0", kv_table, 2 * D, q_table, D, spill, D, scores, H0, "dot",
                        {"we1": we1[:, 0:1], "be1": be1[:, 0:1], "we2t": we2t[:]})
            segment_softmax(nc, c, by_src, "softmax0", scores, H0,
                            {"real": by_src.real[:], "cut": cut[:], "be2": be2}, acc)
            weighted_sum(nc, c, by_src, "sum0", acc, scores, H0, spill=spill)
            node_update(nc, c, "update0", acc, x, "attend",
                        {"w": wo_t[:], "b": bo[:], "g": ln_g[:], "be": ln_b[:]})

        sort_edges(nc, c, by_dst, dst, src, edge_weight, real, dst_counts, True)
        scores1 = scores[:, 0:T * H1]

        lr_w, lr_b = sb("lr_w", [P, 2 * D]), sb("lr_b", [P, 2 * D])
        att, bias1 = sb("att", [P, D]), sb("bias1", [P, D])
        h_w, att_src, att_dst = sb("h_w", [P, D]), sb("att_src", [P, D]), sb("att_dst", [P, D])
        bias2, gamma, beta = sb("bias2", [P, 1]), sb("gamma", [P, 1]), sb("beta", [P, 1])
        conv_w, conv_b = sb("conv_w", [P, 4, D]), sb("conv_b", [P, 2, D])
        column = lambda v: v.rearrange("(d o) -> d o", o=1)
        load_weights(nc, "load1", [
            (lr_w[:, 0:D], p["L1_gnn_W_l"]), (lr_w[:, D:], p["L1_gnn_W_r"]),
            (lr_b[:, 0:D], spread_row(p["L1_gnn_b_l"], D)), (lr_b[:, D:], spread_row(p["L1_gnn_b_r"], D)),
            (att[:], spread_row(p["L1_gnn_att"].rearrange("h c -> (h c)"), D)),
            (bias1[:], spread_row(p["L1_gnn_bias"], D)),
            (h_w[:], p["L2_gnn_W"]), (att_src[:], spread_row(p["L2_gnn_att_src"], D)),
            (att_dst[:], spread_row(p["L2_gnn_att_dst"], D)), (bias2[:], column(p["L2_gnn_bias"])),
            (gamma[:], column(p["L2_gnn_gamma"])), (beta[:], column(p["L2_gnn_beta"])),
            (conv_w[:, 0], p["L3_gnn_Wr0"]), (conv_w[:, 1], p["L3_gnn_Ws0"]),
            (conv_w[:, 2], p["L3_gnn_Wr1"]), (conv_w[:, 3], p["L3_gnn_Ws1"]),
            (conv_b[:, 0], spread_row(p["L3_gnn_br0"], D)), (conv_b[:, 1], spread_row(p["L3_gnn_br1"], D))])
        xl_table, xr_table = dram("xl_table", [NP, D]), dram("xr_table", [NP, D])
        node_tables(nc, c, "lr", x, lr_w[:], lr_b[:], 2 * D, [(xl_table, 0, D), (xr_table, D, D)])
        edge_scores(nc, c, by_dst, "scores1", xl_table, D, xr_table, D, spill, 0, scores1, H1, "gat2", {"att": att[:]})
        segment_softmax(nc, c, by_dst, "softmax1", scores1, H1, None, acc)
        weighted_sum(nc, c, by_dst, "sum1", acc, scores1, H1, spill=spill)
        node_update(nc, c, "update1", acc, x, "plain", {"b": bias1[:]})

        h_table, a_table = dram("h_table", [NP, D]), dram("a_table", [NP, 1])
        node_tables(nc, c, "h", x, h_w[:], None, D, [(h_table, 0, D)], (att_dst[:], a_table))
        scores2 = scores[:, 0:T]
        edge_scores(nc, c, by_dst, "scores2", h_table, D, a_table, 1, spill, 0, scores2, 1, "gat", {"att": att_src[:]})
        segment_softmax(nc, c, by_dst, "softmax2", scores2, 1, None, acc)
        weighted_sum(nc, c, by_dst, "sum2", acc, scores2, 1, spill=spill)
        batch_norm_relu(nc, acc, {"bias": bias2[:, 0:1], "gamma": gamma[:], "beta": beta[:, 0:1]})
        node_update(nc, c, "update2", acc, x, "plain", {})

        x_table, conv_table = dram("x_table", [NP, D]), dram("conv_table", [NP, D])
        h_nodes = scores[:, 0:NB * D].rearrange("p (b d) -> p b d", d=D)
        unit = sb("unit", [P, T])
        load_weights(nc, "store_x", [(x_table.rearrange("(b p) d -> p b d", p=P), x[:])])
        weighted_sum(nc, c, by_dst, "sum3", acc, by_dst.weight, 1, table=x_table)
        node_update(nc, c, "conv0", acc, x, "conv",
                    {"own": x, "wr": conv_w[:, 0], "ws": conv_w[:, 1], "b": conv_b[:, 0], "nodes": h_nodes,
                     "table": conv_table})
        columns_of_real(nc, c, by_dst, unit)
        weighted_sum(nc, c, by_dst, "sum4", acc, unit, 1, table=conv_table)
        node_update(nc, c, "conv1", acc, x, "last",
                    {"own": h_nodes, "wr": conv_w[:, 2], "ws": conv_w[:, 3], "b": conv_b[:, 1], "out": out})


def columns_of_real(nc, c, o, unit):
    with stage(nc, "real_rows") as st:
        rows, real = st.sb("rows", [R, W, 4]), st.sb("real", [R, W])
        loaded, taken = st.sem("loaded"), st.sem("taken")
        with nc.Block() as block:
            @block.sync
            def _(sp):
                sp.dma_start(rows[:].rearrange("r w f -> r (w f)"),
                             o.payload.rearrange("(r w) f -> r (w f)", w=W)).then_inc(loaded, 16)
                sp.wait_ge(loaded, 16)

            @block.vector
            def _(dve):
                dve.wait_ge(loaded, 16)
                dve.tensor_copy(real[:], rows[:, :, 3]).then_inc(taken, 1)
                dve.wait_ge(taken, 1)
        rows_to_columns(nc, c, "turn_real", [(real[:], [unit[:]])])


_WEIGHTS = ["L0_gnn_Wq", "L0_gnn_bq", "L0_gnn_Wk", "L0_gnn_bk", "L0_gnn_Wv", "L0_gnn_bv", "L0_gnn_We1", "L0_gnn_be1",
            "L0_gnn_We2", "L0_gnn_be2", "L0_gnn_Wo", "L0_gnn_bo", "L0_gnn_ln_g", "L0_gnn_ln_b", "L1_gnn_W_l",
            "L1_gnn_b_l", "L1_gnn_W_r", "L1_gnn_b_r", "L1_gnn_att", "L1_gnn_bias", "L2_gnn_W", "L2_gnn_att_src",
            "L2_gnn_att_dst", "L2_gnn_bias", "L2_gnn_gamma", "L2_gnn_beta", "L3_gnn_Wr0", "L3_gnn_br0", "L3_gnn_Ws0",
            "L3_gnn_Wr1", "L3_gnn_br1", "L3_gnn_Ws1"]


def kernel(**inputs):
    import numpy as np
    import concourse.bacc as bacc
    from concourse.bass_utils import run_bass_kernel_spmd

    def columns(a, tail):
        whole = np.concatenate([np.asarray(a).reshape(-1), tail])
        return np.ascontiguousarray(whole.reshape(T, P).T)

    loops = np.full(EP - E, N, np.int32)
    loops[:N] = np.arange(N, dtype=np.int32)
    nothing = np.zeros(EP - E, np.float32)
    x = np.asarray(inputs["x"])
    arrays = {
        "x": np.concatenate([x, np.zeros((NP - N, D), x.dtype)]),
        "src": columns(inputs["src"], loops),
        "dst": columns(inputs["dst"], loops),
        "length": columns(inputs["edge_weight1"], nothing),
        "weight": columns(inputs["edge_weight"], nothing),
        "real": columns(np.ones(E, np.float32), nothing),
    }
    for name in _WEIGHTS:
        arrays[name] = np.ascontiguousarray(inputs[name])
    nc = bacc.Bacc("TRN2", target_bir_lowering=False, num_devices=1)
    aps = {}
    for name, a in arrays.items():
        aps[name] = nc.dram_tensor(f"in_{name}", a.shape, mybir.dt.from_np(a.dtype), kind="ExternalInput").ap()
    out = nc.dram_tensor("out_nodes", [NP, D], F32, kind="ExternalOutput").ap()
    gnn_kernel(nc, out, aps["x"], aps["src"], aps["dst"], aps["length"], aps["weight"], aps["real"],
               {name: aps[name] for name in _WEIGHTS})
    r = run_bass_kernel_spmd(nc, [{f"in_{name}": a for name, a in arrays.items()}], core_ids=[0])
    return r.results[0]["out_nodes"][:N]
```
